# Optimizing a Trainium2 kernel written in Bass

```python
import numpy as np
import jax
import jax.numpy as jnp

def _softmax(x, axis=-1):
    return jax.nn.softmax(x, axis=axis)

def _gelu(x):
    return jax.nn.gelu(x, approximate=True)

def _silu(x):
    return jax.nn.silu(x)

def _sigmoid(x):
    return jax.nn.sigmoid(x)

def _layernorm(x, axis=-1, eps=1e-05):
    m = jnp.mean(x, axis=axis, keepdims=True)
    v = jnp.var(x, axis=axis, keepdims=True)
    return (x - m) / jnp.sqrt(v + eps)

def _scatter_add(tgt, idx, src, axis=0):
    return tgt.at[idx].add(src)

def _segment_sum(src, seg, n):
    return jax.ops.segment_sum(src, seg, n)
kernel_name = 'mk_xattn_ffn_d2_seqx_r8_4420fe'

def setup_inputs(seed: int=0):
    np.random.seed(seed)
    _w = jnp.asarray

    def _rec_inputs():
        import jax
        import jax.numpy as jnp
        _rk = jax.random.key(seed)
        x = -0.000125 + 0.9999 * jax.random.normal(jax.random.fold_in(_rk, 1), (2, 256, 512), jnp.float32)
        _lenS = 256 - jax.random.randint(jax.random.fold_in(_rk, 7), (2,), 0, max(1, 256 // 4) + 1, jnp.int32)
        _lenS2 = 512 - jax.random.randint(jax.random.fold_in(_rk, 8), (2,), 0, max(1, 512 // 4) + 1, jnp.int32)
        _ctx_4096P = jax.random.normal(jax.random.fold_in(_rk, 11), (2, 16, 512), jnp.float32)
        _ctx_4096c = jax.random.dirichlet(jax.random.fold_in(_rk, 511), 0.3 * jnp.ones((16,), jnp.float32), (2, 512))
        _ctx_4096t = jnp.einsum('bsk,bkd->bsd', _ctx_4096c, _ctx_4096P)
        _ctx_4096t = _ctx_4096t * jax.lax.rsqrt(jnp.mean(jnp.square(_ctx_4096t)) + 1e-12) * 0.953939
        ctx_4096 = -5.72187e-05 + 0.999849 * (_ctx_4096t + 0.3 * jax.random.normal(jax.random.fold_in(_rk, 611), (2, 512, 512), jnp.float32))
        return (x, ctx_4096)
    x, ctx_4096 = _rec_inputs()

    def _L0_xattn_setup():
        import jax, jax.numpy as jnp
        import numpy as np
        QMIN = 0.0
        QMAX = 255.0

        def fake_quant(x, scale, zp):
            s = scale.reshape(())
            z = zp.reshape(())
            q = jnp.clip(jnp.round(x / s + z), QMIN, QMAX)
            return (q - z) * s
        key = jax.random.key(seed)
        k1, k2 = jax.random.split(key)
        B, M, K, N = (4, 256, 512, 512)
        x1 = jax.random.normal(k1, (B, M, K), dtype=jnp.float32)
        x2 = jax.random.normal(k2, (B, K, N), dtype=jnp.float32)
        x1_scale = jnp.full((1,), 8.0 / 255.0, dtype=jnp.float32)
        x1_zp = jnp.full((1,), 128.0, dtype=jnp.float32)
        x2_scale = jnp.full((1,), 8.0 / 255.0, dtype=jnp.float32)
        x2_zp = jnp.full((1,), 128.0, dtype=jnp.float32)
        return {'x1': x1, 'x2': x2, 'x1_scale': x1_scale, 'x1_zp': x1_zp, 'x2_scale': x2_scale, 'x2_zp': x2_zp}
    _L0_xattn_all = _L0_xattn_setup()
    _L0_xattn_in = {k: v for k, v in _L0_xattn_all.items() if k in ('x1_scale', 'x1_zp', 'x2_scale', 'x2_zp')}
    del _L0_xattn_all

    def _L0_ffn_setup():
        import jax, jax.numpy as jnp
        import numpy as np
        DIM = 512
        INTER = 1792
        SPARSITY = 32
        RANK = 16
        key = jax.random.key(seed)
        ks = jax.random.split(key, 5)
        B, T = (32, 1)
        x = jax.random.normal(ks[0], (B, T, DIM), dtype=jnp.float32)
        c1_w = jax.random.normal(ks[1], (RANK, DIM), dtype=jnp.float32) * (1.0 / np.sqrt(DIM))
        c2_w = jax.random.normal(ks[2], (INTER, RANK), dtype=jnp.float32) * (1.0 / np.sqrt(RANK))
        w1 = jax.random.normal(ks[3], (INTER, DIM), dtype=jnp.float32) * (1.0 / np.sqrt(DIM))
        w2t = jax.random.normal(ks[4], (INTER, DIM), dtype=jnp.float32) * (1.0 / np.sqrt(INTER))
        return {'x': x, 'c1_w': c1_w, 'c2_w': c2_w, 'w1': w1, 'w2t': w2t}
    _L0_ffn_all = _L0_ffn_setup()
    _L0_ffn_in = {k: v for k, v in _L0_ffn_all.items() if k in ('c1_w', 'c2_w', 'w1', 'w2t')}
    del _L0_ffn_all

    def _L1_xattn_setup():
        import jax, jax.numpy as jnp
        import numpy as np
        HID = 512
        NHEAD = 32
        NKV = 8
        HDIM = 128
        G = NHEAD // NKV
        key = jax.random.key(seed)
        ks = jax.random.split(key, 6)
        s = 0.02
        B, L = (2, 256)
        return {'query': jax.random.normal(ks[0], (B, L, HID), jnp.float32), 'kv': jax.random.normal(ks[1], (B, L, HID), jnp.float32), 'Wq': jax.random.normal(ks[2], (HID, NHEAD * HDIM), jnp.float32) * s, 'bq': jnp.zeros((NHEAD * HDIM,), jnp.float32), 'Wkv': jax.random.normal(ks[3], (HID, 2 * NKV * HDIM), jnp.float32) * s, 'bkv': jnp.zeros((2 * NKV * HDIM,), jnp.float32), 'Wo': jax.random.normal(ks[4], (NHEAD * HDIM, HID), jnp.float32) * s, 'bo': jnp.zeros((HID,), jnp.float32)}
    _L1_xattn_all = _L1_xattn_setup()
    _L1_xattn_in = {k: v for k, v in _L1_xattn_all.items() if k in ('Wq', 'bq', 'Wkv', 'bkv', 'Wo', 'bo')}
    del _L1_xattn_all

    def _L1_ffn_setup():
        import jax, jax.numpy as jnp
        import numpy as np
        R = 16
        LORA_ALPHA = 16
        SCALING = LORA_ALPHA / R
        key = jax.random.key(seed)
        kx, kr, ka = jax.random.split(key, 3)
        B, S, D, DO, E = (4, 256, 512, 512, 8)
        x = jax.random.normal(kx, (B, S, D), dtype=jnp.float32)
        bound_r = 1.0 / np.sqrt(D)
        route_w = jax.random.uniform(kr, (E, D), jnp.float32, -bound_r, bound_r)
        bound_a = 1.0 / np.sqrt(D)
        A = jax.random.uniform(ka, (E, R, D), jnp.float32, -bound_a, bound_a)
        kb = jax.random.fold_in(key, 7)
        Bw = jax.random.normal(kb, (E, DO, R), dtype=jnp.float32) * 0.02
        return {'x': x, 'route_w': route_w, 'A': A, 'Bw': Bw}
    _L1_ffn_all = _L1_ffn_setup()
    _L1_ffn_in = {k: v for k, v in _L1_ffn_all.items() if k in ('route_w', 'A', 'Bw')}
    del _L1_ffn_all
    return {'x': x, 'ctx_4096': ctx_4096, 'L0_xattn_x1_scale': _L0_xattn_in['x1_scale'], 'L0_xattn_x1_zp': _L0_xattn_in['x1_zp'], 'L0_xattn_x2_scale': _L0_xattn_in['x2_scale'], 'L0_xattn_x2_zp': _L0_xattn_in['x2_zp'], 'L0_ffn_c1_w': _L0_ffn_in['c1_w'], 'L0_ffn_c2_w': _L0_ffn_in['c2_w'], 'L0_ffn_w1': _L0_ffn_in['w1'], 'L0_ffn_w2t': _L0_ffn_in['w2t'], 'L1_xattn_Wq': _L1_xattn_in['Wq'], 'L1_xattn_bq': _L1_xattn_in['bq'], 'L1_xattn_Wkv': _L1_xattn_in['Wkv'], 'L1_xattn_bkv': _L1_xattn_in['bkv'], 'L1_xattn_Wo': _L1_xattn_in['Wo'], 'L1_xattn_bo': _L1_xattn_in['bo'], 'L1_ffn_route_w': _L1_ffn_in['route_w'], 'L1_ffn_A': _L1_ffn_in['A'], 'L1_ffn_Bw': _L1_ffn_in['Bw']}

def reference(x, ctx_4096, L0_xattn_x1_scale, L0_xattn_x1_zp, L0_xattn_x2_scale, L0_xattn_x2_zp, L0_ffn_c1_w, L0_ffn_c2_w, L0_ffn_w1, L0_ffn_w2t, L1_xattn_Wq, L1_xattn_bq, L1_xattn_Wkv, L1_xattn_bkv, L1_xattn_Wo, L1_xattn_bo, L1_ffn_route_w, L1_ffn_A, L1_ffn_Bw):
    import jax
    import jax.numpy as jnp

    def _L0_xattn_ref(x1, x2, x1_scale, x1_zp, x2_scale, x2_zp):
        import jax, jax.numpy as jnp
        import numpy as np
        QMIN = 0.0
        QMAX = 255.0

        def fake_quant(x, scale, zp):
            s = scale.reshape(())
            z = zp.reshape(())
            q = jnp.clip(jnp.round(x / s + z), QMIN, QMAX)
            return (q - z) * s
        q1 = fake_quant(x1, x1_scale, x1_zp)
        q2 = fake_quant(x2, x2_scale, x2_zp)
        return jnp.matmul(q1, q2)

    def _L0_ffn_ref(x, c1_w, c2_w, w1, w2t):
        import jax, jax.numpy as jnp
        import numpy as np
        DIM = 512
        INTER = 1792
        SPARSITY = 32
        RANK = 16
        B, T, M = x.shape
        xf = x.reshape(B * T, M)
        inter = xf @ c1_w.T @ c2_w.T
        n_blocks = INTER // SPARSITY
        blk = inter.reshape(B * T, n_blocks, SPARSITY)
        idx = jnp.argmax(blk, axis=-1) + jnp.arange(0, INTER, SPARSITY)
        w1_g = w1[idx]
        w2_g = w2t[idx]
        h = jax.nn.relu(jnp.einsum('bkm,bm->bk', w1_g, xf))
        out = jnp.einsum('bk,bkm->bm', h, w2_g)
        return out.reshape(B, T, M)

    def _L1_xattn_ref(query, kv, Wq, bq, Wkv, bkv, Wo, bo):
        import jax, jax.numpy as jnp
        import numpy as np
        HID = 512
        NHEAD = 32
        NKV = 8
        HDIM = 128
        G = NHEAD // NKV
        B, L, _ = query.shape
        Lk = kv.shape[1]
        scale = jnp.asarray(1.0 / np.sqrt(HDIM), query.dtype)
        q = (query @ Wq + bq).reshape(B, L, NKV, G, HDIM)
        k_, v_ = jnp.split(kv @ Wkv + bkv, 2, axis=-1)
        k = k_.reshape(B, Lk, NKV, HDIM)
        v = v_.reshape(B, Lk, NKV, HDIM)
        scores = jnp.einsum('blkgd,bmkd->bkglm', q, k) * scale
        attn = jax.nn.softmax(scores, axis=-1)
        o = jnp.einsum('bkglm,bmkd->blkgd', attn, v).reshape(B, L, NHEAD * HDIM)
        return o @ Wo + bo

    def _L1_ffn_ref(x, route_w, A, Bw):
        import jax, jax.numpy as jnp
        import numpy as np
        R = 16
        LORA_ALPHA = 16
        SCALING = LORA_ALPHA / R
        logits = jnp.einsum('bsd,ed->bse', x, route_w)
        topk_v, topk_idx = jax.lax.top_k(logits, 1)
        E = logits.shape[-1]
        route_weight = jax.nn.one_hot(topk_idx[..., 0], E, dtype=logits.dtype) * topk_v
        h = jnp.einsum('bsd,erd->bser', x, A)
        wh = route_weight[..., None] * h
        out = jnp.einsum('bser,eor->bso', wh, Bw) * SCALING
        return out
    x = x + _L0_xattn_ref(_layernorm(x, axis=-1), ctx_4096, L0_xattn_x1_scale, L0_xattn_x1_zp, L0_xattn_x2_scale, L0_xattn_x2_zp)
    x = x + _L0_ffn_ref(_layernorm(x, axis=-1), L0_ffn_c1_w, L0_ffn_c2_w, L0_ffn_w1, L0_ffn_w2t)
    x = x + _L1_xattn_ref(_layernorm(x, axis=-1), ctx_4096, L1_xattn_Wq, L1_xattn_bq, L1_xattn_Wkv, L1_xattn_bkv, L1_xattn_Wo, L1_xattn_bo)
    x = x + _L1_ffn_ref(_layernorm(x, axis=-1), L1_ffn_route_w, L1_ffn_A, L1_ffn_Bw)
    return x

_drawn_inputs = setup_inputs


def setup_inputs(seed=0):
    import zlib

    import numpy as np

    out = dict(_drawn_inputs(seed))
    spreads = {'L1_xattn_bq': (0.0, 0.8), 'L1_xattn_bkv': (0.0, 0.8), 'L1_xattn_bo': (0.0, 0.8)}
    factors = {'L0_ffn_c1_w': 8.0,
     'L0_ffn_c2_w': 8.0,
     'L0_ffn_w1': 8.0,
     'L0_ffn_w2t': 8.0,
     'L1_xattn_Wq': 8.0,
     'L1_xattn_Wkv': 3.934,
     'L1_xattn_Wo': 3.647,
     'L1_ffn_route_w': 8.0,
     'L1_ffn_A': 8.0,
     'L1_ffn_Bw': 8.0}
    for name, (base, spread) in spreads.items():
        noise = np.random.default_rng([zlib.crc32(name.encode()), seed]).standard_normal(out[name].shape)
        drawn = base * np.exp(spread * noise) if base else spread * noise
        out[name] = jnp.asarray(drawn.astype(out[name].dtype))
    for name, factor in factors.items():
        out[name] = (out[name] * factor).astype(out[name].dtype)
    return out
```

```python
from contextlib import ExitStack

import concourse.bass as bass
from concourse import mybir

ALU = mybir.AluOpType
ACT = mybir.ActivationFunctionType
AX_X = mybir.AxisListType.X
F32 = mybir.dt.float32
F32R = mybir.dt.float32r
BF16 = mybir.dt.bfloat16

P = 128
BATCH, SEQ, DIM, CTX = 2, 256, 512, 512
TOK = BATCH * SEQ
TT = TOK // P
KD = DIM // P
MT = CTX // P
INTER, BLK, RANK = 1792, 32, 16
CHUNK = 256
NCHUNK = INTER // CHUNK
CI = CHUNK // P
NHEAD, NKV, HDIM = 32, 8, 128
G = NHEAD // NKV
EXP, ER = 8, 128
EPS = 1e-5
QMAX = 255.0
CENTRE = 128.0
ROUND = 1.5 * 2.0 ** 23
SCALE = 1.0 / HDIM ** 0.5
RING = 5
UNITS = 16


def xattn_ffn_kernel(nc: bass.Bass, x_in, ctx_in, s1_in, z1_in, s2_in, z2_in, c1_in, c2_in, w1_in, w2_in,
                     wq_in, bq_in, wkv_in, bkv_in, wo_in, bo_in, route_in, a_in, bw_in, out):
    with ExitStack() as ctx:
        def sbuf(stack, name, shape, dt):
            return stack.enter_context(nc.sbuf_tensor(name, shape, dt))

        def pair(stack, name, shape):
            return (sbuf(stack, name + "_hi", shape, F32R), sbuf(stack, name + "_lo", shape, F32R))

        def sem(name):
            return ctx.enter_context(nc.semaphore(name))

        x = sbuf(ctx, "x", [P, TT, DIM], F32)
        ctxT = pair(ctx, "ctxT", [P, KD, BATCH * CTX])
        xT = pair(ctx, "xT", [P, KD, TOK])
        bo_row = sbuf(ctx, "bo_row", [P, DIM], F32)
        ident = sbuf(ctx, "ident", [P, P], F32)
        ident_b = sbuf(ctx, "ident_b", [P, P], BF16)
        ones_b = sbuf(ctx, "ones_b", [P, P], BF16)
        bias_all = sbuf(ctx, "bias_all", [P, 48], F32)
        bias_q = sbuf(ctx, "bias_q", [P, G], F32)
        bias_k = sbuf(ctx, "bias_k", [P, 1], F32)
        bias_v = sbuf(ctx, "bias_v", [P, 1], F32)
        stats = sbuf(ctx, "stats", [P, TT, 6], F32)
        moments = sbuf(ctx, "moments", [P, TT, 2], F32)
        ln_a = sbuf(ctx, "ln_a", [P, TT], F32)
        ln_b = sbuf(ctx, "ln_b", [P, TT], F32)
        ln_c = sbuf(ctx, "ln_c", [P, TT], F32)
        rstd = sbuf(ctx, "rstd", [P, TT], F32)
        scal = sbuf(ctx, "scal", [P, 4], F32)
        derived = sbuf(ctx, "derived", [P, 10], F32)
        row_sum = sbuf(ctx, "row_sum", [P, TT], F32)
        row_add = sbuf(ctx, "row_add", [P, TT], F32)
        neg_lo_t = sbuf(ctx, "neg_lo_t", [P, 1], F32)
        neg_lo_c = sbuf(ctx, "neg_lo_c", [P, 1], F32)
        neg_max = sbuf(ctx, "neg_max", [P, UNITS], F32)
        neg_bias = sbuf(ctx, "neg_bias", [P, UNITS], F32)
        exp_sum = sbuf(ctx, "exp_sum", [P, UNITS], F32)
        exp_inv = sbuf(ctx, "exp_inv", [P, UNITS], F32)
        w_raw = sbuf(ctx, "w_raw", [P, RING, 512], F32)
        wk = pair(ctx, "wk", [P, KD, HDIM])
        wv = pair(ctx, "wv", [P, KD, HDIM])
        desc8 = sbuf(ctx, "desc8", [P, TT, EXP], F32)
        with ExitStack() as early:
            wq = pair(early, "wq", [P, KD, G * HDIM])
            wq_end = nc.sbuf_base
        a_raw = sbuf(ctx, "a_raw", [P, DIM], F32)
        r_raw = sbuf(ctx, "r_raw", [EXP, DIM], F32)
        b_raw = sbuf(ctx, "b_raw", [P, KD, ER], F32)
        raT = sbuf(ctx, "raT", [P, KD, ER + EXP], F32)
        bT = sbuf(ctx, "bT", [P, DIM], F32)
        whT = sbuf(ctx, "whT", [P, TOK], F32)
        wh = sbuf(ctx, "wh", [P, ER], F32)
        logits = sbuf(ctx, "logits", [P, TT, EXP], F32)
        top = sbuf(ctx, "top", [P, TT], F32)
        r_eq = sbuf(ctx, "r_eq", [P, TT, EXP], F32)
        r_key = sbuf(ctx, "r_key", [P, TT, EXP], F32)
        r_first = sbuf(ctx, "r_first", [P, TT], F32)
        r_gate = sbuf(ctx, "r_gate", [P, TT, EXP], F32)
        wh2 = sbuf(ctx, "wh2", [P, ER], F32)
        sbuf(ctx, "fill", [P, (wq_end - nc.sbuf_base) // 4], F32)
        xT3 = w_raw
        with ExitStack() as first:
            ctx_raw = sbuf(first, "ctx_raw", [P, BATCH * MT, DIM], F32)
            ctx_q = sbuf(first, "ctx_q", [P, BATCH * MT, DIM], BF16)
            x_q = sbuf(first, "x_q", [P, TT, DIM], BF16)
            xqT = sbuf(first, "xqT", [P, KD, TOK], BF16)
            col_add = sbuf(first, "col_add", [P, BATCH, DIM], F32)
            c1_rep = sbuf(first, "c1_rep", [P, DIM], F32)
            c1T = pair(first, "c1T", [P, KD, P])
            c2_raw = sbuf(first, "c2_raw", [P, INTER // P, RANK], F32)
            c2_rep = sbuf(first, "c2_rep", [P, INTER // P, 4, 32], F32)
            bias_rows = sbuf(first, "bias_rows", [48, HDIM], F32)
            c2_stack = sbuf(first, "c2_stack", [P, INTER], F32R)
            t_stack = sbuf(first, "t_stack", [P, TOK], F32R)
            one_hot = sbuf(first, "one_hot", [P, TT, CHUNK], BF16)
            oh_eq = sbuf(first, "oh_eq", [P, 16, BLK], BF16)
            oh_key = sbuf(first, "oh_key", [P, 16, BLK], BF16)
            oh_max = sbuf(first, "oh_max", [P, 16], F32)
            oh_first = sbuf(first, "oh_first", [P, 16], F32)
            desc = sbuf(first, "desc", [P, 16, BLK], BF16)
            w1_raw = sbuf(first, "w1_raw", [P, CI, DIM], F32)
            w2_raw = sbuf(first, "w2_raw", [P, CI, DIM], F32)
            w1T = pair(first, "w1T", [P, KD, CHUNK])
            w2 = pair(first, "w2", [P, CI, DIM])
            h = sbuf(first, "h", [P, 2, CHUNK], F32)
            hT = pair(first, "hT", [P, CI, TOK])
            xn = sbuf(first, "xn", [P, TT, DIM], F32)
        k = pair(ctx, "k", [P, BATCH * CTX])
        v = pair(ctx, "v", [P, BATCH * MT, HDIM])
        vT = sbuf(ctx, "vT", [P, BATCH * CTX], F32)
        q = pair(ctx, "q", [P, G, TOK])
        wo = pair(ctx, "wo", [P, G, DIM])
        prob = sbuf(ctx, "prob", [P, 4, CTX], F32)
        probT = [pair(ctx, f"probT{i}", [P, MT, 512]) for i in range(2)]
        o = pair(ctx, "o", [P, G, TOK])

        bank = [ctx.enter_context(nc.psum_tensor(f"bank{i}", [P, 512], F32)) for i in range(8)]

        ld_scal, ld_x, ld_c1, ld_c2, ld_bias, ld_bo = (sem(f"ld_{n}") for n in ("scal", "x", "c1", "c2", "bias", "bo"))
        ld_ctx = [sem(f"ld_ctx{b}") for b in range(BATCH)]
        ld_w1, ld_w2, ld_last = sem("ld_w1"), sem("ld_w2"), sem("ld_last")
        ld_w = [sem(f"ld_ring{s}") for s in range(RING)]
        stored = sem("stored")
        pool_step, pool_const = sem("pool_step"), sem("pool_const")
        dve_step = sem("dve_step")
        c1T_made, c1T_hi, c1T_lo = sem("c1T_made"), sem("c1T_hi"), sem("c1T_lo")
        c2_spread, c2_made, c2_hi, c2_lo = sem("c2_spread"), sem("c2_made"), sem("c2_hi"), sem("c2_lo")
        bias_made, bias_read = sem("bias_made"), sem("bias_read")
        x_quant, ctx_quant, xq_made, xqT_read = sem("x_quant"), sem("ctx_quant"), sem("xq_made"), sem("xqT_read")
        col_made, col_read, ab_made = sem("col_made"), sem("col_read"), sem("ab_made")
        ctxT_made, ctxT_hi, ctxT_lo = sem("ctxT_made"), sem("ctxT_hi"), sem("ctxT_lo")
        var_made, sqrt_made, xn_made = sem("var_made"), sem("sqrt_made"), sem("xn_made")
        xT_made, xT_hi, xT_lo = sem("xT_made"), sem("xT_hi"), sem("xT_lo")
        t_made, t_hi, t_lo = sem("t_made"), sem("t_hi"), sem("t_lo")
        raT_made, raT_read, bT_made, bT_read = sem("raT_made"), sem("raT_read"), sem("bT_made"), sem("bT_read")
        xT3_made, xT3_read, routed, gated = sem("xT3_made"), sem("xT3_read"), sem("routed"), sem("gated")
        whT_made, whT_read, out_made, x_final = sem("whT_made"), sem("whT_read"), sem("out_made"), sem("x_final")
        w1T_made, w1T_hi, w1T_lo = sem("w1T_made"), sem("w1T_hi"), sem("w1T_lo")
        w2_hi, w2_lo = sem("w2_hi"), sem("w2_lo")
        inter_made, oh_step = sem("inter_made"), sem("oh_step")
        h_made, h_masked, hT_made, hT_hi, hT_lo = (sem(n) for n in ("h_made", "h_masked", "hT_made", "hT_hi", "hT_lo"))
        y_made = sem("y_made")
        w_hi, w_lo = sem("w_hi"), sem("w_lo")
        proj_made, proj_hi, proj_read = sem("proj_made"), sem("proj_hi"), sem("proj_read")
        bias_set, bv_set = sem("bias_set"), sem("bv_set")
        s_made, max_made, exp_made, inv_made, prob_made = (
            sem(n) for n in ("s_made", "max_made", "exp_made", "inv_made", "prob_made"))
        nb_made = sem("nb_made")
        pT_made, pT_hi, pT_lo = sem("pT_made"), sem("pT_hi"), sem("pT_lo")
        o_made, o_hi, o_lo = sem("o_made"), sem("o_hi"), sem("o_lo")
        wo_made, wo_added = sem("wo_made"), sem("wo_added")

        x_rows = x_in.rearrange("b (t p) d -> p (b t) d", p=P)
        out_rows = out.rearrange("b (t p) d -> p (b t) d", p=P)
        ctx_rows = ctx_in.rearrange("b (t p) d -> b p t d", p=P)
        w1_rows = w1_in.rearrange("(c i p) d -> c p i d", i=CI, p=P)
        w2_rows = w2_in.rearrange("(c i p) d -> c p i d", i=CI, p=P)
        wq_cols = wq_in.rearrange("(k p) n -> k p n", p=P)
        wkv_cols = wkv_in.rearrange("(k p) n -> p k n", p=P)
        wo_rows = wo_in.rearrange("(g j p) d -> g j p d", j=G, p=P)

        def mm3(dst, left, right, start, stop, sl=None, sr=None):
            nc.tensor.matmul(dst, left(0), right(0), start=start, stop=False)
            nc.tensor.matmul(dst, left(0), right(1), start=False, stop=False)
            return nc.tensor.matmul(dst, left(1), right(0), start=False, stop=stop)

        block = ctx.enter_context(nc.Block())

        @block.sync
        def _(sp):
            for i, src in enumerate((s1_in, s2_in, z1_in, z2_in)):
                sp.dma_start(scal[:, i:i + 1], src.rearrange("(a n) -> a n", a=1).to_broadcast([P, 1])).then_inc(ld_scal, 16)
            sp.dma_start(x[:, :, :], x_rows).then_inc(ld_x, 16)
            for b in range(BATCH):
                sp.dma_start(ctx_raw[:, b * MT:(b + 1) * MT, :], ctx_rows[b]).then_inc(ld_ctx[b], 16)
            sp.dma_start(c2_raw[:, :, :], c2_in.rearrange("(i p) r -> p i r", p=P)).then_inc(ld_c2, 16)
            sp.wait_ge(pool_const, 1)
            for r in range(4):
                sp.dma_start(c1_rep[32 * r:32 * r + RANK, :], c1_in).then_inc(ld_c1, 16)
            sp.dma_start(bias_rows[0:32, :], bq_in.rearrange("(h d) -> h d", d=HDIM)).then_inc(ld_bias, 16)
            sp.dma_start(bias_rows[32:48, :], bkv_in.rearrange("(h d) -> h d", d=HDIM)).then_inc(ld_bias, 16)
            sp.dma_start(bo_row[:, :], bo_in.rearrange("(a n) -> a n", a=1).to_broadcast([P, DIM])).then_inc(ld_bo, 16)
            sp.dma_start(w1_raw[:, :, :], w1_rows[0]).then_inc(ld_w1, 16)
            sp.dma_start(w2_raw[:, :, :], w2_rows[0]).then_inc(ld_w2, 16)

            def weight(n, src, slot, shaped=False):
                if not isinstance(n, int) or n >= RING:
                    sp.wait_ge(w_lo, n - RING + 1)
                dst = w_raw[:, slot, :]
                if shaped:
                    dst = dst.rearrange("p (k n) -> p k n", k=KD)
                sp.dma_start(dst, src).then_inc(ld_w[slot], 16)

            def projection_weights(n0, s0, g):
                weight(n0, wkv_cols[:, :, bass.ts(g, HDIM)], s0 % RING, True)
                weight(n0 + 1, wkv_cols[:, :, bass.ds(g * HDIM + NKV * HDIM, HDIM)], (s0 + 1) % RING, True)
                for kk in range(KD):
                    weight(n0 + 2 + kk, wq_cols[kk, :, bass.ts(g, G * HDIM)], (s0 + 2 + kk) % RING)

            projection_weights(0, 0, 0)
            with sp.Fori(1, NCHUNK) as c:
                sp.wait_ge(w1T_made, 2 * c)
                sp.dma_start(w1_raw[:, :, :], w1_rows[c]).then_inc(ld_w1, 16)
                sp.wait_ge(w2_lo, c)
                sp.dma_start(w2_raw[:, :, :], w2_rows[c]).then_inc(ld_w2, 16)

            def out_weights(n0, s0, g):
                for j in range(G):
                    weight(n0 + j, wo_rows[g, j], (s0 + j) % RING)

            with sp.Fori(0, NKV - 1) as g:
                out_weights(6 + 10 * g, 6, g)
                projection_weights(10 + 10 * g, 10, g + 1)
            out_weights(6 + 10 * (NKV - 1), 6, NKV - 1)
            sp.wait_ge(proj_made, 10 * NKV)
            sp.dma_start(a_raw[:, :], a_in.rearrange("e r d -> (e r) d")).then_inc(ld_last, 16)
            sp.dma_start(r_raw[:, :], route_in).then_inc(ld_last, 16)
            for j in range(KD):
                sp.dma_start(b_raw[:, j, :].rearrange("p (e r) -> p e r", e=EXP),
                             bw_in[:, j * P:(j + 1) * P, :].rearrange("e p r -> p e r")).then_inc(ld_last, 16)
            for t in range(TT):
                sp.wait_ge(x_final, t + 1)
                sp.dma_start(out_rows[:, t, :], x[:, t, :]).then_inc(stored, 16)
            sp.wait_ge(stored, 16 * TT)

        @block.gpsimd
        def _(pool):
            nc.gpsimd.memset(c1_rep[:, :], 0.0).then_inc(pool_const, 1)
            nc.gpsimd.memset(ident[:, :], 0.0).then_inc(pool_step, 1)
            nc.gpsimd.memset(c2_rep[:, :, :, :], 0.0).then_inc(pool_const, 1)
            pool.wait_ge(pool_step, 1)
            nc.gpsimd.affine_select(out=ident[:, :], in_=ident[:, :], compare_op=ALU.not_equal, fill=1.0, base=0,
                                    pattern=[[-1, P]], channel_multiplier=1).then_inc(pool_const, 1)
            nc.gpsimd.iota(desc[:, :, :], pattern=[[0, 16], [-1, BLK]], base=BLK, channel_multiplier=0,
                           allow_small_or_imprecise_dtypes=True).then_inc(pool_const, 1)
            nc.gpsimd.iota(desc8[:, :, :], pattern=[[0, TT], [-1, EXP]], base=EXP, channel_multiplier=0,
                           allow_small_or_imprecise_dtypes=True).then_inc(pool_const, 1)
            pool.wait_ge(pool_const, 3)
            nc.gpsimd.tensor_copy(ident_b[:, :], ident[:, :]).then_inc(pool_const, 1)

            def low_half(n, slot_count, slot, dst_hi, dst_lo, shaped=False):
                pool.wait_ge(w_hi, n + 1)
                src = w_raw[:, slot, :]
                if shaped:
                    src = src.rearrange("p (k n) -> p k n", k=KD)
                nc.gpsimd.tensor_tensor(dst_lo, src, dst_hi, ALU.subtract).then_inc(w_lo, 1)

            def projection_low(n0, s0):
                low_half(n0, None, s0 % RING, wk[0][:, :, :], wk[1][:, :, :], True)
                low_half(n0 + 1, None, (s0 + 1) % RING, wv[0][:, :, :], wv[1][:, :, :], True)
                for kk in range(KD):
                    low_half(n0 + 2 + kk, None, (s0 + 2 + kk) % RING, wq[0][:, kk, :], wq[1][:, kk, :])

            projection_low(0, 0)
            with pool.Fori(0, NCHUNK) as c:
                pool.wait_ge(w2_hi, c + 1)
                nc.gpsimd.tensor_tensor(w2[1][:, :, :], w2_raw[:, :, :], w2[0][:, :, :], ALU.subtract).then_inc(w2_lo, 1)

            def normalise(g, u):
                pool.wait_ge(inv_made, UNITS * g + u + 1)
                nc.gpsimd.tensor_tensor(prob[:, u % 4, :], prob[:, u % 4, :], exp_inv[:, u:u + 1].to_broadcast([P, CTX]),
                                        ALU.mult).then_inc(prob_made, 1)

            def group(g, last):
                n0 = 6 + 10 * g
                for u in range(UNITS):
                    normalise(g, u)
                    if 2 <= u < 6:
                        j = u - 2
                        low_half(n0 + j, None, (6 + j) % RING, wo[0][:, j, :], wo[1][:, j, :])
                    if last:
                        continue
                    if u == 6:
                        low_half(n0 + 4, None, 10 % RING, wk[0][:, :, :], wk[1][:, :, :], True)
                    if u == 7:
                        low_half(n0 + 5, None, 11 % RING, wv[0][:, :, :], wv[1][:, :, :], True)
                    if 8 <= u < 12:
                        kk = u - 8
                        low_half(n0 + 6 + kk, None, (12 + kk) % RING, wq[0][:, kk, :], wq[1][:, kk, :])

            with pool.Fori(0, NKV - 1) as g:
                group(g, False)
            group(NKV - 1, True)

        @block.tensor
        def _(pe):
            pe.wait_ge(pool_const, 6)
            pe.wait_ge(ld_c1, 64)
            for kk in range(KD):
                ins = nc.tensor.transpose(bank[2][:, kk * P:(kk + 1) * P], c1_rep[:, kk * P:(kk + 1) * P], ident[:, :])
            ins.then_inc(c1T_made, 1)
            pe.wait_ge(c2_spread, 4)
            for b4 in range(4):
                for i in range(4 * b4, min(4 * b4 + 4, INTER // P)):
                    ins = nc.tensor.transpose(bank[3 + b4][:, (i % 4) * P:(i % 4 + 1) * P],
                                              c2_rep[:, i, :, :].rearrange("p a b -> p (a b)"), ident[:, :])
                ins.then_inc(c2_made, 1)
            pe.wait_ge(ld_bias, 32)
            nc.tensor.transpose(bank[7][:, 0:48], bias_rows[:, :], ident[0:48, 0:48]).then_inc(bias_made, 1)
            for t in range(TT):
                pe.wait_ge(x_quant, t + 1)
                if t >= 2:
                    pe.wait_ge(xqT_read, t - 1)
                for kk in range(KD):
                    ins = nc.tensor.transpose(bank[t % 2][:, :].bitcast(BF16)[:, kk * P:(kk + 1) * P],
                                              x_q[:, t, kk * P:(kk + 1) * P], ident_b[:, :])
                ins.then_inc(xq_made, 1)
            pe.wait_ge(xqT_read, TT)
            pe.wait_ge(c1T_lo, 1)
            pe.wait_ge(c2_lo, 1)
            for b in range(BATCH):
                pe.wait_ge(ctx_quant, b + 1)
                for kk in range(MT):
                    ins = nc.tensor.matmul(bank[2 + b][:, :], ones_b[:, :], ctx_q[:, b * MT + kk, :],
                                           start=(kk == 0), stop=(kk == MT - 1))
                ins.then_inc(col_made, 1)
                if b == 0:
                    pe.wait_ge(bias_read, 1)
                    pe.wait_ge(c2_lo, 4)
                for t in range(2 * b, 2 * b + 2):
                    for kk in range(MT):
                        ins = nc.tensor.matmul(bank[4 + t][:, :], xqT[:, kk, t * P:(t + 1) * P],
                                               ctx_q[:, b * MT + kk, :], start=(kk == 0), stop=(kk == MT - 1))
                    ins.then_inc(ab_made, 1)
            for b in range(BATCH):
                pe.wait_ge(ld_ctx[b], 16)
                for kk in range(KD):
                    n = b * KD + kk
                    if n >= 2:
                        pe.wait_ge(ctxT_lo, n - 1)
                    for m in range(MT):
                        ins = nc.tensor.transpose(bank[n % 2][:, m * P:(m + 1) * P],
                                                  ctx_raw[:, b * MT + m, kk * P:(kk + 1) * P], ident[:, :])
                    ins.then_inc(ctxT_made, 1)

            def x_transposed(n):
                for kk in range(KD):
                    if kk >= 2:
                        pe.wait_ge(xT_lo, KD * n + kk - 1)
                    for t in range(TT):
                        if kk == 0:
                            pe.wait_ge(xn_made, TT * (n + 1) + t + 1)
                        ins = nc.tensor.transpose(bank[kk % 2][:, t * P:(t + 1) * P], xn[:, t, kk * P:(kk + 1) * P],
                                                  ident[:, :])
                    ins.then_inc(xT_made, 1)

            pe.wait_ge(ctxT_lo, 2 * KD)
            x_transposed(0)
            pe.wait_ge(xT_lo, KD)
            pe.wait_ge(col_read, 1)
            for kk in range(KD):
                ins = mm3(bank[2][:, :], lambda s: c1T[s][:, kk, :], lambda s: xT[s][:, kk, :], kk == 0, kk == KD - 1)
            ins.then_inc(t_made, 1)

            def transpose_w1(c):
                pe.wait_ge(ld_w1, 16 * (c + 1))
                for part in range(2):
                    if not isinstance(c, int) or c >= 1:
                        pe.wait_ge(h_masked, 4 * c - 1 + part)
                    for kk in range(2):
                        for i in range(CI):
                            ins = nc.tensor.transpose(bank[1 + part][:, kk * CHUNK + i * P:kk * CHUNK + (i + 1) * P],
                                                      w1_raw[:, i, (2 * part + kk) * P:(2 * part + kk + 1) * P], ident[:, :])
                    ins.then_inc(w1T_made, 1)

            def inter(c, half):
                if half == 1:
                    pe.wait_ge(oh_step, 10 * c + 5)
                elif not isinstance(c, int) or c >= 1:
                    pe.wait_ge(oh_step, 10 * c)
                for t in range(2 * half, 2 * half + 2):
                    ins = nc.tensor.matmul(bank[0][:, (t % 2) * CHUNK:(t % 2 + 1) * CHUNK], t_stack[:, t * P:(t + 1) * P],
                                           c2_stack[:, bass.ts(c, CHUNK)], start=True, stop=True)
                ins.then_inc(inter_made, 1)

            def transpose_h(c, t):
                pe.wait_ge(h_masked, 4 * c + t + 1)
                if t >= 1:
                    pe.wait_ge(hT_lo, 4 * c + t)
                for i in range(CI):
                    ins = nc.tensor.transpose(bank[3][:, i * P:(i + 1) * P], h[:, t % 2, i * P:(i + 1) * P], ident[:, :])
                ins.then_inc(hT_made, 1)

            def down(c, t, first, last):
                pe.wait_ge(hT_lo, 4 * c + t + 1)
                for i in range(CI):
                    ins = mm3(bank[4 + t][:, :], lambda s: hT[s][:, i, t * P:(t + 1) * P], lambda s: w2[s][:, i, :],
                              first and i == 0, last and i == CI - 1)
                ins.then_inc(y_made, 1)

            def chunk(c, first, last):
                pe.wait_ge(w1T_lo, 2 * (c + 1))
                for t in range(TT):
                    if t >= 2:
                        pe.wait_ge(h_masked, 4 * c + t - 1)
                    for kk in range(KD):
                        ins = mm3(bank[1 + t % 2][:, 0:CHUNK], lambda s: xT[s][:, kk, t * P:(t + 1) * P],
                                  lambda s: w1T[s][:, kk, :], kk == 0, kk == KD - 1)
                    ins.then_inc(h_made, 1)
                    if t >= 1:
                        transpose_h(c, t - 1)
                if not last:
                    transpose_w1(c + 1)
                    inter(c + 1, 0)
                pe.wait_ge(w2_lo, c + 1)
                down(c, 0, first, last)
                transpose_h(c, 3)
                down(c, 1, first, last)
                if not last:
                    inter(c + 1, 1)
                down(c, 2, first, last)
                down(c, 3, first, last)

            pe.wait_ge(t_lo, 1)
            pe.wait_ge(col_read, 2)
            transpose_w1(0)
            inter(0, 0)
            inter(0, 1)
            chunk(0, True, False)
            with pe.Fori(1, NCHUNK - 1) as c:
                chunk(c, False, False)
            chunk(NCHUNK - 1, False, True)

            def project(idx, base, wo_base, out_ap, left, right, first_set):
                if idx >= 2:
                    pe.wait_ge(proj_read, base + idx - 1)
                else:
                    pe.wait_ge(wo_added, wo_base + 3 + idx)
                for kk in range(KD):
                    ins = mm3(out_ap, lambda s: left(s, kk), lambda s: right(s, kk), kk == 0, kk == KD - 1)
                ins.then_inc(proj_made, 1)

            def project_k(b, base, wb):
                project(b, base, wb, bank[6 + b][:, :], lambda s, kk: wk[s][:, kk, :],
                        lambda s, kk: ctxT[s][:, kk, b * CTX:(b + 1) * CTX], False)

            def project_vT(b, base, wb):
                project(2 + b, base, wb, bank[6 + b][:, :], lambda s, kk: wv[s][:, kk, :],
                        lambda s, kk: ctxT[s][:, kk, b * CTX:(b + 1) * CTX], False)

            def project_q(head, base, wb):
                idx = 4 if head == 0 else 6 + head
                project(idx, base, wb, bank[6 + idx % 2][:, :], lambda s, kk: wq[s][:, kk, head * HDIM:(head + 1) * HDIM],
                        lambda s, kk: xT[s][:, kk, :], False)

            def transpose_v(b, base):
                pe.wait_ge(proj_read, base + 4 + b)
                for m in range(MT):
                    ins = nc.tensor.transpose(bank[6 + (5 + b) % 2][:, m * P:(m + 1) * P],
                                              vT[:, b * CTX + m * P:b * CTX + (m + 1) * P], ident[:, :])
                ins.then_inc(proj_made, 1)

            def weights_ready(n):
                pe.wait_ge(w_lo, n)

            weights_ready(2)
            project_k(0, 0, 1)
            project_k(1, 0, 0)
            project_vT(0, 0, 0)
            project_vT(1, 0, 0)
            x_transposed(1)
            weights_ready(6)
            pe.wait_ge(xT_lo, 2 * KD)
            project_q(0, 0, 0)
            transpose_v(0, 0)
            transpose_v(1, 0)
            for head in range(1, G):
                project_q(head, 0, 0)

            def scores(g, u):
                quad, j = u // 4, u % 4
                b, head, lt = quad // 2, 2 * (quad % 2) + j // 2, j % 2
                if lt == 0 and b == 0:
                    pe.wait_ge(proj_read, 10 * g + (5 if head == 0 else 7 + head))
                if u >= 2:
                    pe.wait_ge(exp_made, UNITS * g + u - 1)
                at = b * SEQ + lt * P
                mm3(bank[u % 2][:, :], lambda s: q[s][:, head, at:at + P], lambda s: k[s][:, b * CTX:(b + 1) * CTX],
                    True, True).then_inc(s_made, 1)

            def transpose_p(g, u):
                pe.wait_ge(prob_made, UNITS * g + u + 1)
                if u >= 2:
                    pe.wait_ge(pT_lo, UNITS * g + u - 1)
                for m in range(MT):
                    ins = nc.tensor.transpose(bank[2 + u % 2][:, m * P:(m + 1) * P], prob[:, u % 4, m * P:(m + 1) * P],
                                              ident[:, :])
                ins.then_inc(pT_made, 1)

            def values(g, quad):
                b = quad // 2
                pe.wait_ge(pT_lo, UNITS * g + 4 * quad + 4)
                if quad >= 1:
                    pe.wait_ge(o_lo, 4 * g + quad)
                for m in range(MT):
                    ins = mm3(bank[4][:, :], lambda s: v[s][:, b * MT + m, :], lambda s: probT[quad % 2][s][:, m, :],
                              m == 0, m == MT - 1)
                ins.then_inc(o_made, 1)

            def output(g, t, last):
                pe.wait_ge(o_lo, 4 * g + 4)
                if t < 2:
                    pe.wait_ge(proj_read, 10 * NKV if last else 10 * g + 19 + t)
                else:
                    pe.wait_ge(wo_added, 4 * g + 4 + t - 1)
                for j in range(G):
                    ins = mm3(bank[6 + t % 2][:, :], lambda s: o[s][:, j, t * P:(t + 1) * P], lambda s: wo[s][:, j, :],
                              j == 0, j == G - 1)
                ins.then_inc(wo_made, 1)

            def group(g, last):
                base, wb = 10 * g + 10, 4 * g
                for u in range(UNITS):
                    scores(g, u)
                    if u >= 3:
                        transpose_p(g, u - 3)
                    if u >= 7 and u % 4 == 3:
                        values(g, (u - 7) // 4)
                transpose_p(g, 13)
                if not last:
                    weights_ready(16 + 10 * g)
                    project_k(0, base, wb)
                transpose_p(g, 14)
                transpose_p(g, 15)
                if not last:
                    project_k(1, base, wb)
                values(g, 3)
                if not last:
                    project_vT(0, base, wb)
                    project_vT(1, base, wb)
                    project_q(0, base, wb)
                    transpose_v(0, base)
                    transpose_v(1, base)
                    for head in range(1, G):
                        project_q(head, base, wb)
                else:
                    weights_ready(10 + 10 * g)
                for t in range(TT):
                    output(g, t, last)

            with pe.Fori(0, NKV - 1) as g:
                group(g, False)
            group(NKV - 1, True)

            pe.wait_ge(ld_last, 16 * (2 + KD))
            for kk in range(KD):
                if kk >= 2:
                    pe.wait_ge(raT_read, kk - 1)
                nc.tensor.transpose(bank[2 + kk % 2][:, 0:ER], a_raw[:, kk * P:(kk + 1) * P], ident[:, :])
                nc.tensor.transpose(bank[2 + kk % 2][:, ER:ER + EXP], r_raw[:, kk * P:(kk + 1) * P],
                                    ident[0:EXP, 0:EXP]).then_inc(raT_made, 1)
            for j in range(KD):
                ins = nc.tensor.transpose(bank[4][:, j * P:(j + 1) * P], b_raw[:, j, :], ident[:, :])
            ins.then_inc(bT_made, 1)
            for kk in range(KD):
                if kk >= 2:
                    pe.wait_ge(xT3_read, kk - 1)
                for t in range(TT):
                    if kk == 0:
                        pe.wait_ge(xn_made, 3 * TT + t + 1)
                    ins = nc.tensor.transpose(bank[kk % 2][:, t * P:(t + 1) * P], xn[:, t, kk * P:(kk + 1) * P], ident[:, :])
                ins.then_inc(xT3_made, 1)
            pe.wait_ge(xT3_read, KD)
            pe.wait_ge(raT_read, KD)
            pe.wait_ge(bT_read, 1)
            for t in range(TT):
                for kk in range(KD):
                    ins = nc.tensor.matmul(bank[4 + t][:, 0:ER + EXP], xT3[:, kk, t * P:(t + 1) * P], raT[:, kk, :],
                                           start=(kk == 0), stop=(kk == KD - 1))
                ins.then_inc(routed, 1)
            for t in range(TT):
                pe.wait_ge(gated, t + 1)
                if t >= 2:
                    pe.wait_ge(whT_read, t - 1)
                nc.tensor.transpose(bank[2 + t % 2][:, 0:P], (wh, wh2)[t % 2][:, :], ident[:, :]).then_inc(whT_made, 1)
            for t in range(TT):
                pe.wait_ge(whT_read, t + 1)
                nc.tensor.matmul(bank[4 + t][:, :], whT[:, t * P:(t + 1) * P], bT[:, :], start=True, stop=True)\
                    .then_inc(out_made, 1)

        @block.scalar
        def _(act):
            def root(n):
                act.wait_ge(var_made, n + 1)
                nc.scalar.activation(ln_b[:, :], ln_a[:, :], ACT.Sqrt).then_inc(sqrt_made, 1)

            root(0)
            act.wait_ge(c1T_made, 1)
            nc.scalar.copy(c1T[0][:, :, :].rearrange("p k n -> p (k n)"), bank[2][:, :]).then_inc(c1T_hi, 1)
            for b4 in range(4):
                at, n = 512 * b4, min(512, INTER - 512 * b4)
                act.wait_ge(c2_made, b4 + 1)
                nc.scalar.copy(c2_stack[:, at:at + n], bank[3 + b4][:, 0:n]).then_inc(c2_hi, 1)
            act.wait_ge(bias_made, 1)
            nc.scalar.copy(bias_all[:, :], bank[7][:, 0:48]).then_inc(bias_read, 1)

            for t in range(TT):
                act.wait_ge(xq_made, t + 1)
                nc.scalar.copy(xqT[:, :, t * P:(t + 1) * P],
                               bank[t % 2][:, 0:256].bitcast(BF16).rearrange("p (k n) -> p k n", k=KD)).then_inc(xqT_read, 1)
            root(1)
            for n in range(2 * KD):
                act.wait_ge(ctxT_made, n + 1)
                b, kk = n // KD, n % KD
                nc.scalar.copy(ctxT[0][:, kk, b * CTX:(b + 1) * CTX], bank[n % 2][:, :]).then_inc(ctxT_hi, 1)

            def x_high(n):
                for kk in range(KD):
                    act.wait_ge(xT_made, KD * n + kk + 1)
                    nc.scalar.copy(xT[0][:, kk, :], bank[kk % 2][:, :]).then_inc(xT_hi, 1)

            x_high(0)
            act.wait_ge(t_made, 1)
            nc.scalar.copy(t_stack[:, :], bank[2][:, :]).then_inc(t_hi, 1)

            def w1_high(c):
                for part in range(2):
                    act.wait_ge(w1T_made, 2 * c + part + 1)
                    nc.scalar.copy(w1T[0][:, 2 * part:2 * part + 2, :],
                                   bank[1 + part][:, :].rearrange("p (k n) -> p k n", k=2)).then_inc(w1T_hi, 1)

            def h_high(c, t):
                act.wait_ge(hT_made, 4 * c + t + 1)
                nc.scalar.copy(hT[0][:, :, t * P:(t + 1) * P],
                               bank[3][:, 0:CHUNK].rearrange("p (i n) -> p i n", i=CI)).then_inc(hT_hi, 1)

            def chunk(c, last):
                for t in range(TT - 1):
                    h_high(c, t)
                if not last:
                    w1_high(c + 1)
                h_high(c, TT - 1)

            w1_high(0)
            with act.Fori(0, NCHUNK - 1) as c:
                chunk(c, False)
            chunk(NCHUNK - 1, True)

            def k_high(s, b):
                if b == 0:
                    act.wait_ge(bias_set, 2 * s + 2)
                act.wait_ge(proj_made, 10 * s + b + 1)
                nc.scalar.activation(k[0][:, b * CTX:(b + 1) * CTX], bank[6 + b][:, :], ACT.Identity,
                                     bias=bias_k[:, 0:1]).then_inc(proj_hi, 1)

            def q_high(s, head):
                idx = 4 if head == 0 else 6 + head
                act.wait_ge(proj_made, 10 * s + idx + 1)
                nc.scalar.activation(q[0][:, head, :], bank[6 + idx % 2][:, :], ACT.Identity,
                                     bias=bias_q[:, head:head + 1]).then_inc(proj_hi, 1)

            def v_high(s, b):
                act.wait_ge(proj_made, 10 * s + 6 + b)
                nc.scalar.copy(v[0][:, b * MT:(b + 1) * MT, :],
                               bank[6 + (5 + b) % 2][:, :].rearrange("p (m d) -> p m d", m=MT)).then_inc(proj_hi, 1)

            k_high(0, 0)
            k_high(0, 1)
            root(2)
            x_high(1)
            q_high(0, 0)
            v_high(0, 0)
            v_high(0, 1)
            for head in range(1, G):
                q_high(0, head)

            def exponentials(g, u):
                act.wait_ge(max_made, UNITS * g + u + 1)
                nc.scalar.activation(prob[:, u % 4, :], bank[u % 2][:, :], ACT.Exp, bias=neg_bias[:, u:u + 1],
                                     scale=SCALE, accum_out=exp_sum[:, u:u + 1]).then_inc(exp_made, 1)

            def p_high(g, u):
                quad, j = u // 4, u % 4
                if quad >= 2 and j == 0:
                    act.wait_ge(o_made, 4 * g + quad - 1)
                act.wait_ge(pT_made, UNITS * g + u + 1)
                nc.scalar.copy(probT[quad % 2][0][:, :, j * P:(j + 1) * P],
                               bank[2 + u % 2][:, :].rearrange("p (m n) -> p m n", m=MT)).then_inc(pT_hi, 1)

            def o_high(g, quad):
                b, hp = quad // 2, quad % 2
                if quad == 0:
                    act.wait_ge(bv_set, g + 1)
                act.wait_ge(o_made, 4 * g + quad + 1)
                nc.scalar.activation(o[0][:, 2 * hp:2 * hp + 2, b * SEQ:(b + 1) * SEQ],
                                     bank[4][:, :].rearrange("p (h n) -> p h n", h=2), ACT.Identity,
                                     bias=bias_v[:, 0:1]).then_inc(o_hi, 1)

            def group(g, last):
                for u in range(UNITS):
                    if u >= 3:
                        p_high(g, u - 3)
                    exponentials(g, u)
                    if u in (9, 13):
                        o_high(g, (u - 9) // 4)
                p_high(g, 13)
                o_high(g, 2)
                if not last:
                    k_high(g + 1, 0)
                p_high(g, 14)
                p_high(g, 15)
                if not last:
                    k_high(g + 1, 1)
                o_high(g, 3)
                if not last:
                    q_high(g + 1, 0)
                    v_high(g + 1, 0)
                    v_high(g + 1, 1)
                    for head in range(1, G):
                        q_high(g + 1, head)

            with act.Fori(0, NKV - 1) as g:
                group(g, False)
            group(NKV - 1, True)

            for kk in range(KD):
                act.wait_ge(raT_made, kk + 1)
                nc.scalar.copy(raT[:, kk, :], bank[2 + kk % 2][:, 0:ER + EXP]).then_inc(raT_read, 1)
            act.wait_ge(bT_made, 1)
            nc.scalar.copy(bT[:, :], bank[4][:, :]).then_inc(bT_read, 1)
            root(3)
            act.wait_ge(w_lo, 10 * NKV)
            for kk in range(KD):
                act.wait_ge(xT3_made, kk + 1)
                nc.scalar.copy(xT3[:, kk, :], bank[kk % 2][:, :]).then_inc(xT3_read, 1)
            for t in range(TT):
                act.wait_ge(whT_made, t + 1)
                nc.scalar.copy(whT[:, t * P:(t + 1) * P], bank[2 + t % 2][:, 0:P]).then_inc(whT_read, 1)

        @block.vector
        def _(dve):
            steps = [0]

            def link(ins):
                steps[0] += 1
                ins.then_inc(dve_step, 1)
                dve.wait_ge(dve_step, steps[0])

            def note(ins):
                steps[0] += 1
                ins.then_inc(dve_step, 1)

            def noted():
                dve.wait_ge(dve_step, steps[0])

            nc.vector.memset(neg_lo_t[:, :], 0.0)
            nc.vector.memset(neg_lo_c[:, :], 0.0)
            note(nc.vector.memset(ones_b[:, :], 1.0))
            noted()
            note(nc.vector.memset(neg_lo_t[64:128, :], -1.0))
            note(nc.vector.memset(neg_lo_c[32:64, :], -1.0))
            note(nc.vector.memset(neg_lo_c[96:128, :], -1.0))
            dve.wait_ge(ld_scal, 64)
            note(nc.vector.reciprocal(derived[:, 0:2], scal[:, 0:2]))
            note(nc.vector.tensor_tensor(derived[:, 2:3], scal[:, 0:1], scal[:, 1:2], ALU.mult))
            note(nc.vector.tensor_scalar(derived[:, 3:5], scal[:, 2:4], CENTRE, None, ALU.subtract))
            noted()
            link(nc.vector.tensor_scalar(derived[:, 5:7], derived[:, 3:5], derived[:, 2:3], -1.0, ALU.mult, ALU.mult))
            link(nc.vector.tensor_scalar(derived[:, 7:8], derived[:, 5:6], derived[:, 4:5], -float(CTX), ALU.mult, ALU.mult))

            def layer_norm(n):
                for t in range(TT):
                    note(nc.vector.bn_stats(stats[:, t, :], x[:, t, :]))
                noted()
                for t in range(TT):
                    note(nc.vector.bn_aggr(moments[:, t, :], stats[:, t, :]))
                noted()
                nc.vector.tensor_scalar(ln_a[:, :], moments[:, :, 1], EPS, None, ALU.add).then_inc(var_made, 1)
                dve.wait_ge(sqrt_made, n + 1)
                link(nc.vector.reciprocal(ln_c[:, :], ln_b[:, :]))
                link(nc.vector.tensor_tensor(ln_b[:, :], ln_c[:, :], ln_c[:, :], ALU.mult))
                link(nc.vector.tensor_tensor(ln_b[:, :], ln_b[:, :], ln_a[:, :], ALU.mult))
                link(nc.vector.tensor_scalar(ln_b[:, :], ln_b[:, :], -0.5, 1.5, ALU.mult, ALU.add))
                link(nc.vector.tensor_tensor(rstd[:, :], ln_b[:, :], ln_c[:, :], ALU.mult))
                for t in range(TT):
                    nc.vector.tensor_scalar(xn[:, t, :], x[:, t, :], moments[:, t, 0:1], rstd[:, t:t + 1],
                                            ALU.subtract, ALU.mult).then_inc(xn_made, 1)

            def quantise(work, to, scale, zero):
                link(nc.vector.tensor_scalar(work, work, scale, zero, ALU.mult, ALU.add))
                link(nc.vector.tensor_scalar(work, work, 0.0, QMAX, ALU.max, ALU.min))
                return nc.vector.tensor_scalar(to, work, ROUND, ROUND + CENTRE, ALU.add, ALU.subtract)

            dve.wait_ge(pool_const, 2)
            dve.wait_ge(ld_c2, 16)
            for r in range(4):
                nc.vector.tensor_copy(c2_rep[:, :, r, 0:RANK], c2_raw[:, :, :]).then_inc(c2_spread, 1)
            dve.wait_ge(ld_x, 16)
            layer_norm(0)
            dve.wait_ge(xn_made, TT)
            for t in range(TT):
                quantise(xn[:, t, :], x_q[:, t, :], derived[:, 0:1], scal[:, 2:3]).then_inc(x_quant, 1)
            for b in range(BATCH):
                dve.wait_ge(ld_ctx[b], 16)
                part = slice(b * MT, (b + 1) * MT)
                if b == 0:
                    dve.wait_ge(x_quant, TT)
                else:
                    dve.wait_ge(ctx_quant, b)
                link(nc.vector.tensor_scalar(xn[:, :, :], ctx_raw[:, part, :], derived[:, 1:2], scal[:, 3:4], ALU.mult, ALU.add))
                link(nc.vector.tensor_scalar(xn[:, :, :], xn[:, :, :], 0.0, QMAX, ALU.max, ALU.min))
                nc.vector.tensor_scalar(ctx_q[:, part, :], xn[:, :, :], ROUND, ROUND + CENTRE, ALU.add,
                                        ALU.subtract).then_inc(ctx_quant, 1)
            dve.wait_ge(c1T_hi, 1)
            nc.vector.tensor_tensor(c1T[1][:, :, :].rearrange("p k n -> p (k n)"), bank[2][:, :],
                                    c1T[0][:, :, :].rearrange("p k n -> p (k n)"), ALU.subtract).then_inc(c1T_lo, 1)
            for b4 in range(4):
                at, n = 512 * b4, min(512, INTER - 512 * b4)
                dve.wait_ge(c2_hi, b4 + 1)
                nc.vector.scalar_tensor_tensor(c2_stack[:, at:at + n], c2_stack[:, at:at + n], neg_lo_c[:, 0:1],
                                               bank[3 + b4][:, 0:n], ALU.mult, ALU.add).then_inc(c2_lo, 1)
            link(nc.vector.tensor_reduce(row_sum[:, :], x_q[:, :, :], AX_X, ALU.add))
            link(nc.vector.tensor_scalar(row_add[:, :], row_sum[:, :], derived[:, 6:7], derived[:, 7:8], ALU.mult, ALU.add))
            for b in range(BATCH):
                dve.wait_ge(col_made, b + 1)
                nc.vector.tensor_scalar(col_add[:, b, :], bank[2 + b][:, :], derived[:, 5:6], None, ALU.mult)\
                    .then_inc(col_read, 1)
                dve.wait_ge(col_read, b + 1)
                for t in range(2 * b, 2 * b + 2):
                    note(nc.vector.scalar_tensor_tensor(x[:, t, :], x[:, t, :], row_add[:, t:t + 1], col_add[:, b, :],
                                                        ALU.add, ALU.add))
                noted()
                for t in range(2 * b, 2 * b + 2):
                    dve.wait_ge(ab_made, t + 1)
                    note(nc.vector.scalar_tensor_tensor(x[:, t, :], bank[4 + t][:, :], derived[:, 2:3], x[:, t, :],
                                                        ALU.mult, ALU.add))
            noted()
            layer_norm(1)
            for n in range(2 * KD):
                b, kk = n // KD, n % KD
                dve.wait_ge(ctxT_hi, n + 1)
                nc.vector.tensor_tensor(ctxT[1][:, kk, b * CTX:(b + 1) * CTX], bank[n % 2][:, :],
                                        ctxT[0][:, kk, b * CTX:(b + 1) * CTX], ALU.subtract).then_inc(ctxT_lo, 1)

            def x_low(n):
                for kk in range(KD):
                    dve.wait_ge(xT_hi, KD * n + kk + 1)
                    nc.vector.tensor_tensor(xT[1][:, kk, :], bank[kk % 2][:, :], xT[0][:, kk, :], ALU.subtract)\
                        .then_inc(xT_lo, 1)

            x_low(0)

            def weight_high(n, slot_turn, slot, dst, shaped=False):
                dve.wait_ge(ld_w[slot], 16 * slot_turn)
                src = w_raw[:, slot, :]
                if shaped:
                    src = src.rearrange("p (k n) -> p k n", k=KD)
                nc.vector.tensor_copy(dst, src).then_inc(w_hi, 1)

            weight_high(0, 1, 0, wk[0][:, :, :], True)
            weight_high(1, 1, 1, wv[0][:, :, :], True)
            for kk in range(3):
                weight_high(2 + kk, 1, 2 + kk, wq[0][:, kk, :])
            dve.wait_ge(t_hi, 1)
            nc.vector.scalar_tensor_tensor(t_stack[:, :], t_stack[:, :], neg_lo_t[:, 0:1], bank[2][:, :],
                                           ALU.mult, ALU.add).then_inc(t_lo, 1)

            def w1_low(c):
                for part in range(2):
                    dve.wait_ge(w1T_hi, 2 * c + part + 1)
                    nc.vector.tensor_tensor(w1T[1][:, 2 * part:2 * part + 2, :],
                                            bank[1 + part][:, :].rearrange("p (k n) -> p k n", k=2),
                                            w1T[0][:, 2 * part:2 * part + 2, :], ALU.subtract).then_inc(w1T_lo, 1)

            def first_maxima(c, half):
                s0 = 10 * c + 5 * half
                scores = bank[0][:, :].rearrange("p (n j) -> p n j", j=BLK)
                dve.wait_ge(inter_made, 2 * c + half + 1)
                nc.vector.tensor_reduce(oh_max[:, :], scores, AX_X, ALU.max).then_inc(oh_step, 1)
                dve.wait_ge(oh_step, s0 + 1)
                nc.vector.tensor_tensor(oh_eq[:, :, :], scores, oh_max[:, :].unsqueeze(2).to_broadcast([P, 16, BLK]),
                                        ALU.is_equal).then_inc(oh_step, 1)
                dve.wait_ge(oh_step, s0 + 2)
                nc.vector.tensor_tensor(oh_key[:, :, :], oh_eq[:, :, :], desc[:, :, :], ALU.mult).then_inc(oh_step, 1)
                dve.wait_ge(oh_step, s0 + 3)
                nc.vector.tensor_reduce(oh_first[:, :], oh_key[:, :, :], AX_X, ALU.max).then_inc(oh_step, 1)
                dve.wait_ge(oh_step, s0 + 4)
                nc.vector.tensor_tensor(one_hot[:, 2 * half:2 * half + 2, :].rearrange("p t (n j) -> p (t n) j", j=BLK),
                                        oh_key[:, :, :], oh_first[:, :].unsqueeze(2).to_broadcast([P, 16, BLK]),
                                        ALU.is_equal).then_inc(oh_step, 1)

            def mask(c, t):
                dve.wait_ge(h_made, 4 * c + t + 1)
                if t >= 2:
                    dve.wait_ge(hT_made, 4 * c + t - 1)
                nc.vector.scalar_tensor_tensor(h[:, t % 2, :], bank[1 + t % 2][:, 0:CHUNK], 0.0, one_hot[:, t, :],
                                               ALU.max, ALU.mult).then_inc(h_masked, 1)

            def h_low(c, t):
                dve.wait_ge(hT_hi, 4 * c + t + 1)
                nc.vector.tensor_tensor(hT[1][:, :, t * P:(t + 1) * P],
                                        bank[3][:, 0:CHUNK].rearrange("p (i n) -> p i n", i=CI),
                                        hT[0][:, :, t * P:(t + 1) * P], ALU.subtract).then_inc(hT_lo, 1)

            def chunk(c, first, last):
                dve.wait_ge(oh_step, 10 * c + 10)
                mask(c, 0)
                if not first:
                    dve.wait_ge(y_made, 4 * c)
                dve.wait_ge(ld_w2, 16 * (c + 1))
                nc.vector.tensor_copy(w2[0][:, :, :], w2_raw[:, :, :]).then_inc(w2_hi, 1)
                mask(c, 1)
                h_low(c, 0)
                mask(c, 2)
                h_low(c, 1)
                mask(c, 3)
                h_low(c, 2)
                if not last:
                    w1_low(c + 1)
                    first_maxima(c + 1, 0)
                h_low(c, 3)
                if not last:
                    first_maxima(c + 1, 1)

            w1_low(0)
            first_maxima(0, 0)
            first_maxima(0, 1)
            weight_high(5, 2, 0, wq[0][:, 3, :])
            chunk(0, True, False)
            with dve.Fori(1, NCHUNK - 1) as c:
                chunk(c, False, False)
            chunk(NCHUNK - 1, False, True)
            for t in range(TT):
                dve.wait_ge(y_made, 4 * (NCHUNK - 1) + t + 1)
                nc.vector.tensor_tensor(x[:, t, :], bank[4 + t][:, :], x[:, t, :], ALU.add).then_inc(wo_added, 1)

            def set_biases(s):
                nc.vector.tensor_copy(bias_q[:, :], bias_all[:, bass.ds(G * s, G)]).then_inc(bias_set, 1)
                nc.vector.tensor_copy(bias_k[:, :], bias_all[:, bass.ds(NHEAD + s, 1)]).then_inc(bias_set, 1)

            def k_low(s, b):
                if b == 0:
                    dve.wait_ge(bias_set, 2 * s + 2)
                dve.wait_ge(proj_hi, 8 * s + b + 1)
                nc.vector.scalar_tensor_tensor(k[1][:, b * CTX:(b + 1) * CTX], bank[6 + b][:, :], bias_k[:, 0:1],
                                               k[0][:, b * CTX:(b + 1) * CTX], ALU.add, ALU.subtract).then_inc(proj_read, 1)

            def vT_copy(s, b):
                dve.wait_ge(proj_made, 10 * s + 3 + b)
                nc.vector.tensor_copy(vT[:, b * CTX:(b + 1) * CTX], bank[6 + b][:, :]).then_inc(proj_read, 1)

            def q_low(s, head):
                idx = 4 if head == 0 else 6 + head
                dve.wait_ge(proj_hi, 8 * s + (3 if head == 0 else 5 + head))
                nc.vector.scalar_tensor_tensor(q[1][:, head, :], bank[6 + idx % 2][:, :], bias_q[:, head:head + 1],
                                               q[0][:, head, :], ALU.add, ALU.subtract).then_inc(proj_read, 1)

            def v_low(s, b):
                dve.wait_ge(proj_hi, 8 * s + 4 + b)
                nc.vector.tensor_tensor(v[1][:, b * MT:(b + 1) * MT, :],
                                        bank[6 + (5 + b) % 2][:, :].rearrange("p (m d) -> p m d", m=MT),
                                        v[0][:, b * MT:(b + 1) * MT, :], ALU.subtract).then_inc(proj_read, 1)

            dve.wait_ge(bias_read, 1)
            set_biases(0)
            k_low(0, 0)
            k_low(0, 1)
            dve.wait_ge(wo_added, TT)
            layer_norm(2)
            dve.wait_ge(ld_bo, 16)
            for t in range(TT):
                note(nc.vector.tensor_tensor(x[:, t, :], x[:, t, :], bo_row[:, :], ALU.add))
            noted()
            vT_copy(0, 0)
            vT_copy(0, 1)
            x_low(1)
            q_low(0, 0)
            v_low(0, 0)
            v_low(0, 1)
            for head in range(1, G):
                q_low(0, head)

            def row_max(g, u):
                dve.wait_ge(s_made, UNITS * g + u + 1)
                nc.vector.tensor_reduce(neg_max[:, u:u + 1], bank[u % 2][:, :], AX_X, ALU.max, negate=True).then_inc(nb_made, 1)
                dve.wait_ge(nb_made, UNITS * g + u + 1)
                nc.vector.tensor_scalar(neg_bias[:, u:u + 1], neg_max[:, u:u + 1], SCALE, None, ALU.mult).then_inc(max_made, 1)

            def inverse(g, u):
                dve.wait_ge(exp_made, UNITS * g + u + 1)
                nc.vector.reciprocal(exp_inv[:, u:u + 1], exp_sum[:, u:u + 1]).then_inc(inv_made, 1)

            def p_low(g, u):
                quad, j = u // 4, u % 4
                dve.wait_ge(pT_hi, UNITS * g + u + 1)
                nc.vector.tensor_tensor(probT[quad % 2][1][:, :, j * P:(j + 1) * P],
                                        bank[2 + u % 2][:, :].rearrange("p (m n) -> p m n", m=MT),
                                        probT[quad % 2][0][:, :, j * P:(j + 1) * P], ALU.subtract).then_inc(pT_lo, 1)

            def o_low(g, quad):
                b, hp = quad // 2, quad % 2
                if quad == 0:
                    dve.wait_ge(bv_set, g + 1)
                dve.wait_ge(o_hi, 4 * g + quad + 1)
                at = (slice(None), slice(2 * hp, 2 * hp + 2), slice(b * SEQ, (b + 1) * SEQ))
                nc.vector.scalar_tensor_tensor(o[1][at], bank[4][:, :].rearrange("p (h n) -> p h n", h=2), bias_v[:, 0:1],
                                               o[0][at], ALU.add, ALU.subtract).then_inc(o_lo, 1)

            def group(g, last):
                nc.vector.tensor_copy(bias_v[:, :], bias_all[:, bass.ds(NHEAD + NKV + g, 1)]).then_inc(bv_set, 1)
                n0 = 6 + 10 * g
                for u in range(UNITS):
                    row_max(g, u)
                    if u >= 1:
                        inverse(g, u - 1)
                    if u >= 3:
                        p_low(g, u - 3)
                    if u in (9, 13):
                        o_low(g, (u - 9) // 4)
                    i = u - 1
                    if 0 <= i < (4 if last else 10):
                        dst = (wo[0][:, i, :] if i < 4 else wk[0][:, :, :] if i == 4 else wv[0][:, :, :] if i == 5
                               else wq[0][:, i - 6, :])
                        weight_high(n0 + i, 2 * g + (6 + i) // RING + 1, (6 + i) % RING, dst, i in (4, 5))
                inverse(g, 15)
                p_low(g, 13)
                o_low(g, 2)
                if not last:
                    set_biases(g + 1)
                    k_low(g + 1, 0)
                p_low(g, 14)
                p_low(g, 15)
                if not last:
                    k_low(g + 1, 1)
                o_low(g, 3)
                if not last:
                    vT_copy(g + 1, 0)
                    vT_copy(g + 1, 1)
                    q_low(g + 1, 0)
                    v_low(g + 1, 0)
                    v_low(g + 1, 1)
                    for head in range(1, G):
                        q_low(g + 1, head)
                for t in range(TT):
                    dve.wait_ge(wo_added, 4 * g + t + 1)
                    dve.wait_ge(wo_made, 4 * g + t + 1)
                    nc.vector.tensor_tensor(x[:, t, :], bank[6 + t % 2][:, :], x[:, t, :], ALU.add).then_inc(wo_added, 1)

            with dve.Fori(0, NKV - 1) as g:
                group(g, False)
            group(NKV - 1, True)

            dve.wait_ge(wo_added, 4 * (NKV + 1))
            layer_norm(3)
            for t in range(TT):
                dve.wait_ge(routed, t + 1)
                note(nc.vector.tensor_copy(logits[:, t, :], bank[4 + t][:, ER:ER + EXP]))
            noted()
            link(nc.vector.tensor_reduce(top[:, :], logits[:, :, :], AX_X, ALU.max))
            link(nc.vector.tensor_tensor(r_eq[:, :, :], logits[:, :, :], top[:, :].unsqueeze(2).to_broadcast([P, TT, EXP]),
                                         ALU.is_equal))
            link(nc.vector.tensor_tensor(r_key[:, :, :], r_eq[:, :, :], desc8[:, :, :], ALU.mult))
            link(nc.vector.tensor_reduce(r_first[:, :], r_key[:, :, :], AX_X, ALU.max))
            link(nc.vector.tensor_tensor(r_gate[:, :, :], r_key[:, :, :],
                                         r_first[:, :].unsqueeze(2).to_broadcast([P, TT, EXP]), ALU.is_equal))
            link(nc.vector.tensor_tensor(r_gate[:, :, :], r_gate[:, :, :], top[:, :].unsqueeze(2).to_broadcast([P, TT, EXP]),
                                         ALU.mult))
            for t in range(TT):
                if t >= 2:
                    dve.wait_ge(whT_made, t - 1)
                nc.vector.tensor_tensor((wh, wh2)[t % 2][:, :].rearrange("p (e r) -> p e r", e=EXP),
                                        bank[4 + t][:, 0:ER].rearrange("p (e r) -> p e r", e=EXP),
                                        r_gate[:, t, :].unsqueeze(2).to_broadcast([P, EXP, ER // EXP]),
                                        ALU.mult).then_inc(gated, 1)
            for t in range(TT):
                dve.wait_ge(out_made, t + 1)
                nc.vector.tensor_tensor(x[:, t, :], bank[4 + t][:, :], x[:, t, :], ALU.add).then_inc(x_final, 1)


_INS = ["x", "ctx_4096", "L0_xattn_x1_scale", "L0_xattn_x1_zp", "L0_xattn_x2_scale", "L0_xattn_x2_zp", "L0_ffn_c1_w",
        "L0_ffn_c2_w", "L0_ffn_w1", "L0_ffn_w2t", "L1_xattn_Wq", "L1_xattn_bq", "L1_xattn_Wkv", "L1_xattn_bkv",
        "L1_xattn_Wo", "L1_xattn_bo", "L1_ffn_route_w", "L1_ffn_A", "L1_ffn_Bw"]
_OUTS = [((BATCH, SEQ, DIM), "float32")]


def kernel(**inputs):
    import numpy as _np
    import concourse.bacc as _bacc
    from concourse import mybir as _mybir
    from concourse.bass_utils import run_bass_kernel_spmd as _run

    nc = _bacc.Bacc("TRN2", target_bir_lowering=False, num_devices=1)
    arrays, args = {}, []
    for name in _INS:
        a = _np.ascontiguousarray(inputs[name])
        arrays[f"in_{name}_dram"] = a
        args.append(nc.dram_tensor(f"in_{name}_dram", a.shape, _mybir.dt.from_np(a.dtype), kind="ExternalInput").ap())
    for i, (shape, dtype) in enumerate(_OUTS):
        dt = _mybir.dt.from_np(_np.dtype(dtype))
        args.append(nc.dram_tensor(f"out_{i}_dram", shape, dt, kind="ExternalOutput").ap())
    xattn_ffn_kernel(nc, *args)
    r = _run(nc, [arrays], core_ids=[0])
    got = tuple(r.results[0][f"out_{i}_dram"] for i in range(len(_OUTS)))
    return got[0]
```

```python
from contextlib import ExitStack

import concourse.bass as bass
from concourse import mybir

ALU = mybir.AluOpType
ACT = mybir.ActivationFunctionType
AX_X = mybir.AxisListType.X
F32 = mybir.dt.float32
F32R = mybir.dt.float32r
BF16 = mybir.dt.bfloat16

P = 128
BATCH, SEQ, DIM, CTX = 2, 256, 512, 512
TOK = BATCH * SEQ
TT = TOK // P
KD = DIM // P
MT = CTX // P
INTER, BLK, RANK = 1792, 32, 16
CHUNK = 256
NCHUNK = INTER // CHUNK
CI = CHUNK // P
NHEAD, NKV, HDIM = 32, 8, 128
G = NHEAD // NKV
EXP, ER = 8, 128
EPS = 1e-5
QMAX = 255.0
CENTRE = 128.0
ROUND = 1.5 * 2.0 ** 23
SCALE = 1.0 / HDIM ** 0.5
RING = 5
UNITS = 16


def xattn_ffn_kernel(nc: bass.Bass, x_in, ctx_in, s1_in, z1_in, s2_in, z2_in, c1_in, c2_in, w1_in, w2_in,
                     wq_in, bq_in, wkv_in, bkv_in, wo_in, bo_in, route_in, a_in, bw_in, out):
    with ExitStack() as ctx:
        def sbuf(stack, name, shape, dt):
            return stack.enter_context(nc.sbuf_tensor(name, shape, dt))

        def pair(stack, name, shape):
            return (sbuf(stack, name + "_hi", shape, F32R), sbuf(stack, name + "_lo", shape, F32R))

        def sem(name):
            return ctx.enter_context(nc.semaphore(name))

        x = sbuf(ctx, "x", [P, TT, DIM], F32)
        ctxT = pair(ctx, "ctxT", [P, KD, BATCH * CTX])
        xT = pair(ctx, "xT", [P, KD, TOK])
        bo_row = sbuf(ctx, "bo_row", [P, DIM], F32)
        ident = sbuf(ctx, "ident", [P, P], F32)
        ident_b = sbuf(ctx, "ident_b", [P, P], BF16)
        ones_b = sbuf(ctx, "ones_b", [P, P], BF16)
        bias_all = sbuf(ctx, "bias_all", [P, 48], F32)
        bias_q = sbuf(ctx, "bias_q", [P, G], F32)
        bias_k = sbuf(ctx, "bias_k", [P, 1], F32)
        bias_v = sbuf(ctx, "bias_v", [P, 1], F32)
        stats = sbuf(ctx, "stats", [P, TT, 6], F32)
        moments = sbuf(ctx, "moments", [P, TT, 2], F32)
        ln_a = sbuf(ctx, "ln_a", [P, TT], F32)
        ln_b = sbuf(ctx, "ln_b", [P, TT], F32)
        ln_c = sbuf(ctx, "ln_c", [P, TT], F32)
        rstd = sbuf(ctx, "rstd", [P, TT], F32)
        scal = sbuf(ctx, "scal", [P, 4], F32)
        derived = sbuf(ctx, "derived", [P, 10], F32)
        row_sum = sbuf(ctx, "row_sum", [P, TT], F32)
        row_add = sbuf(ctx, "row_add", [P, TT], F32)
        neg_lo_t = sbuf(ctx, "neg_lo_t", [P, 1], F32)
        neg_lo_c = sbuf(ctx, "neg_lo_c", [P, 1], F32)
        neg_max = sbuf(ctx, "neg_max", [P, UNITS], F32)
        neg_bias = sbuf(ctx, "neg_bias", [P, UNITS], F32)
        exp_sum = sbuf(ctx, "exp_sum", [P, UNITS], F32)
        exp_inv = sbuf(ctx, "exp_inv", [P, UNITS], F32)
        w_raw = sbuf(ctx, "w_raw", [P, RING, 512], F32)
        wk = pair(ctx, "wk", [P, KD, HDIM])
        wv = pair(ctx, "wv", [P, KD, HDIM])
        desc8 = sbuf(ctx, "desc8", [P, TT, EXP], F32)
        with ExitStack() as early:
            wq = pair(early, "wq", [P, KD, G * HDIM])
            wq_end = nc.sbuf_base
        a_raw = sbuf(ctx, "a_raw", [P, DIM], F32)
        r_raw = sbuf(ctx, "r_raw", [EXP, DIM], F32)
        b_raw = sbuf(ctx, "b_raw", [P, KD, ER], F32)
        raT = sbuf(ctx, "raT", [P, KD, ER + EXP], F32)
        bT = sbuf(ctx, "bT", [P, DIM], F32)
        whT = sbuf(ctx, "whT", [P, TOK], F32)
        wh = sbuf(ctx, "wh", [P, ER], F32)
        logits = sbuf(ctx, "logits", [P, TT, EXP], F32)
        top = sbuf(ctx, "top", [P, TT], F32)
        r_eq = sbuf(ctx, "r_eq", [P, TT, EXP], F32)
        r_key = sbuf(ctx, "r_key", [P, TT, EXP], F32)
        r_first = sbuf(ctx, "r_first", [P, TT], F32)
        r_gate = sbuf(ctx, "r_gate", [P, TT, EXP], F32)
        wh2 = sbuf(ctx, "wh2", [P, ER], F32)
        sbuf(ctx, "fill", [P, (wq_end - nc.sbuf_base) // 4], F32)
        xT3 = w_raw
        with ExitStack() as first:
            ctx_raw = sbuf(first, "ctx_raw", [P, BATCH * MT, DIM], F32)
            ctx_q = sbuf(first, "ctx_q", [P, BATCH * MT, DIM], BF16)
            x_q = sbuf(first, "x_q", [P, TT, DIM], BF16)
            xqT = sbuf(first, "xqT", [P, KD, TOK], BF16)
            col_add = sbuf(first, "col_add", [P, BATCH, DIM], F32)
            c1_rep = sbuf(first, "c1_rep", [P, DIM], F32)
            c1T = pair(first, "c1T", [P, KD, P])
            c2_raw = sbuf(first, "c2_raw", [P, INTER // P, RANK], F32)
            c2_rep = sbuf(first, "c2_rep", [P, INTER // P, 4, 32], F32)
            bias_rows = sbuf(first, "bias_rows", [48, HDIM], F32)
            c2_stack = sbuf(first, "c2_stack", [P, INTER], F32R)
            t_stack = sbuf(first, "t_stack", [P, TOK], F32R)
            one_hot = sbuf(first, "one_hot", [P, TT, CHUNK], BF16)
            oh_eq = sbuf(first, "oh_eq", [P, 16, BLK], BF16)
            oh_key = sbuf(first, "oh_key", [P, 16, BLK], BF16)
            oh_max = sbuf(first, "oh_max", [P, 16], F32)
            oh_first = sbuf(first, "oh_first", [P, 16], F32)
            desc = sbuf(first, "desc", [P, 16, BLK], BF16)
            w1_raw = sbuf(first, "w1_raw", [P, CI, DIM], F32)
            w2_raw = sbuf(first, "w2_raw", [P, CI, DIM], F32)
            w1T = pair(first, "w1T", [P, KD, CHUNK])
            w2 = pair(first, "w2", [P, CI, DIM])
            h = sbuf(first, "h", [P, 2, CHUNK], F32)
            hT = pair(first, "hT", [P, CI, TOK])
            xn = sbuf(first, "xn", [P, TT, DIM], F32)
        k = pair(ctx, "k", [P, BATCH * CTX])
        v = pair(ctx, "v", [P, BATCH * MT, HDIM])
        vT = sbuf(ctx, "vT", [P, BATCH * CTX], F32)
        q = pair(ctx, "q", [P, G, TOK])
        wo = pair(ctx, "wo", [P, G, DIM])
        prob = sbuf(ctx, "prob", [P, 4, CTX], F32)
        probT = [pair(ctx, f"probT{i}", [P, MT, 512]) for i in range(2)]
        o = pair(ctx, "o", [P, G, TOK])

        bank = [ctx.enter_context(nc.psum_tensor(f"bank{i}", [P, 512], F32)) for i in range(8)]

        ld_scal, ld_x, ld_c1, ld_c2, ld_bias, ld_bo = (sem(f"ld_{n}") for n in ("scal", "x", "c1", "c2", "bias", "bo"))
        ld_ctx = [sem(f"ld_ctx{b}") for b in range(BATCH)]
        ld_w1, ld_w2, ld_last = sem("ld_w1"), sem("ld_w2"), sem("ld_last")
        ld_w = [sem(f"ld_ring{s}") for s in range(RING)]
        stored = sem("stored")
        pool_step, pool_const = sem("pool_step"), sem("pool_const")
        dve_step = sem("dve_step")
        c1T_made, c1T_hi, c1T_lo = sem("c1T_made"), sem("c1T_hi"), sem("c1T_lo")
        c2_spread, c2_made, c2_hi, c2_lo = sem("c2_spread"), sem("c2_made"), sem("c2_hi"), sem("c2_lo")
        bias_made, bias_read = sem("bias_made"), sem("bias_read")
        x_quant, ctx_quant, xq_made, xqT_read = sem("x_quant"), sem("ctx_quant"), sem("xq_made"), sem("xqT_read")
        col_made, col_read, ab_made = sem("col_made"), sem("col_read"), sem("ab_made")
        ctxT_made, ctxT_hi, ctxT_lo = sem("ctxT_made"), sem("ctxT_hi"), sem("ctxT_lo")
        var_made, sqrt_made, xn_made = sem("var_made"), sem("sqrt_made"), sem("xn_made")
        xT_made, xT_hi, xT_lo = sem("xT_made"), sem("xT_hi"), sem("xT_lo")
        t_made, t_hi, t_lo = sem("t_made"), sem("t_hi"), sem("t_lo")
        raT_made, raT_read, bT_made, bT_read = sem("raT_made"), sem("raT_read"), sem("bT_made"), sem("bT_read")
        xT3_made, xT3_read, routed, gated = sem("xT3_made"), sem("xT3_read"), sem("routed"), sem("gated")
        whT_made, whT_read, out_made, x_final = sem("whT_made"), sem("whT_read"), sem("out_made"), sem("x_final")
        w1T_made, w1T_hi, w1T_lo = sem("w1T_made"), sem("w1T_hi"), sem("w1T_lo")
        w2_hi, w2_lo = sem("w2_hi"), sem("w2_lo")
        inter_made, oh_step = sem("inter_made"), sem("oh_step")
        h_made, h_masked, hT_made, hT_hi, hT_lo = (sem(n) for n in ("h_made", "h_masked", "hT_made", "hT_hi", "hT_lo"))
        y_made = sem("y_made")
        w_hi, w_lo = sem("w_hi"), sem("w_lo")
        proj_made, proj_hi, proj_read = sem("proj_made"), sem("proj_hi"), sem("proj_read")
        bias_set, bv_set = sem("bias_set"), sem("bv_set")
        s_made, max_made, exp_made, inv_made, prob_made = (
            sem(n) for n in ("s_made", "max_made", "exp_made", "inv_made", "prob_made"))
        nb_made = sem("nb_made")
        pT_made, pT_hi, pT_lo = sem("pT_made"), sem("pT_hi"), sem("pT_lo")
        o_made, o_hi, o_lo = sem("o_made"), sem("o_hi"), sem("o_lo")
        wo_made, wo_added = sem("wo_made"), sem("wo_added")

        x_rows = x_in.rearrange("b (t p) d -> p (b t) d", p=P)
        out_rows = out.rearrange("b (t p) d -> p (b t) d", p=P)
        ctx_rows = ctx_in.rearrange("b (t p) d -> b p t d", p=P)
        w1_rows = w1_in.rearrange("(c i p) d -> c p i d", i=CI, p=P)
        w2_rows = w2_in.rearrange("(c i p) d -> c p i d", i=CI, p=P)
        wq_cols = wq_in.rearrange("(k p) n -> k p n", p=P)
        wkv_cols = wkv_in.rearrange("(k p) n -> p k n", p=P)
        wo_rows = wo_in.rearrange("(g j p) d -> g j p d", j=G, p=P)

        def s_bank(u):
            return bank[(0, 1, 6, 7)[u % 4]][:, :]

        def o_bank(quad):
            return bank[4 + quad % 2][:, :]

        def set_bank(idx):
            return bank[(0, 1, 6, 7, 6, 2, 3, 7, 6, 7)[idx]][:, :]

        def q_index(head):
            return 4 if head == 0 else 6 + head

        def out_bank(t, last):
            return bank[(0, 1, 6, 7)[t] if last else 6 + t % 2][:, :]

        def mm3(dst, left, right, start, stop, sl=None, sr=None):
            nc.tensor.matmul(dst, left(0), right(0), start=start, stop=False)
            nc.tensor.matmul(dst, left(0), right(1), start=False, stop=False)
            return nc.tensor.matmul(dst, left(1), right(0), start=False, stop=stop)

        block = ctx.enter_context(nc.Block())

        @block.sync
        def _(sp):
            for i, src in enumerate((s1_in, s2_in, z1_in, z2_in)):
                sp.dma_start(scal[:, i:i + 1], src.rearrange("(a n) -> a n", a=1).to_broadcast([P, 1])).then_inc(ld_scal, 16)
            sp.dma_start(x[:, :, :], x_rows).then_inc(ld_x, 16)
            for b in range(BATCH):
                sp.dma_start(ctx_raw[:, b * MT:(b + 1) * MT, :], ctx_rows[b]).then_inc(ld_ctx[b], 16)
            sp.dma_start(c2_raw[:, :, :], c2_in.rearrange("(i p) r -> p i r", p=P)).then_inc(ld_c2, 16)
            sp.wait_ge(pool_const, 1)
            for r in range(4):
                sp.dma_start(c1_rep[32 * r:32 * r + RANK, :], c1_in).then_inc(ld_c1, 16)
            sp.dma_start(bias_rows[0:32, :], bq_in.rearrange("(h d) -> h d", d=HDIM)).then_inc(ld_bias, 16)
            sp.dma_start(bias_rows[32:48, :], bkv_in.rearrange("(h d) -> h d", d=HDIM)).then_inc(ld_bias, 16)
            sp.dma_start(bo_row[:, :], bo_in.rearrange("(a n) -> a n", a=1).to_broadcast([P, DIM])).then_inc(ld_bo, 16)
            sp.dma_start(w1_raw[:, :, :], w1_rows[0]).then_inc(ld_w1, 16)
            sp.dma_start(w2_raw[:, :, :], w2_rows[0]).then_inc(ld_w2, 16)

            def weight(n, src, slot, shaped=False):
                if not isinstance(n, int) or n >= RING:
                    sp.wait_ge(w_lo, n - RING + 1)
                dst = w_raw[:, slot, :]
                if shaped:
                    dst = dst.rearrange("p (k n) -> p k n", k=KD)
                sp.dma_start(dst, src).then_inc(ld_w[slot], 16)

            def projection_weights(n0, s0, g):
                weight(n0, wkv_cols[:, :, bass.ts(g, HDIM)], s0 % RING, True)
                weight(n0 + 1, wkv_cols[:, :, bass.ds(g * HDIM + NKV * HDIM, HDIM)], (s0 + 1) % RING, True)
                for kk in range(KD):
                    weight(n0 + 2 + kk, wq_cols[kk, :, bass.ts(g, G * HDIM)], (s0 + 2 + kk) % RING)

            projection_weights(0, 0, 0)
            with sp.Fori(1, NCHUNK) as c:
                sp.wait_ge(w1T_made, 2 * c)
                sp.dma_start(w1_raw[:, :, :], w1_rows[c]).then_inc(ld_w1, 16)
                sp.wait_ge(w2_lo, c)
                sp.dma_start(w2_raw[:, :, :], w2_rows[c]).then_inc(ld_w2, 16)

            def out_weights(n0, s0, g):
                for j in range(G):
                    weight(n0 + j, wo_rows[g, j], (s0 + j) % RING)

            with sp.Fori(0, NKV - 1) as g:
                projection_weights(6 + 10 * g, 6, g + 1)
                out_weights(12 + 10 * g, 12, g)
            out_weights(6 + 10 * (NKV - 1), 6, NKV - 1)
            sp.wait_ge(proj_made, 10 * NKV)
            sp.dma_start(a_raw[:, :], a_in.rearrange("e r d -> (e r) d")).then_inc(ld_last, 16)
            sp.dma_start(r_raw[:, :], route_in).then_inc(ld_last, 16)
            for j in range(KD):
                sp.dma_start(b_raw[:, j, :].rearrange("p (e r) -> p e r", e=EXP),
                             bw_in[:, j * P:(j + 1) * P, :].rearrange("e p r -> p e r")).then_inc(ld_last, 16)
            for t in range(TT):
                sp.wait_ge(x_final, t + 1)
                sp.dma_start(out_rows[:, t, :], x[:, t, :]).then_inc(stored, 16)
            sp.wait_ge(stored, 16 * TT)

        @block.gpsimd
        def _(pool):
            nc.gpsimd.memset(c1_rep[:, :], 0.0).then_inc(pool_const, 1)
            nc.gpsimd.memset(ident[:, :], 0.0).then_inc(pool_step, 1)
            nc.gpsimd.memset(c2_rep[:, :, :, :], 0.0).then_inc(pool_const, 1)
            pool.wait_ge(pool_step, 1)
            nc.gpsimd.affine_select(out=ident[:, :], in_=ident[:, :], compare_op=ALU.not_equal, fill=1.0, base=0,
                                    pattern=[[-1, P]], channel_multiplier=1).then_inc(pool_const, 1)
            nc.gpsimd.iota(desc[:, :, :], pattern=[[0, 16], [-1, BLK]], base=BLK, channel_multiplier=0,
                           allow_small_or_imprecise_dtypes=True).then_inc(pool_const, 1)
            nc.gpsimd.iota(desc8[:, :, :], pattern=[[0, TT], [-1, EXP]], base=EXP, channel_multiplier=0,
                           allow_small_or_imprecise_dtypes=True).then_inc(pool_const, 1)
            pool.wait_ge(pool_const, 3)
            nc.gpsimd.tensor_copy(ident_b[:, :], ident[:, :]).then_inc(pool_const, 1)

            def low_half(n, slot, dst_hi, dst_lo, shaped=False):
                pool.wait_ge(w_hi, n + 1)
                src = w_raw[:, slot, :]
                if shaped:
                    src = src.rearrange("p (k n) -> p k n", k=KD)
                nc.gpsimd.tensor_tensor(dst_lo, src, dst_hi, ALU.subtract).then_inc(w_lo, 1)

            def projection_low(n0, s0):
                low_half(n0, s0 % RING, wk[0][:, :, :], wk[1][:, :, :], True)
                low_half(n0 + 1, (s0 + 1) % RING, wv[0][:, :, :], wv[1][:, :, :], True)
                for kk in range(KD):
                    low_half(n0 + 2 + kk, (s0 + 2 + kk) % RING, wq[0][:, kk, :], wq[1][:, kk, :])

            projection_low(0, 0)
            with pool.Fori(0, NCHUNK) as c:
                pool.wait_ge(w2_hi, c + 1)
                nc.gpsimd.tensor_tensor(w2[1][:, :, :], w2_raw[:, :, :], w2[0][:, :, :], ALU.subtract).then_inc(w2_lo, 1)

            def normalise(g, u):
                pool.wait_ge(inv_made, UNITS * g + u + 1)
                nc.gpsimd.tensor_tensor(prob[:, u % 4, :], prob[:, u % 4, :], exp_inv[:, u:u + 1].to_broadcast([P, CTX]),
                                        ALU.mult).then_inc(prob_made, 1)

            def group(g, last):
                if not last:
                    projection_low(6 + 10 * g, 6)
                for u in range(UNITS):
                    normalise(g, u)
                at = 6 if last else 12
                for j in range(G):
                    low_half(at + 10 * g + j, (at + j) % RING, wo[0][:, j, :], wo[1][:, j, :])

            with pool.Fori(0, NKV - 1) as g:
                group(g, False)
            group(NKV - 1, True)

        @block.tensor
        def _(pe):
            pe.wait_ge(pool_const, 6)
            pe.wait_ge(ld_c1, 64)
            for kk in range(KD):
                ins = nc.tensor.transpose(bank[2][:, kk * P:(kk + 1) * P], c1_rep[:, kk * P:(kk + 1) * P], ident[:, :])
            ins.then_inc(c1T_made, 1)
            pe.wait_ge(c2_spread, 4)
            for b4 in range(4):
                for i in range(4 * b4, min(4 * b4 + 4, INTER // P)):
                    ins = nc.tensor.transpose(bank[3 + b4][:, (i % 4) * P:(i % 4 + 1) * P],
                                              c2_rep[:, i, :, :].rearrange("p a b -> p (a b)"), ident[:, :])
                ins.then_inc(c2_made, 1)
            pe.wait_ge(ld_bias, 32)
            nc.tensor.transpose(bank[7][:, 0:48], bias_rows[:, :], ident[0:48, 0:48]).then_inc(bias_made, 1)
            for t in range(TT):
                pe.wait_ge(x_quant, t + 1)
                if t >= 2:
                    pe.wait_ge(xqT_read, t - 1)
                for kk in range(KD):
                    ins = nc.tensor.transpose(bank[t % 2][:, :].bitcast(BF16)[:, kk * P:(kk + 1) * P],
                                              x_q[:, t, kk * P:(kk + 1) * P], ident_b[:, :])
                ins.then_inc(xq_made, 1)
            pe.wait_ge(xqT_read, TT)
            pe.wait_ge(c1T_lo, 1)
            pe.wait_ge(c2_lo, 1)
            for b in range(BATCH):
                pe.wait_ge(ctx_quant, b + 1)
                for kk in range(MT):
                    ins = nc.tensor.matmul(bank[2 + b][:, :], ones_b[:, :], ctx_q[:, b * MT + kk, :],
                                           start=(kk == 0), stop=(kk == MT - 1))
                ins.then_inc(col_made, 1)
                if b == 0:
                    pe.wait_ge(bias_read, 1)
                    pe.wait_ge(c2_lo, 4)
                for t in range(2 * b, 2 * b + 2):
                    for kk in range(MT):
                        ins = nc.tensor.matmul(bank[4 + t][:, :], xqT[:, kk, t * P:(t + 1) * P],
                                               ctx_q[:, b * MT + kk, :], start=(kk == 0), stop=(kk == MT - 1))
                    ins.then_inc(ab_made, 1)
            for b in range(BATCH):
                pe.wait_ge(ld_ctx[b], 16)
                for kk in range(KD):
                    n = b * KD + kk
                    if n >= 2:
                        pe.wait_ge(ctxT_lo, n - 1)
                    for m in range(MT):
                        ins = nc.tensor.transpose(bank[n % 2][:, m * P:(m + 1) * P],
                                                  ctx_raw[:, b * MT + m, kk * P:(kk + 1) * P], ident[:, :])
                    ins.then_inc(ctxT_made, 1)

            def x_transposed(n):
                for kk in range(KD):
                    if kk >= 2:
                        pe.wait_ge(xT_lo, KD * n + kk - 1)
                    for t in range(TT):
                        if kk == 0:
                            pe.wait_ge(xn_made, TT * (n + 1) + t + 1)
                        ins = nc.tensor.transpose(bank[2 * n + kk % 2][:, t * P:(t + 1) * P], xn[:, t, kk * P:(kk + 1) * P],
                                                  ident[:, :])
                    ins.then_inc(xT_made, 1)

            pe.wait_ge(ctxT_lo, 2 * KD)
            x_transposed(0)
            pe.wait_ge(xT_lo, KD)
            pe.wait_ge(col_read, 1)
            for kk in range(KD):
                ins = mm3(bank[2][:, :], lambda s: c1T[s][:, kk, :], lambda s: xT[s][:, kk, :], kk == 0, kk == KD - 1)
            ins.then_inc(t_made, 1)

            def transpose_w1(c):
                pe.wait_ge(ld_w1, 16 * (c + 1))
                for part in range(2):
                    if not isinstance(c, int) or c >= 1:
                        pe.wait_ge(h_masked, 4 * c - 1 + part)
                    for kk in range(2):
                        for i in range(CI):
                            ins = nc.tensor.transpose(bank[1 + part][:, kk * CHUNK + i * P:kk * CHUNK + (i + 1) * P],
                                                      w1_raw[:, i, (2 * part + kk) * P:(2 * part + kk + 1) * P], ident[:, :])
                    ins.then_inc(w1T_made, 1)

            def inter(c, half):
                if half == 1:
                    pe.wait_ge(oh_step, 10 * c + 5)
                elif not isinstance(c, int) or c >= 1:
                    pe.wait_ge(oh_step, 10 * c)
                for t in range(2 * half, 2 * half + 2):
                    ins = nc.tensor.matmul(bank[0][:, (t % 2) * CHUNK:(t % 2 + 1) * CHUNK], t_stack[:, t * P:(t + 1) * P],
                                           c2_stack[:, bass.ts(c, CHUNK)], start=True, stop=True)
                ins.then_inc(inter_made, 1)

            def transpose_h(c, t):
                pe.wait_ge(h_masked, 4 * c + t + 1)
                if t >= 1:
                    pe.wait_ge(hT_lo, 4 * c + t)
                for i in range(CI):
                    ins = nc.tensor.transpose(bank[3][:, i * P:(i + 1) * P], h[:, t % 2, i * P:(i + 1) * P], ident[:, :])
                ins.then_inc(hT_made, 1)

            def down(c, t, first, last):
                pe.wait_ge(hT_lo, 4 * c + t + 1)
                for i in range(CI):
                    ins = mm3(bank[4 + t][:, :], lambda s: hT[s][:, i, t * P:(t + 1) * P], lambda s: w2[s][:, i, :],
                              first and i == 0, last and i == CI - 1)
                ins.then_inc(y_made, 1)

            def chunk(c, first, last):
                pe.wait_ge(w1T_lo, 2 * (c + 1))
                for t in range(TT):
                    if t >= 2:
                        pe.wait_ge(h_masked, 4 * c + t - 1)
                    for kk in range(KD):
                        ins = mm3(bank[1 + t % 2][:, 0:CHUNK], lambda s: xT[s][:, kk, t * P:(t + 1) * P],
                                  lambda s: w1T[s][:, kk, :], kk == 0, kk == KD - 1)
                    ins.then_inc(h_made, 1)
                    if t >= 1:
                        transpose_h(c, t - 1)
                if not last:
                    transpose_w1(c + 1)
                    inter(c + 1, 0)
                pe.wait_ge(w2_lo, c + 1)
                down(c, 0, first, last)
                transpose_h(c, 3)
                down(c, 1, first, last)
                if not last:
                    inter(c + 1, 1)
                down(c, 2, first, last)
                down(c, 3, first, last)

            pe.wait_ge(t_lo, 1)
            pe.wait_ge(col_read, 2)
            transpose_w1(0)
            inter(0, 0)
            inter(0, 1)
            chunk(0, True, False)
            with pe.Fori(1, NCHUNK - 1) as c:
                chunk(c, False, False)
            chunk(NCHUNK - 1, False, True)

            def project(idx, base, g, left, right):
                if idx < 4 and g is None:
                    if idx >= 2:
                        pe.wait_ge(wo_added, 1 + idx)
                elif idx < 4:
                    pe.wait_ge(exp_made, UNITS * g + 13 + idx)
                else:
                    pe.wait_ge(proj_read, base + {4: 3, 7: 4, 8: 5, 9: 8}[idx])
                for kk in range(KD):
                    ins = mm3(set_bank(idx), lambda s: left(s, kk), lambda s: right(s, kk), kk == 0, kk == KD - 1)
                ins.then_inc(proj_made, 1)

            def project_k(b, base, g):
                project(b, base, g, lambda s, kk: wk[s][:, kk, :], lambda s, kk: ctxT[s][:, kk, b * CTX:(b + 1) * CTX])

            def project_vT(b, base, g):
                project(2 + b, base, g, lambda s, kk: wv[s][:, kk, :], lambda s, kk: ctxT[s][:, kk, b * CTX:(b + 1) * CTX])

            def project_q(head, base, g):
                project(q_index(head), base, g, lambda s, kk: wq[s][:, kk, head * HDIM:(head + 1) * HDIM],
                        lambda s, kk: xT[s][:, kk, :])

            def transpose_v(b, base, g):
                pe.wait_ge(proj_read, base + 3 + b)
                if g is not None:
                    pe.wait_ge(pT_lo, UNITS * g + 15 + b)
                for m in range(MT):
                    ins = nc.tensor.transpose(set_bank(5 + b)[:, m * P:(m + 1) * P],
                                              vT[:, b * CTX + m * P:b * CTX + (m + 1) * P], ident[:, :])
                ins.then_inc(proj_made, 1)

            def weights_ready(n):
                pe.wait_ge(w_lo, n)

            weights_ready(2)
            project_k(0, 0, None)
            project_k(1, 0, None)
            project_vT(0, 0, None)
            project_vT(1, 0, None)
            x_transposed(1)
            weights_ready(6)
            pe.wait_ge(xT_lo, 2 * KD)
            project_q(0, 0, None)
            transpose_v(0, 0, None)
            transpose_v(1, 0, None)
            for head in range(1, G):
                project_q(head, 0, None)

            def scores(g, u):
                quad, j = u // 4, u % 4
                b, head, lt = quad // 2, 2 * (quad % 2) + j // 2, j % 2
                if lt == 0 and b == 0:
                    pe.wait_ge(proj_read, 10 * g + (5 if head == 0 else 7 + head))
                if u >= 4:
                    pe.wait_ge(exp_made, UNITS * g + u - 3)
                elif u >= 2:
                    pe.wait_ge(wo_added, 4 * g + 1 + u)
                    pe.wait_ge(proj_read, 10 * g + 7 + u)
                at = b * SEQ + lt * P
                mm3(s_bank(u), lambda s: q[s][:, head, at:at + P], lambda s: k[s][:, b * CTX:(b + 1) * CTX],
                    True, True).then_inc(s_made, 1)

            def transpose_p(g, u):
                pe.wait_ge(prob_made, UNITS * g + u + 1)
                if u >= 2:
                    pe.wait_ge(pT_lo, UNITS * g + u - 1)
                for m in range(MT):
                    ins = nc.tensor.transpose(bank[2 + u % 2][:, m * P:(m + 1) * P], prob[:, u % 4, m * P:(m + 1) * P],
                                              ident[:, :])
                ins.then_inc(pT_made, 1)

            def values(g, quad, m):
                b = quad // 2
                if m == 0:
                    pe.wait_ge(pT_lo, UNITS * g + 4 * quad + 4)
                    if quad >= 2:
                        pe.wait_ge(o_lo, 4 * g + quad - 1)
                ins = mm3(o_bank(quad), lambda s: v[s][:, b * MT + m, :], lambda s: probT[quad % 2][s][:, m, :],
                          m == 0, m == MT - 1)
                if m == MT - 1:
                    ins.then_inc(o_made, 1)

            def output(g, t, last):
                pe.wait_ge(o_lo, 4 * g + (2 if t < 2 else 4))
                if last:
                    pe.wait_ge(exp_made, UNITS * g + 13 + t)
                elif t < 2:
                    pe.wait_ge(proj_read, 10 * g + 19 + t)
                else:
                    pe.wait_ge(wo_added, 4 * g + 4 + t - 1)
                for j in range(G):
                    ins = mm3(out_bank(t, last), lambda s: o[s][:, j, t * P:(t + 1) * P], lambda s: wo[s][:, j, :],
                              j == 0, j == G - 1)
                ins.then_inc(wo_made, 1)

            def group(g, last):
                base = 10 * g + 10
                for u in range(2, UNITS):
                    scores(g, u)
                    if u >= 3:
                        transpose_p(g, u - 3)
                    if u >= 7:
                        values(g, (u - 7) // 4, (u - 7) % 4)
                transpose_p(g, 13)
                values(g, 2, 1)
                if not last:
                    weights_ready(12 + 10 * g)
                    project_k(0, base, g)
                else:
                    weights_ready(10 + 10 * g)
                    output(g, 0, True)
                transpose_p(g, 14)
                values(g, 2, 2)
                values(g, 2, 3)
                transpose_p(g, 15)
                if not last:
                    project_k(1, base, g)
                else:
                    output(g, 1, True)
                for m in range(MT):
                    values(g, 3, m)
                if not last:
                    project_vT(0, base, g)
                    project_vT(1, base, g)
                    project_q(0, base, g)
                    transpose_v(0, base, g)
                    transpose_v(1, base, g)
                    for head in range(1, G):
                        project_q(head, base, g)
                    weights_ready(16 + 10 * g)
                    for t in range(3):
                        output(g, t, False)
                    scores(g + 1, 0)
                    scores(g + 1, 1)
                    output(g, 3, False)
                else:
                    output(g, 2, True)
                    output(g, 3, True)

            scores(0, 0)
            scores(0, 1)
            with pe.Fori(0, NKV - 1) as g:
                group(g, False)
            group(NKV - 1, True)

            pe.wait_ge(ld_last, 16 * (2 + KD))
            for kk in range(KD):
                if kk >= 2:
                    pe.wait_ge(raT_read, kk - 1)
                nc.tensor.transpose(bank[2 + kk % 2][:, 0:ER], a_raw[:, kk * P:(kk + 1) * P], ident[:, :])
                nc.tensor.transpose(bank[2 + kk % 2][:, ER:ER + EXP], r_raw[:, kk * P:(kk + 1) * P],
                                    ident[0:EXP, 0:EXP]).then_inc(raT_made, 1)
            for j in range(KD):
                ins = nc.tensor.transpose(bank[4][:, j * P:(j + 1) * P], b_raw[:, j, :], ident[:, :])
            ins.then_inc(bT_made, 1)
            for kk in range(KD):
                if kk >= 2:
                    pe.wait_ge(xT3_read, kk - 1)
                for t in range(TT):
                    if kk == 0:
                        pe.wait_ge(xn_made, 3 * TT + t + 1)
                    ins = nc.tensor.transpose(bank[kk % 2][:, t * P:(t + 1) * P], xn[:, t, kk * P:(kk + 1) * P], ident[:, :])
                ins.then_inc(xT3_made, 1)
            pe.wait_ge(xT3_read, KD)
            pe.wait_ge(raT_read, KD)
            pe.wait_ge(bT_read, 1)
            for t in range(TT):
                for kk in range(KD):
                    ins = nc.tensor.matmul(bank[4 + t][:, 0:ER + EXP], xT3[:, kk, t * P:(t + 1) * P], raT[:, kk, :],
                                           start=(kk == 0), stop=(kk == KD - 1))
                ins.then_inc(routed, 1)
            for t in range(TT):
                pe.wait_ge(gated, t + 1)
                if t >= 2:
                    pe.wait_ge(whT_read, t - 1)
                nc.tensor.transpose(bank[2 + t % 2][:, 0:P], (wh, wh2)[t % 2][:, :], ident[:, :]).then_inc(whT_made, 1)
            for t in range(TT):
                pe.wait_ge(whT_read, t + 1)
                nc.tensor.matmul(bank[4 + t][:, :], whT[:, t * P:(t + 1) * P], bT[:, :], start=True, stop=True)\
                    .then_inc(out_made, 1)

        @block.scalar
        def _(act):
            def root(n):
                act.wait_ge(var_made, n + 1)
                nc.scalar.activation(ln_b[:, :], ln_a[:, :], ACT.Sqrt).then_inc(sqrt_made, 1)

            def weight_high(turn, slot, dst, shaped=False):
                act.wait_ge(ld_w[slot], 16 * turn)
                src = w_raw[:, slot, :]
                if shaped:
                    src = src.rearrange("p (k n) -> p k n", k=KD)
                nc.scalar.copy(dst, src).then_inc(w_hi, 1)

            def projection_high(turns, s0):
                for i in range(6):
                    dst = wk[0][:, :, :] if i == 0 else wv[0][:, :, :] if i == 1 else wq[0][:, i - 2, :]
                    weight_high(turns + (s0 + i) // RING + 1, (s0 + i) % RING, dst, i < 2)

            root(0)
            act.wait_ge(c1T_made, 1)
            nc.scalar.copy(c1T[0][:, :, :].rearrange("p k n -> p (k n)"), bank[2][:, :]).then_inc(c1T_hi, 1)
            for b4 in range(4):
                at, n = 512 * b4, min(512, INTER - 512 * b4)
                act.wait_ge(c2_made, b4 + 1)
                nc.scalar.copy(c2_stack[:, at:at + n], bank[3 + b4][:, 0:n]).then_inc(c2_hi, 1)
            act.wait_ge(bias_made, 1)
            nc.scalar.copy(bias_all[:, :], bank[7][:, 0:48]).then_inc(bias_read, 1)

            for t in range(TT):
                act.wait_ge(xq_made, t + 1)
                nc.scalar.copy(xqT[:, :, t * P:(t + 1) * P],
                               bank[t % 2][:, 0:256].bitcast(BF16).rearrange("p (k n) -> p k n", k=KD)).then_inc(xqT_read, 1)
            projection_high(0, 0)
            root(1)
            for n in range(2 * KD):
                act.wait_ge(ctxT_made, n + 1)
                b, kk = n // KD, n % KD
                nc.scalar.copy(ctxT[0][:, kk, b * CTX:(b + 1) * CTX], bank[n % 2][:, :]).then_inc(ctxT_hi, 1)

            def x_high(n):
                for kk in range(KD):
                    act.wait_ge(xT_made, KD * n + kk + 1)
                    nc.scalar.copy(xT[0][:, kk, :], bank[2 * n + kk % 2][:, :]).then_inc(xT_hi, 1)

            x_high(0)
            act.wait_ge(t_made, 1)
            nc.scalar.copy(t_stack[:, :], bank[2][:, :]).then_inc(t_hi, 1)

            def w1_high(c):
                for part in range(2):
                    act.wait_ge(w1T_made, 2 * c + part + 1)
                    nc.scalar.copy(w1T[0][:, 2 * part:2 * part + 2, :],
                                   bank[1 + part][:, :].rearrange("p (k n) -> p k n", k=2)).then_inc(w1T_hi, 1)

            def h_high(c, t):
                act.wait_ge(hT_made, 4 * c + t + 1)
                nc.scalar.copy(hT[0][:, :, t * P:(t + 1) * P],
                               bank[3][:, 0:CHUNK].rearrange("p (i n) -> p i n", i=CI)).then_inc(hT_hi, 1)

            def chunk(c, last):
                for t in range(TT - 1):
                    h_high(c, t)
                if not last:
                    w1_high(c + 1)
                h_high(c, TT - 1)

            w1_high(0)
            with act.Fori(0, NCHUNK - 1) as c:
                chunk(c, False)
            chunk(NCHUNK - 1, True)

            def k_high(s, b):
                if b == 0:
                    act.wait_ge(bias_set, 2 * s + 2)
                act.wait_ge(proj_made, 10 * s + b + 1)
                nc.scalar.activation(k[0][:, b * CTX:(b + 1) * CTX], set_bank(b), ACT.Identity,
                                     bias=bias_k[:, 0:1]).then_inc(proj_hi, 1)

            def q_high(s, head):
                idx = q_index(head)
                act.wait_ge(proj_made, 10 * s + idx + 1)
                nc.scalar.activation(q[0][:, head, :], set_bank(idx), ACT.Identity,
                                     bias=bias_q[:, head:head + 1]).then_inc(proj_hi, 1)

            def v_high(s, b):
                act.wait_ge(proj_made, 10 * s + 6 + b)
                nc.scalar.copy(v[0][:, b * MT:(b + 1) * MT, :],
                               set_bank(5 + b).rearrange("p (m d) -> p m d", m=MT)).then_inc(proj_hi, 1)

            k_high(0, 0)
            k_high(0, 1)
            root(2)
            x_high(1)
            q_high(0, 0)
            v_high(0, 0)
            v_high(0, 1)
            for head in range(1, G):
                q_high(0, head)

            def exponentials(g, u):
                act.wait_ge(max_made, UNITS * g + u + 1)
                nc.scalar.activation(prob[:, u % 4, :], s_bank(u), ACT.Exp, bias=neg_bias[:, u:u + 1],
                                     scale=SCALE, accum_out=exp_sum[:, u:u + 1]).then_inc(exp_made, 1)

            def p_high(g, u):
                quad, j = u // 4, u % 4
                if quad >= 2 and j == 0:
                    act.wait_ge(o_made, 4 * g + quad - 1)
                act.wait_ge(pT_made, UNITS * g + u + 1)
                nc.scalar.copy(probT[quad % 2][0][:, :, j * P:(j + 1) * P],
                               bank[2 + u % 2][:, :].rearrange("p (m n) -> p m n", m=MT)).then_inc(pT_hi, 1)

            def o_high(g, quad):
                b, hp = quad // 2, quad % 2
                if quad == 0:
                    act.wait_ge(bv_set, g + 1)
                act.wait_ge(o_made, 4 * g + quad + 1)
                nc.scalar.activation(o[0][:, 2 * hp:2 * hp + 2, b * SEQ:(b + 1) * SEQ],
                                     o_bank(quad).rearrange("p (h n) -> p h n", h=2), ACT.Identity,
                                     bias=bias_v[:, 0:1]).then_inc(o_hi, 1)

            def group(g, last):
                if not last:
                    act.wait_ge(proj_made, 10 * g + 10)
                    projection_high(2 * g, 6)
                at = 6 if last else 12
                for u in range(UNITS):
                    if u == 12:
                        o_high(g, 0)
                    if u >= 3:
                        p_high(g, u - 3)
                    exponentials(g, u)
                    if 4 <= u < 8:
                        j = u - 4
                        weight_high(2 * g + (at + j) // RING + 1, (at + j) % RING, wo[0][:, j, :])
                o_high(g, 1)
                p_high(g, 13)
                if not last:
                    k_high(g + 1, 0)
                p_high(g, 14)
                o_high(g, 2)
                p_high(g, 15)
                if not last:
                    k_high(g + 1, 1)
                o_high(g, 3)
                if not last:
                    q_high(g + 1, 0)
                    v_high(g + 1, 0)
                    v_high(g + 1, 1)
                    for head in range(1, G):
                        q_high(g + 1, head)

            with act.Fori(0, NKV - 1) as g:
                group(g, False)
            group(NKV - 1, True)

            for kk in range(KD):
                act.wait_ge(raT_made, kk + 1)
                nc.scalar.copy(raT[:, kk, :], bank[2 + kk % 2][:, 0:ER + EXP]).then_inc(raT_read, 1)
            act.wait_ge(bT_made, 1)
            nc.scalar.copy(bT[:, :], bank[4][:, :]).then_inc(bT_read, 1)
            root(3)
            act.wait_ge(w_lo, 10 * NKV)
            for kk in range(KD):
                act.wait_ge(xT3_made, kk + 1)
                nc.scalar.copy(xT3[:, kk, :], bank[kk % 2][:, :]).then_inc(xT3_read, 1)
            for t in range(TT):
                act.wait_ge(whT_made, t + 1)
                nc.scalar.copy(whT[:, t * P:(t + 1) * P], bank[2 + t % 2][:, 0:P]).then_inc(whT_read, 1)

        @block.vector
        def _(dve):
            steps = [0]

            def link(ins):
                steps[0] += 1
                ins.then_inc(dve_step, 1)
                dve.wait_ge(dve_step, steps[0])

            def note(ins):
                steps[0] += 1
                ins.then_inc(dve_step, 1)

            def noted():
                dve.wait_ge(dve_step, steps[0])

            nc.vector.memset(neg_lo_t[:, :], 0.0)
            nc.vector.memset(neg_lo_c[:, :], 0.0)
            note(nc.vector.memset(ones_b[:, :], 1.0))
            noted()
            note(nc.vector.memset(neg_lo_t[64:128, :], -1.0))
            note(nc.vector.memset(neg_lo_c[32:64, :], -1.0))
            note(nc.vector.memset(neg_lo_c[96:128, :], -1.0))
            dve.wait_ge(ld_scal, 64)
            note(nc.vector.reciprocal(derived[:, 0:2], scal[:, 0:2]))
            note(nc.vector.tensor_tensor(derived[:, 2:3], scal[:, 0:1], scal[:, 1:2], ALU.mult))
            note(nc.vector.tensor_scalar(derived[:, 3:5], scal[:, 2:4], CENTRE, None, ALU.subtract))
            noted()
            link(nc.vector.tensor_scalar(derived[:, 5:7], derived[:, 3:5], derived[:, 2:3], -1.0, ALU.mult, ALU.mult))
            link(nc.vector.tensor_scalar(derived[:, 7:8], derived[:, 5:6], derived[:, 4:5], -float(CTX), ALU.mult, ALU.mult))

            def layer_norm(n):
                for t in range(TT):
                    note(nc.vector.bn_stats(stats[:, t, :], x[:, t, :]))
                noted()
                for t in range(TT):
                    note(nc.vector.bn_aggr(moments[:, t, :], stats[:, t, :]))
                noted()
                nc.vector.tensor_scalar(ln_a[:, :], moments[:, :, 1], EPS, None, ALU.add).then_inc(var_made, 1)
                dve.wait_ge(sqrt_made, n + 1)
                link(nc.vector.reciprocal(ln_c[:, :], ln_b[:, :]))
                link(nc.vector.tensor_tensor(ln_b[:, :], ln_c[:, :], ln_c[:, :], ALU.mult))
                link(nc.vector.tensor_tensor(ln_b[:, :], ln_b[:, :], ln_a[:, :], ALU.mult))
                link(nc.vector.tensor_scalar(ln_b[:, :], ln_b[:, :], -0.5, 1.5, ALU.mult, ALU.add))
                link(nc.vector.tensor_tensor(rstd[:, :], ln_b[:, :], ln_c[:, :], ALU.mult))
                for t in range(TT):
                    nc.vector.tensor_scalar(xn[:, t, :], x[:, t, :], moments[:, t, 0:1], rstd[:, t:t + 1],
                                            ALU.subtract, ALU.mult).then_inc(xn_made, 1)

            def quantise(work, to, scale, zero):
                link(nc.vector.tensor_scalar(work, work, scale, zero, ALU.mult, ALU.add))
                link(nc.vector.tensor_scalar(work, work, 0.0, QMAX, ALU.max, ALU.min))
                return nc.vector.tensor_scalar(to, work, ROUND, ROUND + CENTRE, ALU.add, ALU.subtract)

            dve.wait_ge(pool_const, 2)
            dve.wait_ge(ld_c2, 16)
            for r in range(4):
                nc.vector.tensor_copy(c2_rep[:, :, r, 0:RANK], c2_raw[:, :, :]).then_inc(c2_spread, 1)
            dve.wait_ge(ld_x, 16)
            layer_norm(0)
            dve.wait_ge(xn_made, TT)
            for t in range(TT):
                quantise(xn[:, t, :], x_q[:, t, :], derived[:, 0:1], scal[:, 2:3]).then_inc(x_quant, 1)
            for b in range(BATCH):
                dve.wait_ge(ld_ctx[b], 16)
                part = slice(b * MT, (b + 1) * MT)
                if b == 0:
                    dve.wait_ge(x_quant, TT)
                else:
                    dve.wait_ge(ctx_quant, b)
                link(nc.vector.tensor_scalar(xn[:, :, :], ctx_raw[:, part, :], derived[:, 1:2], scal[:, 3:4], ALU.mult, ALU.add))
                link(nc.vector.tensor_scalar(xn[:, :, :], xn[:, :, :], 0.0, QMAX, ALU.max, ALU.min))
                nc.vector.tensor_scalar(ctx_q[:, part, :], xn[:, :, :], ROUND, ROUND + CENTRE, ALU.add,
                                        ALU.subtract).then_inc(ctx_quant, 1)
            dve.wait_ge(c1T_hi, 1)
            nc.vector.tensor_tensor(c1T[1][:, :, :].rearrange("p k n -> p (k n)"), bank[2][:, :],
                                    c1T[0][:, :, :].rearrange("p k n -> p (k n)"), ALU.subtract).then_inc(c1T_lo, 1)
            for b4 in range(4):
                at, n = 512 * b4, min(512, INTER - 512 * b4)
                dve.wait_ge(c2_hi, b4 + 1)
                nc.vector.scalar_tensor_tensor(c2_stack[:, at:at + n], c2_stack[:, at:at + n], neg_lo_c[:, 0:1],
                                               bank[3 + b4][:, 0:n], ALU.mult, ALU.add).then_inc(c2_lo, 1)
            link(nc.vector.tensor_reduce(row_sum[:, :], x_q[:, :, :], AX_X, ALU.add))
            link(nc.vector.tensor_scalar(row_add[:, :], row_sum[:, :], derived[:, 6:7], derived[:, 7:8], ALU.mult, ALU.add))
            for b in range(BATCH):
                dve.wait_ge(col_made, b + 1)
                nc.vector.tensor_scalar(col_add[:, b, :], bank[2 + b][:, :], derived[:, 5:6], None, ALU.mult)\
                    .then_inc(col_read, 1)
                dve.wait_ge(col_read, b + 1)
                for t in range(2 * b, 2 * b + 2):
                    note(nc.vector.scalar_tensor_tensor(x[:, t, :], x[:, t, :], row_add[:, t:t + 1], col_add[:, b, :],
                                                        ALU.add, ALU.add))
                noted()
                for t in range(2 * b, 2 * b + 2):
                    dve.wait_ge(ab_made, t + 1)
                    note(nc.vector.scalar_tensor_tensor(x[:, t, :], bank[4 + t][:, :], derived[:, 2:3], x[:, t, :],
                                                        ALU.mult, ALU.add))
            noted()
            layer_norm(1)
            for n in range(2 * KD):
                b, kk = n // KD, n % KD
                dve.wait_ge(ctxT_hi, n + 1)
                nc.vector.tensor_tensor(ctxT[1][:, kk, b * CTX:(b + 1) * CTX], bank[n % 2][:, :],
                                        ctxT[0][:, kk, b * CTX:(b + 1) * CTX], ALU.subtract).then_inc(ctxT_lo, 1)

            def x_low(n):
                for kk in range(KD):
                    dve.wait_ge(xT_hi, KD * n + kk + 1)
                    nc.vector.tensor_tensor(xT[1][:, kk, :], bank[2 * n + kk % 2][:, :], xT[0][:, kk, :], ALU.subtract)\
                        .then_inc(xT_lo, 1)

            x_low(0)

            dve.wait_ge(t_hi, 1)
            nc.vector.scalar_tensor_tensor(t_stack[:, :], t_stack[:, :], neg_lo_t[:, 0:1], bank[2][:, :],
                                           ALU.mult, ALU.add).then_inc(t_lo, 1)

            def w1_low(c):
                for part in range(2):
                    dve.wait_ge(w1T_hi, 2 * c + part + 1)
                    nc.vector.tensor_tensor(w1T[1][:, 2 * part:2 * part + 2, :],
                                            bank[1 + part][:, :].rearrange("p (k n) -> p k n", k=2),
                                            w1T[0][:, 2 * part:2 * part + 2, :], ALU.subtract).then_inc(w1T_lo, 1)

            def first_maxima(c, half):
                s0 = 10 * c + 5 * half
                scores = bank[0][:, :].rearrange("p (n j) -> p n j", j=BLK)
                dve.wait_ge(inter_made, 2 * c + half + 1)
                nc.vector.tensor_reduce(oh_max[:, :], scores, AX_X, ALU.max).then_inc(oh_step, 1)
                dve.wait_ge(oh_step, s0 + 1)
                nc.vector.tensor_tensor(oh_eq[:, :, :], scores, oh_max[:, :].unsqueeze(2).to_broadcast([P, 16, BLK]),
                                        ALU.is_equal).then_inc(oh_step, 1)
                dve.wait_ge(oh_step, s0 + 2)
                nc.vector.tensor_tensor(oh_key[:, :, :], oh_eq[:, :, :], desc[:, :, :], ALU.mult).then_inc(oh_step, 1)
                dve.wait_ge(oh_step, s0 + 3)
                nc.vector.tensor_reduce(oh_first[:, :], oh_key[:, :, :], AX_X, ALU.max).then_inc(oh_step, 1)
                dve.wait_ge(oh_step, s0 + 4)
                nc.vector.tensor_tensor(one_hot[:, 2 * half:2 * half + 2, :].rearrange("p t (n j) -> p (t n) j", j=BLK),
                                        oh_key[:, :, :], oh_first[:, :].unsqueeze(2).to_broadcast([P, 16, BLK]),
                                        ALU.is_equal).then_inc(oh_step, 1)

            def mask(c, t):
                dve.wait_ge(h_made, 4 * c + t + 1)
                if t >= 2:
                    dve.wait_ge(hT_made, 4 * c + t - 1)
                nc.vector.scalar_tensor_tensor(h[:, t % 2, :], bank[1 + t % 2][:, 0:CHUNK], 0.0, one_hot[:, t, :],
                                               ALU.max, ALU.mult).then_inc(h_masked, 1)

            def h_low(c, t):
                dve.wait_ge(hT_hi, 4 * c + t + 1)
                nc.vector.tensor_tensor(hT[1][:, :, t * P:(t + 1) * P],
                                        bank[3][:, 0:CHUNK].rearrange("p (i n) -> p i n", i=CI),
                                        hT[0][:, :, t * P:(t + 1) * P], ALU.subtract).then_inc(hT_lo, 1)

            def chunk(c, first, last):
                dve.wait_ge(oh_step, 10 * c + 10)
                mask(c, 0)
                if not first:
                    dve.wait_ge(y_made, 4 * c)
                dve.wait_ge(ld_w2, 16 * (c + 1))
                nc.vector.tensor_copy(w2[0][:, :, :], w2_raw[:, :, :]).then_inc(w2_hi, 1)
                mask(c, 1)
                h_low(c, 0)
                mask(c, 2)
                h_low(c, 1)
                mask(c, 3)
                h_low(c, 2)
                if not last:
                    w1_low(c + 1)
                    first_maxima(c + 1, 0)
                h_low(c, 3)
                if not last:
                    first_maxima(c + 1, 1)

            w1_low(0)
            first_maxima(0, 0)
            first_maxima(0, 1)
            chunk(0, True, False)
            with dve.Fori(1, NCHUNK - 1) as c:
                chunk(c, False, False)
            chunk(NCHUNK - 1, False, True)
            for t in range(TT):
                dve.wait_ge(y_made, 4 * (NCHUNK - 1) + t + 1)
                nc.vector.tensor_tensor(x[:, t, :], bank[4 + t][:, :], x[:, t, :], ALU.add).then_inc(wo_added, 1)

            def set_biases(s):
                nc.vector.tensor_copy(bias_q[:, :], bias_all[:, bass.ds(G * s, G)]).then_inc(bias_set, 1)
                nc.vector.tensor_copy(bias_k[:, :], bias_all[:, bass.ds(NHEAD + s, 1)]).then_inc(bias_set, 1)

            def k_low(s, b):
                if b == 0:
                    dve.wait_ge(bias_set, 2 * s + 2)
                dve.wait_ge(proj_hi, 8 * s + b + 1)
                nc.vector.scalar_tensor_tensor(k[1][:, b * CTX:(b + 1) * CTX], set_bank(b), bias_k[:, 0:1],
                                               k[0][:, b * CTX:(b + 1) * CTX], ALU.add, ALU.subtract).then_inc(proj_read, 1)

            def vT_copy(s, b):
                dve.wait_ge(proj_made, 10 * s + 3 + b)
                nc.vector.tensor_copy(vT[:, b * CTX:(b + 1) * CTX], set_bank(2 + b)).then_inc(proj_read, 1)

            def q_low(s, head):
                dve.wait_ge(proj_hi, 8 * s + (3 if head == 0 else 5 + head))
                nc.vector.scalar_tensor_tensor(q[1][:, head, :], set_bank(q_index(head)), bias_q[:, head:head + 1],
                                               q[0][:, head, :], ALU.add, ALU.subtract).then_inc(proj_read, 1)

            def v_low(s, b):
                dve.wait_ge(proj_hi, 8 * s + 4 + b)
                nc.vector.tensor_tensor(v[1][:, b * MT:(b + 1) * MT, :],
                                        set_bank(5 + b).rearrange("p (m d) -> p m d", m=MT),
                                        v[0][:, b * MT:(b + 1) * MT, :], ALU.subtract).then_inc(proj_read, 1)

            dve.wait_ge(bias_read, 1)
            set_biases(0)
            k_low(0, 0)
            k_low(0, 1)
            dve.wait_ge(wo_added, TT)
            layer_norm(2)
            dve.wait_ge(ld_bo, 16)
            for t in range(TT):
                note(nc.vector.tensor_tensor(x[:, t, :], x[:, t, :], bo_row[:, :], ALU.add))
            noted()
            vT_copy(0, 0)
            vT_copy(0, 1)
            x_low(1)
            q_low(0, 0)
            v_low(0, 0)
            v_low(0, 1)
            for head in range(1, G):
                q_low(0, head)

            def row_max(g, u):
                dve.wait_ge(s_made, UNITS * g + u + 1)
                nc.vector.tensor_reduce(neg_max[:, u:u + 1], s_bank(u), AX_X, ALU.max, negate=True).then_inc(nb_made, 1)
                dve.wait_ge(nb_made, UNITS * g + u + 1)
                nc.vector.tensor_scalar(neg_bias[:, u:u + 1], neg_max[:, u:u + 1], SCALE, None, ALU.mult).then_inc(max_made, 1)

            def inverse(g, u):
                dve.wait_ge(exp_made, UNITS * g + u + 1)
                nc.vector.reciprocal(exp_inv[:, u:u + 1], exp_sum[:, u:u + 1]).then_inc(inv_made, 1)

            def p_low(g, u):
                quad, j = u // 4, u % 4
                dve.wait_ge(pT_hi, UNITS * g + u + 1)
                nc.vector.tensor_tensor(probT[quad % 2][1][:, :, j * P:(j + 1) * P],
                                        bank[2 + u % 2][:, :].rearrange("p (m n) -> p m n", m=MT),
                                        probT[quad % 2][0][:, :, j * P:(j + 1) * P], ALU.subtract).then_inc(pT_lo, 1)

            def o_low(g, quad):
                b, hp = quad // 2, quad % 2
                if quad == 0:
                    dve.wait_ge(bv_set, g + 1)
                dve.wait_ge(o_hi, 4 * g + quad + 1)
                at = (slice(None), slice(2 * hp, 2 * hp + 2), slice(b * SEQ, (b + 1) * SEQ))
                nc.vector.scalar_tensor_tensor(o[1][at], o_bank(quad).rearrange("p (h n) -> p h n", h=2), bias_v[:, 0:1],
                                               o[0][at], ALU.add, ALU.subtract).then_inc(o_lo, 1)

            def add_output(g, t, last):
                dve.wait_ge(wo_added, 4 * g + t + 1)
                dve.wait_ge(wo_made, 4 * g + t + 1)
                nc.vector.tensor_tensor(x[:, t, :], out_bank(t, last), x[:, t, :], ALU.add).then_inc(wo_added, 1)

            def group(g, last):
                nc.vector.tensor_copy(bias_v[:, :], bias_all[:, bass.ds(NHEAD + NKV + g, 1)]).then_inc(bv_set, 1)
                inverse(g, 0)
                for u in range(2, UNITS):
                    row_max(g, u)
                    inverse(g, u - 1)
                    if u >= 3:
                        p_low(g, u - 3)
                    if u == 12:
                        o_low(g, 0)
                inverse(g, 15)
                o_low(g, 1)
                p_low(g, 13)
                if not last:
                    set_biases(g + 1)
                    k_low(g + 1, 0)
                else:
                    add_output(g, 0, True)
                p_low(g, 14)
                o_low(g, 2)
                p_low(g, 15)
                if not last:
                    k_low(g + 1, 1)
                else:
                    add_output(g, 1, True)
                o_low(g, 3)
                if not last:
                    vT_copy(g + 1, 0)
                    vT_copy(g + 1, 1)
                    q_low(g + 1, 0)
                    v_low(g + 1, 0)
                    v_low(g + 1, 1)
                    for head in range(1, G):
                        q_low(g + 1, head)
                    for t in range(3):
                        add_output(g, t, False)
                    row_max(g + 1, 0)
                    row_max(g + 1, 1)
                    add_output(g, 3, False)
                else:
                    add_output(g, 2, True)
                    add_output(g, 3, True)

            row_max(0, 0)
            row_max(0, 1)
            with dve.Fori(0, NKV - 1) as g:
                group(g, False)
            group(NKV - 1, True)

            dve.wait_ge(wo_added, 4 * (NKV + 1))
            layer_norm(3)
            for t in range(TT):
                dve.wait_ge(routed, t + 1)
                note(nc.vector.tensor_copy(logits[:, t, :], bank[4 + t][:, ER:ER + EXP]))
            noted()
            link(nc.vector.tensor_reduce(top[:, :], logits[:, :, :], AX_X, ALU.max))
            link(nc.vector.tensor_tensor(r_eq[:, :, :], logits[:, :, :], top[:, :].unsqueeze(2).to_broadcast([P, TT, EXP]),
                                         ALU.is_equal))
            link(nc.vector.tensor_tensor(r_key[:, :, :], r_eq[:, :, :], desc8[:, :, :], ALU.mult))
            link(nc.vector.tensor_reduce(r_first[:, :], r_key[:, :, :], AX_X, ALU.max))
            link(nc.vector.tensor_tensor(r_gate[:, :, :], r_key[:, :, :],
                                         r_first[:, :].unsqueeze(2).to_broadcast([P, TT, EXP]), ALU.is_equal))
            link(nc.vector.tensor_tensor(r_gate[:, :, :], r_gate[:, :, :], top[:, :].unsqueeze(2).to_broadcast([P, TT, EXP]),
                                         ALU.mult))
            for t in range(TT):
                if t >= 2:
                    dve.wait_ge(whT_made, t - 1)
                nc.vector.tensor_tensor((wh, wh2)[t % 2][:, :].rearrange("p (e r) -> p e r", e=EXP),
                                        bank[4 + t][:, 0:ER].rearrange("p (e r) -> p e r", e=EXP),
                                        r_gate[:, t, :].unsqueeze(2).to_broadcast([P, EXP, ER // EXP]),
                                        ALU.mult).then_inc(gated, 1)
            for t in range(TT):
                dve.wait_ge(out_made, t + 1)
                nc.vector.tensor_tensor(x[:, t, :], bank[4 + t][:, :], x[:, t, :], ALU.add).then_inc(x_final, 1)


_INS = ["x", "ctx_4096", "L0_xattn_x1_scale", "L0_xattn_x1_zp", "L0_xattn_x2_scale", "L0_xattn_x2_zp", "L0_ffn_c1_w",
        "L0_ffn_c2_w", "L0_ffn_w1", "L0_ffn_w2t", "L1_xattn_Wq", "L1_xattn_bq", "L1_xattn_Wkv", "L1_xattn_bkv",
        "L1_xattn_Wo", "L1_xattn_bo", "L1_ffn_route_w", "L1_ffn_A", "L1_ffn_Bw"]
_OUTS = [((BATCH, SEQ, DIM), "float32")]


def kernel(**inputs):
    import numpy as _np
    import concourse.bacc as _bacc
    from concourse import mybir as _mybir
    from concourse.bass_utils import run_bass_kernel_spmd as _run

    nc = _bacc.Bacc("TRN2", target_bir_lowering=False, num_devices=1)
    arrays, args = {}, []
    for name in _INS:
        a = _np.ascontiguousarray(inputs[name])
        arrays[f"in_{name}_dram"] = a
        args.append(nc.dram_tensor(f"in_{name}_dram", a.shape, _mybir.dt.from_np(a.dtype), kind="ExternalInput").ap())
    for i, (shape, dtype) in enumerate(_OUTS):
        dt = _mybir.dt.from_np(_np.dtype(dtype))
        args.append(nc.dram_tensor(f"out_{i}_dram", shape, dt, kind="ExternalOutput").ap())
    xattn_ffn_kernel(nc, *args)
    r = _run(nc, [arrays], core_ids=[0])
    got = tuple(r.results[0][f"out_{i}_dram"] for i in range(len(_OUTS)))
    return got[0]
```

```python
from contextlib import ExitStack

import concourse.bass as bass
from concourse import mybir

ALU = mybir.AluOpType
ACT = mybir.ActivationFunctionType
AX_X = mybir.AxisListType.X
F32 = mybir.dt.float32
F32R = mybir.dt.float32r
BF16 = mybir.dt.bfloat16

P = 128
BATCH, SEQ, DIM, CTX = 2, 256, 512, 512
TOK = BATCH * SEQ
TT = TOK // P
KD = DIM // P
MT = CTX // P
INTER, BLK, RANK = 1792, 32, 16
CHUNK = 256
NCHUNK = INTER // CHUNK
CI = CHUNK // P
NHEAD, NKV, HDIM = 32, 8, 128
G = NHEAD // NKV
EXP, ER = 8, 128
EPS = 1e-5
QMAX = 255.0
CENTRE = 128.0
ROUND = 1.5 * 2.0 ** 23
SCALE = 1.0 / HDIM ** 0.5
RING = 5
UNITS = 16
LOW_SET = (0, 0, 2, 4, 6, 8)
HIGH_SET = (0, 0, 0, 1, 2, 3)
LOW_WO = (9, 11, 15, 15)
LOW_WO_LAST = (9, 10, 12, 13)
SETUP = (("ctx", 0, 0), ("ctx", 0, 1), ("xq", 0), ("ctx", 0, 2), ("xq", 1), ("ctx", 0, 3), ("ctx", 1, 0), ("col", 0),
         ("xq", 2), ("xq", 3), ("col", 1), ("c1",), ("c2", 0), ("c2", 1), ("c2", 2), ("c2", 3), ("bias",), ("ctx", 1, 1),
         ("ctx", 1, 2), ("ctx", 1, 3))
SETUP_BANKS = 4
LAST_DOWN = ((0, 1, 2), (3,))
C2_PIECES = -(-INTER // 512)


def xattn_ffn_kernel(nc: bass.Bass, x_in, ctx_in, s1_in, z1_in, s2_in, z2_in, c1_in, c2_in, w1_in, w2_in,
                     wq_in, bq_in, wkv_in, bkv_in, wo_in, bo_in, route_in, a_in, bw_in, out):
    with ExitStack() as ctx:
        def sbuf(stack, name, shape, dt):
            return stack.enter_context(nc.sbuf_tensor(name, shape, dt))

        def pair(stack, name, shape):
            return (sbuf(stack, name + "_hi", shape, F32R), sbuf(stack, name + "_lo", shape, F32R))

        def sem(name):
            return ctx.enter_context(nc.semaphore(name))

        x = sbuf(ctx, "x", [P, TT, DIM], F32)
        ctxT = pair(ctx, "ctxT", [P, KD, BATCH * CTX])
        xT = pair(ctx, "xT", [P, KD, TOK])
        bo_row = sbuf(ctx, "bo_row", [P, DIM], F32)
        ident = sbuf(ctx, "ident", [P, P], F32)
        ident_b = sbuf(ctx, "ident_b", [P, P], BF16)
        ones_b = sbuf(ctx, "ones_b", [P, P], BF16)
        bias_all = sbuf(ctx, "bias_all", [P, 48], F32)
        bias_q = sbuf(ctx, "bias_q", [P, G], F32)
        bias_k = sbuf(ctx, "bias_k", [P, 1], F32)
        bias_v = sbuf(ctx, "bias_v", [P, 1], F32)
        stats = sbuf(ctx, "stats", [P, TT, 6], F32)
        moments = sbuf(ctx, "moments", [P, TT, 2], F32)
        ln_a = sbuf(ctx, "ln_a", [P, TT], F32)
        ln_b = sbuf(ctx, "ln_b", [P, TT], F32)
        ln_c = sbuf(ctx, "ln_c", [P, TT], F32)
        rstd = sbuf(ctx, "rstd", [P, TT], F32)
        scal = sbuf(ctx, "scal", [P, 4], F32)
        unread = sbuf(ctx, "unread", [P, 1], F32)
        derived = sbuf(ctx, "derived", [P, 10], F32)
        row_sum = sbuf(ctx, "row_sum", [P, TT], F32)
        row_add = sbuf(ctx, "row_add", [P, TT], F32)
        neg_lo_t = sbuf(ctx, "neg_lo_t", [P, 1], F32)
        neg_lo_c = sbuf(ctx, "neg_lo_c", [P, 1], F32)
        neg_max = sbuf(ctx, "neg_max", [P, UNITS], F32)
        neg_bias = sbuf(ctx, "neg_bias", [P, UNITS], F32)
        exp_sum = sbuf(ctx, "exp_sum", [P, UNITS], F32)
        exp_inv = sbuf(ctx, "exp_inv", [P, UNITS], F32)
        w_raw = sbuf(ctx, "w_raw", [P, RING, 512], F32)
        wk = pair(ctx, "wk", [P, KD, HDIM])
        wv = pair(ctx, "wv", [P, KD, HDIM])
        desc8 = sbuf(ctx, "desc8", [P, TT, EXP], F32)
        with ExitStack() as early:
            wq = pair(early, "wq", [P, KD, G * HDIM])
            wq_end = nc.sbuf_base
        with ExitStack() as early:
            ctxT_whole = sbuf(early, "ctxT_whole", [P, KD, BATCH * CTX], F32)
            assert nc.sbuf_base <= wq_end
        a_raw = sbuf(ctx, "a_raw", [P, DIM], F32)
        r_raw = sbuf(ctx, "r_raw", [EXP, DIM], F32)
        b_raw = sbuf(ctx, "b_raw", [P, KD, ER], F32)
        raT = sbuf(ctx, "raT", [P, KD, ER + EXP], F32)
        bT = sbuf(ctx, "bT", [P, DIM], F32)
        whT = sbuf(ctx, "whT", [P, TOK], F32)
        wh = sbuf(ctx, "wh", [P, TT, ER], F32)
        top = sbuf(ctx, "top", [P, TT], F32)
        r_eq = sbuf(ctx, "r_eq", [P, TT, EXP], F32)
        r_key = sbuf(ctx, "r_key", [P, TT, EXP], F32)
        r_first = sbuf(ctx, "r_first", [P, TT], F32)
        r_gate = sbuf(ctx, "r_gate", [P, TT, EXP], F32)
        sbuf(ctx, "fill", [P, (wq_end - nc.sbuf_base) // 4], F32)
        xT3 = w_raw
        with ExitStack() as first:
            ctx_raw = sbuf(first, "ctx_raw", [P, BATCH * MT, DIM], F32)
            xn_last = ctx_raw
            ctx_q = sbuf(first, "ctx_q", [P, BATCH * MT, DIM], BF16)
            x_q = sbuf(first, "x_q", [P, TT, DIM], BF16)
            xqT = sbuf(first, "xqT", [P, KD, TOK], BF16)
            col_add = sbuf(first, "col_add", [P, BATCH, DIM], F32)
            c1_rep = sbuf(first, "c1_rep", [P, DIM], F32)
            c1T = pair(first, "c1T", [P, KD, P])
            c2_raw = sbuf(first, "c2_raw", [P, INTER // P, RANK], F32)
            c2_rep = sbuf(first, "c2_rep", [P, INTER // P, 4, 32], F32)
            bias_rows = sbuf(first, "bias_rows", [48, HDIM], F32)
            c2_stack = sbuf(first, "c2_stack", [P, INTER], F32R)
            t_stack = sbuf(first, "t_stack", [P, TOK], F32R)
            one_hot = sbuf(first, "one_hot", [P, TT, CHUNK], BF16)
            oh_eq = sbuf(first, "oh_eq", [P, 16, BLK], BF16)
            oh_key = sbuf(first, "oh_key", [P, 16, BLK], BF16)
            oh_max = sbuf(first, "oh_max", [P, 16], F32)
            oh_first = sbuf(first, "oh_first", [P, 16], F32)
            desc = sbuf(first, "desc", [P, 16, BLK], BF16)
            w1_raw = sbuf(first, "w1_raw", [P, CI, DIM], F32)
            w2_raw = sbuf(first, "w2_raw", [P, CI, DIM], F32)
            w1T = pair(first, "w1T", [P, KD, CHUNK])
            h = sbuf(first, "h", [P, CI, TOK], F32)
            one_hotT = sbuf(first, "one_hotT", [P, CI, TOK], BF16)
            with ExitStack() as work:
                ctx_work = sbuf(work, "ctx_work", [P, BATCH * MT, DIM], F32)
            hT = pair(first, "hT", [P, CI, TOK])
            w2 = pair(first, "w2", [P, CI, DIM])
            xn = sbuf(first, "xn", [P, TT, DIM], F32)
        k = pair(ctx, "k", [P, BATCH * CTX])
        v = pair(ctx, "v", [P, BATCH * MT, HDIM])
        vT = sbuf(ctx, "vT", [P, BATCH * CTX], F32)
        q = pair(ctx, "q", [P, G, TOK])
        wo = pair(ctx, "wo", [P, G, DIM])
        prob = sbuf(ctx, "prob", [P, 4, CTX], F32)
        probT = [pair(ctx, f"probT{i}", [P, MT, 512]) for i in range(2)]
        o = pair(ctx, "o", [P, G, TOK])

        bank = [ctx.enter_context(nc.psum_tensor(f"bank{i}", [P, 512], F32)) for i in range(8)]

        ld_scal, ld_c1, ld_c2, ld_bias, ld_bo = (sem(f"ld_{n}") for n in ("scal", "c1", "c2", "bias", "bo"))
        ld_x = [sem(f"ld_x{b}") for b in range(BATCH)]
        ld_ctx = [sem(f"ld_ctx{b}") for b in range(BATCH)]
        ld_w1, ld_w2, ld_last = sem("ld_w1"), sem("ld_w2"), sem("ld_last")
        ld_w = [sem(f"ld_ring{s}") for s in range(RING)]
        stored = sem("stored")
        pool_step, pool_const = sem("pool_step"), sem("pool_const")
        dve_step = sem("dve_step")
        setup_made, setup_read = sem("setup_made"), sem("setup_read")
        c1T_lo, c2_spread, c2_made = sem("c1T_lo"), sem("c2_spread"), sem("c2_made")
        scales_ready, x_scaled, ctx_scaled, ctx_clipped, x_quant = (
            sem(n) for n in ("scales_ready", "x_scaled", "ctx_scaled", "ctx_clipped", "x_quant"))
        ctx_quant = [sem(f"ctx_quant{b}") for b in range(BATCH)]
        row_summed, ab_made, ctxT_lo = sem("row_summed"), sem("ab_made"), sem("ctxT_lo")
        var_made, sqrt_made, xn_made = sem("var_made"), sem("sqrt_made"), sem("xn_made")
        xT_made, xT_hi, xT_lo = sem("xT_made"), sem("xT_hi"), sem("xT_lo")
        t_made, t_hi, t_lo = sem("t_made"), sem("t_hi"), sem("t_lo")
        raT_made, raT_read, bT_made, bT_read = sem("raT_made"), sem("raT_read"), sem("bT_made"), sem("bT_read")
        xT3_made, xT3_read, routed, gated = sem("xT3_made"), sem("xT3_read"), sem("routed"), sem("gated")
        whT_made, whT_read, out_made, x_final = sem("whT_made"), sem("whT_read"), sem("out_made"), sem("x_final")
        w1T_made, w1T_hi, w1T_lo = sem("w1T_made"), sem("w1T_hi"), sem("w1T_lo")
        w2_hi, w2_lo = sem("w2_hi"), sem("w2_lo")
        inter_made, oh_step = sem("inter_made"), sem("oh_step")
        h_made, h_masked, hT_hi, hT_lo = (sem(n) for n in ("h_made", "h_masked", "hT_hi", "hT_lo"))
        oh_turned, oh_read = sem("oh_turned"), sem("oh_read")
        y_made = sem("y_made")
        w_hi, w_lo = sem("w_hi"), sem("w_lo")
        proj_made, proj_hi, proj_read = sem("proj_made"), sem("proj_hi"), sem("proj_read")
        early_made, early_read = sem("early_made"), sem("early_read")
        bo_added = sem("bo_added")
        bias_set, bv_set = sem("bias_set"), sem("bv_set")
        s_made, max_made, exp_made, inv_made, prob_made = (
            sem(n) for n in ("s_made", "max_made", "exp_made", "inv_made", "prob_made"))
        nb_made = sem("nb_made")
        pT_made, pT_hi, pT_lo = sem("pT_made"), sem("pT_hi"), sem("pT_lo")
        o_made, o_hi, o_lo = sem("o_made"), sem("o_hi"), sem("o_lo")
        wo_made, wo_added = sem("wo_made"), sem("wo_added")

        x_rows = x_in.rearrange("b (t p) d -> p (b t) d", p=P)
        out_rows = out.rearrange("b (t p) d -> p (b t) d", p=P)
        ctx_rows = ctx_in.rearrange("b (t p) d -> b p t d", p=P)
        w1_rows = w1_in.rearrange("(c i p) d -> c p i d", i=CI, p=P)
        w2_rows = w2_in.rearrange("(c i p) d -> c p i d", i=CI, p=P)
        wq_cols = wq_in.rearrange("(k p) n -> k p n", p=P)
        wkv_cols = wkv_in.rearrange("(k p) n -> p k n", p=P)
        wo_rows = wo_in.rearrange("(g j p) d -> g j p d", j=G, p=P)

        def s_bank(u):
            return bank[(0, 1, 6, 7)[u % 4]][:, :]

        def o_bank(quad):
            return bank[4 + quad % 2][:, :]

        def set_bank(idx):
            return bank[(0, 1, 6, 7, 2, 3, 6, 7, 6, 7)[idx]][:, :]

        def early_bank(b):
            return bank[5 + b][:, :]

        def out_bank(t, last):
            return bank[((0, 1, 6, 7) if last else (6, 7, 5, 5))[t]][:, :]

        def last_down_count(t):
            done = 0
            for tiles in LAST_DOWN:
                if t in tiles:
                    return done + len(tiles) + tiles.index(t) + 1
                done += 2 * len(tiles)

        def setup_count(*job):
            return SETUP.index(job) + 1

        def x_bank(n, kk):
            return bank[((0, 1, 2, 3), (6, 7, 4, 5))[n][kk]][:, :]

        def w1_bank(c, part):
            return bank[(5 if isinstance(c, int) and c == 0 else 1) + part][:, :]

        def flat(tile):
            return tile[:, :, :].rearrange("p a b -> p (a b)")

        def c2_piece(i):
            at, n = 512 * i, min(512, INTER - 512 * i)
            return c2_stack[:, at:at + n], ctx_work[:, i, 0:n]

        def hidden(b):
            return bank[4 + b][:, 0:2 * (ER + EXP)].rearrange("p (t n) -> p t n", t=2)

        def mm3(dst, left, right, start, stop):
            nc.tensor.matmul(dst, left(0), right(0), start=start, stop=False)
            nc.tensor.matmul(dst, left(0), right(1), start=False, stop=False)
            return nc.tensor.matmul(dst, left(1), right(0), start=False, stop=stop)

        block = ctx.enter_context(nc.Block())

        @block.sync
        def _(sp):
            for b in range(BATCH):
                sp.dma_start(x[:, 2 * b:2 * b + 2, :], x_rows[:, 2 * b:2 * b + 2, :]).then_inc(ld_x[b], 16)
            for i, src in enumerate((s1_in, s2_in, z1_in, z2_in)):
                sp.dma_start(scal[:, i:i + 1], src.rearrange("(a n) -> a n", a=1).to_broadcast([P, 1])).then_inc(ld_scal, 16)
            for b in range(BATCH):
                sp.dma_start(ctx_raw[:, b * MT:(b + 1) * MT, :], ctx_rows[b]).then_inc(ld_ctx[b], 16)
            sp.wait_ge(pool_const, 1)
            for r in range(4):
                sp.dma_start(c1_rep[32 * r:32 * r + RANK, :], c1_in).then_inc(ld_c1, 16)
            sp.dma_start(c2_raw[:, :, :], c2_in.rearrange("(i p) r -> p i r", p=P)).then_inc(ld_c2, 16)
            sp.dma_start(bias_rows[0:32, :], bq_in.rearrange("(h d) -> h d", d=HDIM)).then_inc(ld_bias, 16)
            sp.dma_start(bias_rows[32:48, :], bkv_in.rearrange("(h d) -> h d", d=HDIM)).then_inc(ld_bias, 16)
            sp.dma_start(bo_row[:, :], bo_in.rearrange("(a n) -> a n", a=1).to_broadcast([P, DIM])).then_inc(ld_bo, 16)
            sp.dma_start(w1_raw[:, :, :], w1_rows[0]).then_inc(ld_w1, 16)
            sp.dma_start(w2_raw[:, :, :], w2_rows[0]).then_inc(ld_w2, 16)

            def weight(n, src, slot, shaped=False):
                if not isinstance(n, int) or n >= RING:
                    sp.wait_ge(w_lo, n - RING + 1)
                dst = w_raw[:, slot, :]
                if shaped:
                    dst = dst.rearrange("p (k n) -> p k n", k=KD)
                sp.dma_start(dst, src).then_inc(ld_w[slot], 16)

            def projection_weights(n0, s0, g, parts=range(2 + KD)):
                for i in parts:
                    if i == 0:
                        weight(n0, wkv_cols[:, :, bass.ts(g, HDIM)], s0 % RING, True)
                    elif i == 1:
                        weight(n0 + 1, wkv_cols[:, :, bass.ds(g * HDIM + NKV * HDIM, HDIM)], (s0 + 1) % RING, True)
                    else:
                        weight(n0 + i, wq_cols[i - 2, :, bass.ts(g, G * HDIM)], (s0 + i) % RING)

            def chunk_weights(c):
                sp.wait_ge(w1T_made, 2 * c)
                sp.dma_start(w1_raw[:, :, :], w1_rows[c]).then_inc(ld_w1, 16)
                sp.wait_ge(w2_lo, c)
                sp.dma_start(w2_raw[:, :, :], w2_rows[c]).then_inc(ld_w2, 16)

            projection_weights(0, 0, 0, range(RING))
            chunk_weights(1)
            projection_weights(0, 0, 0, range(RING, 2 + KD))
            with sp.Fori(2, NCHUNK) as c:
                chunk_weights(c)

            def out_weights(n0, s0, g):
                for j in range(G):
                    weight(n0 + j, wo_rows[g, j], (s0 + j) % RING)

            with sp.Fori(0, NKV - 1) as g:
                projection_weights(6 + 10 * g, 6, g + 1)
                out_weights(12 + 10 * g, 12, g)
            out_weights(6 + 10 * (NKV - 1), 6, NKV - 1)
            sp.wait_ge(proj_made, 10 * NKV)
            sp.dma_start(a_raw[:, :], a_in.rearrange("e r d -> (e r) d")).then_inc(ld_last, 16)
            sp.dma_start(r_raw[:, :], route_in).then_inc(ld_last, 16)
            for j in range(KD):
                sp.dma_start(b_raw[:, j, :].rearrange("p (e r) -> p e r", e=EXP),
                             bw_in[:, j * P:(j + 1) * P, :].rearrange("e p r -> p e r")).then_inc(ld_last, 16)
            for t in range(TT):
                sp.wait_ge(x_final, t + 1)
                sp.dma_start(out_rows[:, t, :], x[:, t, :]).then_inc(stored, 16)
            sp.wait_ge(stored, 16 * TT)

        @block.gpsimd
        def _(pool):
            nc.gpsimd.memset(c1_rep[:, :], 0.0).then_inc(pool_const, 1)
            nc.gpsimd.memset(ident[:, :], 0.0).then_inc(pool_step, 1)
            nc.gpsimd.memset(c2_rep[:, :, :, :], 0.0).then_inc(pool_const, 1)
            pool.wait_ge(pool_step, 1)
            nc.gpsimd.affine_select(out=ident[:, :], in_=ident[:, :], compare_op=ALU.not_equal, fill=1.0, base=0,
                                    pattern=[[-1, P]], channel_multiplier=1).then_inc(pool_const, 1)
            nc.gpsimd.iota(desc[:, :, :], pattern=[[0, 16], [-1, BLK]], base=BLK, channel_multiplier=0,
                           allow_small_or_imprecise_dtypes=True).then_inc(pool_const, 1)
            nc.gpsimd.iota(desc8[:, :, :], pattern=[[0, TT], [-1, EXP]], base=EXP, channel_multiplier=0,
                           allow_small_or_imprecise_dtypes=True).then_inc(pool_const, 1)
            pool.wait_ge(pool_const, 3)
            nc.gpsimd.tensor_copy(ident_b[:, :], ident[:, :]).then_inc(pool_const, 1)

            def low_half(n, slot, dst_hi, dst_lo, shaped=False):
                pool.wait_ge(w_hi, n + 1)
                src = w_raw[:, slot, :]
                if shaped:
                    src = src.rearrange("p (k n) -> p k n", k=KD)
                nc.gpsimd.tensor_tensor(dst_lo, src, dst_hi, ALU.subtract).then_inc(w_lo, 1)

            def projection_low(n0, s0, i):
                hi, lo = ((w[:, :, :] for w in wk) if i == 0 else (w[:, :, :] for w in wv) if i == 1 else
                          (w[:, i - 2, :] for w in wq))
                low_half(n0 + i, (s0 + i) % RING, hi, lo, i < 2)

            pool.wait_ge(scales_ready, 1)
            for b in range(BATCH):
                if b == 1:
                    for t in range(1, TT):
                        pool.wait_ge(xn_made, t + 1)
                        nc.gpsimd.tensor_scalar(xn[:, t, :], xn[:, t, :], derived[:, 0:1], scal[:, 2:3],
                                                ALU.mult, ALU.add).then_inc(x_scaled, 1)
                pool.wait_ge(ld_ctx[b], 16)
                for i in range(MT):
                    nc.gpsimd.tensor_scalar(ctx_work[:, b * MT + i, :], ctx_raw[:, b * MT + i, :], derived[:, 1:2], scal[:, 3:4],
                                            ALU.mult, ALU.add).then_inc(ctx_scaled, 1)
            for i in range(MT):
                pool.wait_ge(ctx_clipped, MT + i + 1)
                nc.gpsimd.tensor_scalar(ctx_work[:, MT + i, :], ctx_work[:, MT + i, :], 1.0, ROUND, ALU.mult,
                                        ALU.add).then_inc(pool_step, 1)
            for i in range(MT):
                pool.wait_ge(pool_step, 2 + i)
                nc.gpsimd.tensor_scalar(ctx_q[:, MT + i, :], ctx_work[:, MT + i, :], 1.0, -(ROUND + CENTRE), ALU.mult,
                                        ALU.add).then_inc(ctx_quant[1], 1)
            for job in SETUP:
                if job[0] == "c1":
                    pool.wait_ge(setup_read, setup_count(*job))
                    nc.gpsimd.tensor_tensor(flat(c1T[1]), h[:, 0, :], flat(c1T[0]),
                                            ALU.subtract).then_inc(c1T_lo, 1)
            for job in SETUP:
                if job[0] == "ctx":
                    pool.wait_ge(setup_read, setup_count(*job))
                    at = (slice(None), job[2], slice(job[1] * CTX, (job[1] + 1) * CTX))
                    nc.gpsimd.tensor_tensor(ctxT[1][at], ctxT_whole[at], ctxT[0][at],
                                            ALU.subtract).then_inc(ctxT_lo, 1)

            def w2_low(c):
                pool.wait_ge(w2_hi, c + 1)
                nc.gpsimd.tensor_tensor(w2[1][:, :, :], w2_raw[:, :, :], w2[0][:, :, :], ALU.subtract).then_inc(w2_lo, 1)

            w2_low(0)
            for i in range(6):
                projection_low(0, 0, i)
            with pool.Fori(1, NCHUNK) as c:
                w2_low(c)

            def normalise(g, u):
                pool.wait_ge(inv_made, UNITS * g + u + 1)
                nc.gpsimd.tensor_tensor(prob[:, u % 4, :], prob[:, u % 4, :], exp_inv[:, u:u + 1].to_broadcast([P, CTX]),
                                        ALU.mult).then_inc(prob_made, 1)

            def group(g, last):
                at = 6 if last else 12
                for u in range(UNITS):
                    normalise(g, u)
                    if not last:
                        for i in range(2 + KD):
                            if u == LOW_SET[i]:
                                projection_low(6 + 10 * g, 6, i)
                    for j in range(G):
                        if u == (LOW_WO_LAST if last else LOW_WO)[j]:
                            low_half(at + 10 * g + j, (at + j) % RING, wo[0][:, j, :], wo[1][:, j, :])

            pool.wait_ge(ld_bo, 16)
            for t in range(TT):
                pool.wait_ge(xn_made, 2 * TT + t + 1)
                nc.gpsimd.tensor_tensor(x[:, t, :], x[:, t, :], bo_row[:, :], ALU.add).then_inc(bo_added, 1)
            with pool.Fori(0, NKV - 1) as g:
                group(g, False)
            group(NKV - 1, True)

        @block.tensor
        def _(pe):
            def setup_job(n, job):
                if n >= SETUP_BANKS:
                    pe.wait_ge(setup_read, n - SETUP_BANKS + 1)
                to, kind = bank[n % SETUP_BANKS][:, :], job[0]
                if kind == "ctx":
                    b, kk = job[1:]
                    pe.wait_ge(ld_ctx[b], 16)
                    for m in range(MT):
                        ins = nc.tensor.transpose(to[:, m * P:(m + 1) * P], ctx_raw[:, b * MT + m, kk * P:(kk + 1) * P],
                                                  ident[:, :])
                elif kind == "xq":
                    pe.wait_ge(x_quant, job[1] + 1)
                    for kk in range(KD):
                        ins = nc.tensor.transpose(to.bitcast(BF16)[:, kk * P:(kk + 1) * P],
                                                  x_q[:, job[1], kk * P:(kk + 1) * P], ident_b[:, :])
                elif kind == "c1":
                    pe.wait_ge(ld_c1, 64)
                    for kk in range(KD):
                        ins = nc.tensor.transpose(to[:, kk * P:(kk + 1) * P], c1_rep[:, kk * P:(kk + 1) * P], ident[:, :])
                elif kind == "c2":
                    pe.wait_ge(c2_spread, 4)
                    for i in range(4 * job[1], min(4 * job[1] + 4, INTER // P)):
                        ins = nc.tensor.transpose(to[:, (i % 4) * P:(i % 4 + 1) * P],
                                                  c2_rep[:, i, :, :].rearrange("p a b -> p (a b)"), ident[:, :])
                elif kind == "bias":
                    pe.wait_ge(ld_bias, 32)
                    ins = nc.tensor.transpose(to[:, 0:48], bias_rows[:, :], ident[0:48, 0:48])
                else:
                    b = job[1]
                    pe.wait_ge(ctx_quant[b], MT)
                    for kk in range(MT):
                        ins = nc.tensor.matmul(to, ones_b[:, :], ctx_q[:, b * MT + kk, :],
                                               start=(kk == 0), stop=(kk == MT - 1))
                ins.then_inc(setup_made, 1)

            def quantised_product(t):
                pe.wait_ge(setup_read, setup_count("xq", t))
                pe.wait_ge(ctx_quant[t // 2], MT)
                for kk in range(MT):
                    ins = nc.tensor.matmul(bank[4 + t][:, :], xqT[:, kk, t * P:(t + 1) * P],
                                           ctx_q[:, t // 2 * MT + kk, :], start=(kk == 0), stop=(kk == MT - 1))
                ins.then_inc(ab_made, 1)

            pe.wait_ge(pool_const, 6)
            for n, job in enumerate(SETUP):
                setup_job(n, job)
                for t in {("col", 0): (0,), ("xq", 2): (1,), ("col", 1): (2, 3)}.get(job, ()):
                    quantised_product(t)

            def x_transposed(n, kk):
                for t in range(TT):
                    if kk == 0:
                        pe.wait_ge(xn_made, TT * (n + 1) + t + 1)
                    ins = nc.tensor.transpose(x_bank(n, kk)[:, t * P:(t + 1) * P], xn[:, t, kk * P:(kk + 1) * P],
                                              ident[:, :])
                ins.then_inc(xT_made, 1)

            def transpose_w1(c, part):
                pe.wait_ge(ld_w1, 16 * (c + 1))
                if not isinstance(c, int) or c >= 1:
                    pe.wait_ge(h_masked, 2 * c - 1 + part)
                for kk in range(2):
                    for i in range(CI):
                        ins = nc.tensor.transpose(w1_bank(c, part)[:, kk * CHUNK + i * P:kk * CHUNK + (i + 1) * P],
                                                  w1_raw[:, i, (2 * part + kk) * P:(2 * part + kk + 1) * P], ident[:, :])
                ins.then_inc(w1T_made, 1)

            def inter(c, half):
                if half == 0 and isinstance(c, int) and c == 0:
                    pe.wait_ge(t_lo, 1)
                    pe.wait_ge(c2_made, 1)
                if half == 1:
                    pe.wait_ge(oh_step, 10 * c + 2)
                elif not isinstance(c, int) or c >= 1:
                    pe.wait_ge(oh_step, 10 * c - 3)
                for t in range(2 * half, 2 * half + 2):
                    ins = nc.tensor.matmul(bank[0][:, (t % 2) * CHUNK:(t % 2 + 1) * CHUNK], t_stack[:, t * P:(t + 1) * P],
                                           c2_stack[:, bass.ts(c, CHUNK)], start=True, stop=True)
                ins.then_inc(inter_made, 1)

            def turn_one_hot(c):
                pe.wait_ge(oh_step, 10 * c + 10)
                if not isinstance(c, int) or c >= 1:
                    pe.wait_ge(oh_read, c)
                for i in range(CI):
                    for t in range(TT):
                        ins = nc.tensor.transpose(bank[3][:, :].bitcast(BF16)[:, i * TOK + t * P:i * TOK + (t + 1) * P],
                                                  one_hot[:, t, i * P:(i + 1) * P], ident_b[:, :])
                ins.then_inc(oh_turned, 1)

            def up(c, i, between=None):
                if i == 0:
                    pe.wait_ge(w1T_lo, 2 * (c + 1))
                for kk in range(KD):
                    if kk == 2 and between is not None:
                        between()
                    ins = mm3(bank[1 + i][:, :], lambda s: w1T[s][:, kk, i * P:(i + 1) * P], lambda s: xT[s][:, kk, :],
                              kk == 0, kk == KD - 1)
                ins.then_inc(h_made, 1)

            def early_vT(b):
                pe.wait_ge(w_lo, 2)
                pe.wait_ge(ctxT_lo, 2 * KD)
                for kk in range(KD):
                    ins = mm3(early_bank(b), lambda s: wv[s][:, kk, :], lambda s: ctxT[s][:, kk, b * CTX:(b + 1) * CTX],
                              kk == 0, kk == KD - 1)
                ins.then_inc(early_made, 1)

            def down(c, i, first, last, tiles=range(TT)):
                pe.wait_ge(hT_lo, 2 * c + i + 1)
                for t in tiles:
                    mm3(bank[4 + t][:, :], lambda s: hT[s][:, i, t * P:(t + 1) * P], lambda s: w2[s][:, i, :],
                        first and i == 0, last and i == CI - 1).then_inc(y_made, 1)

            def chunk(c, first, last):
                def one_hots():
                    turn_one_hot(c)
                    if not last:
                        inter(c + 1, 0)

                up(c, 0, between=(lambda: inter(c, 0)) if first else one_hots)
                if first:
                    up(c, 1)
                    inter(c, 1)
                    early_vT(0)
                    turn_one_hot(c)
                    inter(c + 1, 0)
                    early_vT(1)
                else:
                    up(c, 1)
                if not last:
                    transpose_w1(c + 1, 0)
                pe.wait_ge(w2_lo, c + 1)
                if first:
                    pe.wait_ge(early_read, BATCH)
                if last:
                    for tiles in LAST_DOWN:
                        down(c, 0, first, last, tiles)
                        down(c, 1, first, last, tiles)
                else:
                    down(c, 0, first, last)
                    inter(c + 1, 1)
                    transpose_w1(c + 1, 1)
                    down(c, 1, first, last)
                if first:
                    pe.wait_ge(c2_made, C2_PIECES)

            pe.wait_ge(var_made, 2)
            transpose_w1(0, 0)
            transpose_w1(0, 1)
            pe.wait_ge(setup_read, len(SETUP))
            for kk in range(KD):
                x_transposed(0, kk)
            pe.wait_ge(c1T_lo, 1)
            for kk in range(KD):
                pe.wait_ge(xT_lo, kk + 1)
                ins = mm3(bank[4][:, :], lambda s: c1T[s][:, kk, :], lambda s: xT[s][:, kk, :], kk == 0, kk == KD - 1)
            ins.then_inc(t_made, 1)
            chunk(0, True, False)
            with pe.Fori(1, NCHUNK - 1) as c:
                chunk(c, False, False)
            chunk(NCHUNK - 1, False, True)

            def project(idx, base, g, left, right):
                if idx < 4 and g is not None:
                    pe.wait_ge(exp_made, UNITS * g + 13 + idx)
                elif idx >= 4:
                    pe.wait_ge(proj_read, base + (3, 4, 7, 8)[idx - 6])
                for kk in range(KD):
                    if g is None and idx == 6:
                        pe.wait_ge(xT_lo, KD + kk + 1)
                    ins = mm3(set_bank(idx), lambda s: left(s, kk), lambda s: right(s, kk), kk == 0, kk == KD - 1)
                ins.then_inc(proj_made, 3 if g is None and idx == 1 else 1)

            def project_k(b, base, g):
                project(b, base, g, lambda s, kk: wk[s][:, kk, :], lambda s, kk: ctxT[s][:, kk, b * CTX:(b + 1) * CTX])

            def project_vT(b, base, g):
                project(2 + b, base, g, lambda s, kk: wv[s][:, kk, :], lambda s, kk: ctxT[s][:, kk, b * CTX:(b + 1) * CTX])

            def project_q(head, base, g):
                project(6 + head, base, g, lambda s, kk: wq[s][:, kk, head * HDIM:(head + 1) * HDIM],
                        lambda s, kk: xT[s][:, kk, :])

            def transpose_v(b, base, g):
                if g is None:
                    pe.wait_ge(early_read, BATCH)
                else:
                    pe.wait_ge(proj_read, base + 3 + b)
                    pe.wait_ge(pT_lo, UNITS * g + 15 + b)
                for m in range(MT):
                    ins = nc.tensor.transpose(set_bank(4 + b)[:, m * P:(m + 1) * P],
                                              vT[:, b * CTX + m * P:b * CTX + (m + 1) * P], ident[:, :])
                ins.then_inc(proj_made, 1)

            def weights_ready(n):
                pe.wait_ge(w_lo, n)

            def scores(g, u):
                quad, j = u // 4, u % 4
                b, head, lt = quad // 2, 2 * (quad % 2) + j // 2, j % 2
                if lt == 0 and b == 0:
                    pe.wait_ge(proj_read, 10 * g + 7 + head)
                if u >= 4:
                    pe.wait_ge(exp_made, UNITS * g + u - 3)
                elif u >= 2:
                    pe.wait_ge(wo_added, 4 * g + u - 1)
                    pe.wait_ge(proj_read, 10 * g + 7 + u)
                at = b * SEQ + lt * P
                mm3(s_bank(u), lambda s: q[s][:, head, at:at + P], lambda s: k[s][:, b * CTX:(b + 1) * CTX],
                    True, True).then_inc(s_made, 1)

            def transpose_p(g, u):
                pe.wait_ge(prob_made, UNITS * g + u + 1)
                if u >= 2:
                    pe.wait_ge(pT_lo, UNITS * g + u - 1)
                for m in range(MT):
                    ins = nc.tensor.transpose(bank[2 + u % 2][:, m * P:(m + 1) * P], prob[:, u % 4, m * P:(m + 1) * P],
                                              ident[:, :])
                ins.then_inc(pT_made, 1)

            def values(g, quad, m):
                b = quad // 2
                if m == 0:
                    pe.wait_ge(pT_lo, UNITS * g + 4 * quad + 4)
                    if quad >= 2:
                        pe.wait_ge(o_lo, 4 * g + quad - 1)
                    if quad == 1:
                        pe.wait_ge(wo_added, 4 * g + 4)
                ins = mm3(o_bank(quad), lambda s: v[s][:, b * MT + m, :], lambda s: probT[quad % 2][s][:, m, :],
                          m == 0, m == MT - 1)
                if m == MT - 1:
                    ins.then_inc(o_made, 1)

            def output(g, t, last):
                pe.wait_ge(o_lo, 4 * g + (2 if t < 2 else 4))
                if last:
                    pe.wait_ge(exp_made, UNITS * g + 13 + t)
                elif t < 2:
                    pe.wait_ge(proj_read, 10 * g + 19 + t)
                for j in range(G):
                    output_part(g, t, j, last)

            def output_part(g, t, j, last):
                if t == 3 and j == 0 and not last:
                    pe.wait_ge(wo_added, 4 * g + 7)
                ins = mm3(out_bank(t, last), lambda s: o[s][:, j, t * P:(t + 1) * P], lambda s: wo[s][:, j, :],
                          j == 0, j == G - 1)
                if j == G - 1:
                    ins.then_inc(wo_made, 1)

            def last_weights():
                pe.wait_ge(ld_last, 16 * (2 + KD))
                for kk in range(KD):
                    if kk >= 2:
                        pe.wait_ge(raT_read, kk - 1)
                    nc.tensor.transpose(bank[2 + kk % 2][:, 0:ER], a_raw[:, kk * P:(kk + 1) * P], ident[:, :])
                    nc.tensor.transpose(bank[2 + kk % 2][:, ER:ER + EXP], r_raw[:, kk * P:(kk + 1) * P],
                                        ident[0:EXP, 0:EXP]).then_inc(raT_made, 1)
                pe.wait_ge(o_lo, 4 * NKV - 1)
                for j in range(KD):
                    ins = nc.tensor.transpose(bank[4][:, j * P:(j + 1) * P], b_raw[:, j, :], ident[:, :])
                ins.then_inc(bT_made, 1)

            def group_head(g, first):
                for u in range(2, 7):
                    if first and u == 3:
                        transpose_p(g, 0)
                    scores(g, u)
                    if u >= 3:
                        if not (first and u == 3):
                            transpose_p(g, u - 3)
                        if not first:
                            output_part(g - 1, 3, u - 3, False)

            def group_rest(g, last):
                base = 10 * g + 10
                for u in range(7, UNITS):
                    scores(g, u)
                    transpose_p(g, u - 3)
                    if u == 15 and not last:
                        weights_ready(12 + 10 * g)
                        project_k(0, base, g)
                    values(g, (u - 7) // 4, (u - 7) % 4)
                transpose_p(g, 13)
                values(g, 2, 1)
                if last:
                    weights_ready(10 + 10 * g)
                    output(g, 0, True)
                transpose_p(g, 14)
                values(g, 2, 2)
                values(g, 2, 3)
                transpose_p(g, 15)
                if not last:
                    project_k(1, base, g)
                    project_vT(0, base, g)
                    project_vT(1, base, g)
                else:
                    output(g, 1, True)
                for m in range(MT):
                    values(g, 3, m)
                if last:
                    last_weights()
                if not last:
                    transpose_v(0, base, g)
                    transpose_v(1, base, g)
                    for head in range(G):
                        project_q(head, base, g)
                    weights_ready(16 + 10 * g)
                    output(g, 0, False)
                    scores(g + 1, 0)
                    output(g, 1, False)
                    scores(g + 1, 1)
                    output(g, 2, False)
                else:
                    output(g, 2, True)
                    output(g, 3, True)

            project_k(0, 0, None)
            project_k(1, 0, None)
            transpose_v(0, 0, None)
            transpose_v(1, 0, None)
            for kk in range(KD):
                x_transposed(1, kk)
            weights_ready(6)
            project_q(0, 0, None)
            project_q(1, 0, None)
            scores(0, 0)
            scores(0, 1)
            project_q(2, 0, None)
            project_q(3, 0, None)
            group_head(0, True)
            with pe.Fori(0, NKV - 1) as g:
                group_rest(g, False)
                group_head(g + 1, False)
            group_rest(NKV - 1, True)

            for b in range(BATCH):
                for t in (2 * b, 2 * b + 1):
                    pe.wait_ge(xn_made, 3 * TT + t + 1)
                    pe.wait_ge(raT_read, KD)
                    for kk in range(KD):
                        ins = nc.tensor.transpose(bank[t][:, kk * P:(kk + 1) * P], xn_last[:, t, kk * P:(kk + 1) * P], ident[:, :])
                    ins.then_inc(xT3_made, 1)
                pe.wait_ge(bT_read, 1)
                for t in (2 * b, 2 * b + 1):
                    pe.wait_ge(xT3_read, t + 1)
                    for kk in range(KD):
                        ins = nc.tensor.matmul(hidden(b)[:, t % 2, :], xT3[:, t, kk * P:(kk + 1) * P], raT[:, kk, :],
                                               start=(kk == 0), stop=(kk == KD - 1))
                ins.then_inc(routed, 1)
            def turn_gated(b):
                pe.wait_ge(gated, b + 1)
                for t in (2 * b, 2 * b + 1):
                    ins = nc.tensor.transpose(bank[6 + b][:, (t % 2) * P:(t % 2 + 1) * P], wh[:, t, :], ident[:, :])
                ins.then_inc(whT_made, 1)

            def layer_output(t):
                pe.wait_ge(whT_read, t // 2 + 1)
                nc.tensor.matmul(bank[t][:, :], whT[:, t * P:(t + 1) * P], bT[:, :], start=True, stop=True)\
                    .then_inc(out_made, 1)

            turn_gated(0)
            layer_output(0)
            turn_gated(1)
            for t in range(1, TT):
                layer_output(t)

        @block.scalar
        def _(act):
            def root(n, tiles=slice(0, TT)):
                act.wait_ge(var_made, n + 1)
                nc.scalar.activation(ln_b[:, tiles], ln_a[:, tiles], ACT.Sqrt).then_inc(sqrt_made, 1)

            def weight_high(turn, slot, dst, shaped=False):
                act.wait_ge(ld_w[slot], 16 * turn)
                src = w_raw[:, slot, :]
                if shaped:
                    src = src.rearrange("p (k n) -> p k n", k=KD)
                nc.scalar.copy(dst, src).then_inc(w_hi, 1)

            def projection_high(turns, s0, i):
                dst = wk[0][:, :, :] if i == 0 else wv[0][:, :, :] if i == 1 else wq[0][:, i - 2, :]
                weight_high(turns + (s0 + i) // RING + 1, (s0 + i) % RING, dst, i < 2)

            root(0)
            for n, job in enumerate(SETUP):
                kind, src = job[0], bank[n % SETUP_BANKS][:, :]
                if kind == "c1":
                    act.wait_ge(pool_const, 2)
                    act.wait_ge(ld_c2, 16)
                    for r in range(4):
                        nc.scalar.copy(c2_rep[:, :, r, 0:RANK], c2_raw[:, :, :]).then_inc(c2_spread, 1)
                if job == ("ctx", 1, 1):
                    root(1)
                act.wait_ge(setup_made, n + 1)
                if kind == "ctx":
                    at = (slice(None), job[2], slice(job[1] * CTX, (job[1] + 1) * CTX))
                    nc.scalar.copy(ctxT[0][at], src)
                    nc.scalar.copy(ctxT_whole[at], src).then_inc(setup_read, 1)
                elif kind == "xq":
                    t = job[1]
                    nc.scalar.copy(xqT[:, :, t * P:(t + 1) * P],
                                   src[:, 0:256].bitcast(BF16).rearrange("p (k n) -> p k n", k=KD)).then_inc(setup_read, 1)
                    if t >= 1:
                        act.wait_ge(row_summed, t)
                    nc.scalar.activation(h[:, 0, :], x_q[:, t, :], ACT.Identity,
                                         accum_out=row_sum[:, t:t + 1]).then_inc(row_summed, 1)
                elif kind == "c1":
                    nc.scalar.copy(flat(c1T[0]), src)
                    act.wait_ge(row_summed, TT)
                    nc.scalar.copy(h[:, 0, :], src).then_inc(setup_read, 1)
                elif kind == "c2":
                    hi, whole = c2_piece(job[1])
                    nc.scalar.copy(hi, src[:, 0:whole.shape[1]])
                    nc.scalar.copy(whole, src[:, 0:whole.shape[1]]).then_inc(setup_read, 1)
                elif kind == "bias":
                    nc.scalar.copy(bias_all[:, :], src[:, 0:48]).then_inc(setup_read, 1)
                else:
                    nc.scalar.activation(col_add[:, job[1], :], src, ACT.Identity,
                                         scale=derived[:, 5:6]).then_inc(setup_read, 1)

            def x_high(n):
                for kk in range(KD):
                    act.wait_ge(xT_made, KD * n + kk + 1)
                    nc.scalar.copy(xT[0][:, kk, :], x_bank(n, kk)).then_inc(xT_hi, 1)

            def w1_high(c, part):
                act.wait_ge(w1T_made, 2 * c + part + 1)
                nc.scalar.copy(w1T[0][:, 2 * part:2 * part + 2, :],
                               w1_bank(c, part).rearrange("p (k n) -> p k n", k=2)).then_inc(w1T_hi, 1)

            def early_vT_copy(b):
                act.wait_ge(early_made, b + 1)
                nc.scalar.copy(vT[:, b * CTX:(b + 1) * CTX], early_bank(b)).then_inc(early_read, 1)

            def h_high(c, i):
                act.wait_ge(h_masked, 2 * c + i + 1)
                nc.scalar.copy(hT[0][:, i, :], h[:, i, :]).then_inc(hT_hi, 1)

            def chunk(c, first, last):
                if not first:
                    act.wait_ge(y_made, 8 * c)
                act.wait_ge(ld_w2, 16 * (c + 1))
                nc.scalar.copy(w2[0][:, :, :], w2_raw[:, :, :]).then_inc(w2_hi, 1)
                if first:
                    for i in range(RING):
                        if i == 2:
                            act.wait_ge(ctxT_lo, 2 * KD)
                        projection_high(0, 0, i)
                    early_vT_copy(0)
                act.wait_ge(oh_turned, c + 1)
                nc.scalar.copy(flat(one_hotT), bank[3][:, :].bitcast(BF16)).then_inc(oh_read, 1)
                h_high(c, 0)
                if first:
                    early_vT_copy(1)
                if not last:
                    w1_high(c + 1, 0)
                h_high(c, 1)
                if not last:
                    w1_high(c + 1, 1)

            w1_high(0, 0)
            w1_high(0, 1)
            x_high(0)
            act.wait_ge(t_made, 1)
            nc.scalar.copy(t_stack[:, :], bank[4][:, :]).then_inc(t_hi, 1)
            chunk(0, True, False)
            for i in range(RING, 2 + KD):
                projection_high(0, 0, i)
            with act.Fori(1, NCHUNK - 1) as c:
                chunk(c, False, False)
            chunk(NCHUNK - 1, False, True)

            def k_high(s, b):
                if b == 0:
                    act.wait_ge(bias_set, 2 * s + 2)
                act.wait_ge(proj_made, 10 * s + b + 1)
                nc.scalar.activation(k[0][:, b * CTX:(b + 1) * CTX], set_bank(b), ACT.Identity,
                                     bias=bias_k[:, 0:1]).then_inc(proj_hi, 1)

            def v_high(s, b):
                act.wait_ge(proj_made, 10 * s + 5 + b)
                nc.scalar.copy(v[0][:, b * MT:(b + 1) * MT, :],
                               set_bank(4 + b).rearrange("p (m d) -> p m d", m=MT)).then_inc(proj_hi, 1)

            def q_high(s, head):
                act.wait_ge(proj_made, 10 * s + 7 + head)
                nc.scalar.activation(q[0][:, head, :], set_bank(6 + head), ACT.Identity,
                                     bias=bias_q[:, head:head + 1]).then_inc(proj_hi, 1)

            root(2)
            k_high(0, 0)
            k_high(0, 1)
            x_high(1)
            v_high(0, 0)
            v_high(0, 1)

            def exponentials(g, u):
                act.wait_ge(max_made, UNITS * g + u + 1)
                nc.scalar.activation(prob[:, u % 4, :], s_bank(u), ACT.Exp, bias=neg_bias[:, u:u + 1],
                                     scale=SCALE, accum_out=exp_sum[:, u:u + 1]).then_inc(exp_made, 1)

            def p_high(g, u):
                quad, j = u // 4, u % 4
                if quad >= 2 and j == 0:
                    act.wait_ge(o_made, 4 * g + quad - 1)
                act.wait_ge(pT_made, UNITS * g + u + 1)
                nc.scalar.copy(probT[quad % 2][0][:, :, j * P:(j + 1) * P],
                               bank[2 + u % 2][:, :].rearrange("p (m n) -> p m n", m=MT)).then_inc(pT_hi, 1)

            def o_high(g, quad):
                b, hp = quad // 2, quad % 2
                if quad == 0:
                    act.wait_ge(bv_set, g + 1)
                act.wait_ge(o_made, 4 * g + quad + 1)
                nc.scalar.activation(o[0][:, 2 * hp:2 * hp + 2, b * SEQ:(b + 1) * SEQ],
                                     o_bank(quad).rearrange("p (h n) -> p h n", h=2), ACT.Identity,
                                     bias=bias_v[:, 0:1]).then_inc(o_hi, 1)

            def group(g, last):
                at = 6 if last else 12
                for u in range(UNITS):
                    if u == 12:
                        o_high(g, 0)
                    if u >= 3:
                        p_high(g, u - 3)
                    if u >= 1:
                        exponentials(g, u)
                    if not last:
                        if u == 0:
                            act.wait_ge(proj_made, 10 * g + 10)
                        for i in range(2 + KD):
                            if u == HIGH_SET[i]:
                                projection_high(2 * g, 6, i)
                    if 8 <= u < 12:
                        j = u - 8
                        weight_high(2 * g + (at + j) // RING + 1, (at + j) % RING, wo[0][:, j, :])
                o_high(g, 1)
                if not last:
                    k_high(g + 1, 0)
                p_high(g, 13)
                p_high(g, 14)
                o_high(g, 2)
                p_high(g, 15)
                if not last:
                    k_high(g + 1, 1)
                else:
                    nc.scalar.activation(unread[:, :], rstd[:, 0:1], ACT.Sqrt)
                    root(3, slice(0, 2))
                o_high(g, 3)
                if not last:
                    v_high(g + 1, 0)
                    v_high(g + 1, 1)
                    for head in range(G):
                        q_high(g + 1, head)
                    exponentials(g + 1, 0)

            q_high(0, 0)
            q_high(0, 1)
            exponentials(0, 0)
            q_high(0, 2)
            q_high(0, 3)
            with act.Fori(0, NKV - 1) as g:
                group(g, False)
            group(NKV - 1, True)

            for kk in range(KD):
                act.wait_ge(raT_made, kk + 1)
                nc.scalar.copy(raT[:, kk, :], bank[2 + kk % 2][:, 0:ER + EXP]).then_inc(raT_read, 1)
            act.wait_ge(bT_made, 1)
            nc.scalar.copy(bT[:, :], bank[4][:, :]).then_inc(bT_read, 1)
            act.wait_ge(w_lo, 10 * NKV)
            for b in range(BATCH):
                if b == 1:
                    root(4, slice(2, 4))
                for t in (2 * b, 2 * b + 1):
                    act.wait_ge(xT3_made, t + 1)
                    nc.scalar.copy(xT3[:, t, :], bank[t][:, :]).then_inc(xT3_read, 1)
            for b in range(BATCH):
                act.wait_ge(whT_made, b + 1)
                nc.scalar.copy(whT[:, 2 * b * P:(2 * b + 2) * P], bank[6 + b][:, 0:2 * P]).then_inc(whT_read, 1)

        @block.vector
        def _(dve):
            steps = [0]

            def link(ins):
                steps[0] += 1
                ins.then_inc(dve_step, 1)
                dve.wait_ge(dve_step, steps[0])

            def note(ins):
                steps[0] += 1
                ins.then_inc(dve_step, 1)

            def noted():
                dve.wait_ge(dve_step, steps[0])

            nc.vector.memset(neg_lo_t[:, :], 0.0)
            nc.vector.memset(neg_lo_c[:, :], 0.0)
            note(nc.vector.memset(ones_b[:, :], 1.0))
            noted()
            note(nc.vector.memset(neg_lo_t[64:128, :], -1.0))
            note(nc.vector.memset(neg_lo_c[32:64, :], -1.0))
            note(nc.vector.memset(neg_lo_c[96:128, :], -1.0))

            def tile_moments(t):
                note(nc.vector.bn_stats(stats[:, t, :], x[:, t, :]))
                noted()
                note(nc.vector.bn_aggr(moments[:, t, :], stats[:, t, :]))

            def layer_norm(n, tiles=range(TT), between=None):
                at = slice(tiles[0], tiles[-1] + 1)
                noted()
                nc.vector.tensor_scalar(ln_a[:, at], moments[:, at, 1], EPS, None, ALU.add).then_inc(var_made, 1)
                dve.wait_ge(sqrt_made, n + 1)
                link(nc.vector.reciprocal(ln_c[:, at], ln_b[:, at]))
                link(nc.vector.tensor_tensor(ln_b[:, at], ln_c[:, at], ln_c[:, at], ALU.mult))
                link(nc.vector.tensor_tensor(ln_b[:, at], ln_b[:, at], ln_a[:, at], ALU.mult))
                link(nc.vector.tensor_scalar(ln_b[:, at], ln_b[:, at], -0.5, 1.5, ALU.mult, ALU.add))
                link(nc.vector.tensor_tensor(rstd[:, at], ln_b[:, at], ln_c[:, at], ALU.mult))
                if between is not None:
                    between()
                for t in tiles:
                    nc.vector.tensor_scalar((xn if n < 3 else xn_last)[:, t, :], x[:, t, :], moments[:, t, 0:1],
                                            rstd[:, t:t + 1], ALU.subtract, ALU.mult).then_inc(xn_made, 1)

            for t in range(TT):
                if t % 2 == 0:
                    dve.wait_ge(ld_x[t // 2], 16)
                tile_moments(t)
            dve.wait_ge(ld_scal, 64)
            note(nc.vector.reciprocal(derived[:, 0:2], scal[:, 0:2]))
            note(nc.vector.tensor_tensor(derived[:, 2:3], scal[:, 0:1], scal[:, 1:2], ALU.mult))
            note(nc.vector.tensor_scalar(derived[:, 3:5], scal[:, 2:4], CENTRE, None, ALU.subtract))
            noted()
            link(nc.vector.tensor_scalar(derived[:, 5:7], derived[:, 3:5], derived[:, 2:3], -1.0, ALU.mult, ALU.mult))
            nc.vector.tensor_scalar(derived[:, 7:8], derived[:, 5:6], derived[:, 4:5], -float(CTX), ALU.mult, ALU.mult)\
                .then_inc(scales_ready, 1)
            layer_norm(0)
            for t in range(TT):
                dve.wait_ge(xn_made, t + 1)
                if t == 0:
                    link(nc.vector.tensor_scalar(xn[:, t, :], xn[:, t, :], derived[:, 0:1], scal[:, 2:3], ALU.mult, ALU.add))
                else:
                    dve.wait_ge(x_scaled, t)
                link(nc.vector.tensor_scalar(xn[:, t, :], xn[:, t, :], 0.0, QMAX, ALU.max, ALU.min))
                nc.vector.tensor_scalar(x_q[:, t, :], xn[:, t, :], ROUND, ROUND + CENTRE, ALU.add,
                                        ALU.subtract).then_inc(x_quant, 1)
                if t == 1:
                    for i in range(BATCH * MT):
                        dve.wait_ge(ctx_scaled, i + 1)
                        nc.vector.tensor_scalar(ctx_work[:, i, :], ctx_work[:, i, :], 0.0, QMAX, ALU.max, ALU.min)\
                            .then_inc(ctx_clipped, 1)
                        if i >= 1 and i <= MT:
                            dve.wait_ge(ctx_clipped, i)
                            nc.vector.tensor_scalar(ctx_q[:, i - 1, :], ctx_work[:, i - 1, :], ROUND, ROUND + CENTRE, ALU.add,
                                                    ALU.subtract).then_inc(ctx_quant[0], 1)
            dve.wait_ge(scales_ready, 1)
            for b in range(BATCH):
                at = slice(2 * b, 2 * b + 2)
                dve.wait_ge(row_summed, 2 * b + 2)
                link(nc.vector.tensor_scalar(row_add[:, at], row_sum[:, at], derived[:, 6:7], derived[:, 7:8], ALU.mult,
                                             ALU.add))
                dve.wait_ge(setup_read, setup_count("col", b))
                for t in range(2 * b, 2 * b + 2):
                    note(nc.vector.scalar_tensor_tensor(x[:, t, :], x[:, t, :], row_add[:, t:t + 1], col_add[:, b, :],
                                                        ALU.add, ALU.add))
                noted()
                for t in range(2 * b, 2 * b + 2):
                    dve.wait_ge(ab_made, t + 1)
                    link(nc.vector.scalar_tensor_tensor(x[:, t, :], bank[4 + t][:, :], derived[:, 2:3], x[:, t, :],
                                                        ALU.mult, ALU.add))
                    tile_moments(t)
            layer_norm(1)

            def x_low(n, kk):
                dve.wait_ge(xT_hi, KD * n + kk + 1)
                nc.vector.tensor_tensor(xT[1][:, kk, :], x_bank(n, kk), xT[0][:, kk, :], ALU.subtract)\
                    .then_inc(xT_lo, 1)

            def c2_together(i):
                dve.wait_ge(setup_read, setup_count("c2", i))
                hi, whole = c2_piece(i)
                nc.vector.scalar_tensor_tensor(hi, hi, neg_lo_c[:, 0:1], whole, ALU.mult,
                                               ALU.add).then_inc(c2_made, 1)

            def w1_low(c, part):
                dve.wait_ge(w1T_hi, 2 * c + part + 1)
                nc.vector.tensor_tensor(w1T[1][:, 2 * part:2 * part + 2, :],
                                        w1_bank(c, part).rearrange("p (k n) -> p k n", k=2),
                                        w1T[0][:, 2 * part:2 * part + 2, :], ALU.subtract).then_inc(w1T_lo, 1)

            def first_maxima(c, half, between=None):
                s0 = 10 * c + 5 * half
                scores = bank[0][:, :].rearrange("p (n j) -> p n j", j=BLK)
                dve.wait_ge(inter_made, 2 * c + half + 1)
                nc.vector.tensor_reduce(oh_max[:, :], scores, AX_X, ALU.max).then_inc(oh_step, 1)
                dve.wait_ge(oh_step, s0 + 1)
                nc.vector.tensor_tensor(oh_eq[:, :, :], scores, oh_max[:, :].unsqueeze(2).to_broadcast([P, 16, BLK]),
                                        ALU.is_equal).then_inc(oh_step, 1)
                if between is not None:
                    between()
                dve.wait_ge(oh_step, s0 + 2)
                nc.vector.tensor_tensor(oh_key[:, :, :], oh_eq[:, :, :], desc[:, :, :], ALU.mult).then_inc(oh_step, 1)
                dve.wait_ge(oh_step, s0 + 3)
                nc.vector.tensor_reduce(oh_first[:, :], oh_key[:, :, :], AX_X, ALU.max).then_inc(oh_step, 1)
                dve.wait_ge(oh_step, s0 + 4)
                nc.vector.tensor_tensor(one_hot[:, 2 * half:2 * half + 2, :].rearrange("p t (n j) -> p (t n) j", j=BLK),
                                        oh_key[:, :, :], oh_first[:, :].unsqueeze(2).to_broadcast([P, 16, BLK]),
                                        ALU.is_equal).then_inc(oh_step, 1)

            def mask(c, i):
                if i == 0:
                    dve.wait_ge(oh_read, c + 1)
                dve.wait_ge(h_made, 2 * c + i + 1)
                nc.vector.scalar_tensor_tensor(h[:, i, :], bank[1 + i][:, :], 0.0, one_hotT[:, i, :],
                                               ALU.max, ALU.mult).then_inc(h_masked, 1)

            def h_low(c, i):
                dve.wait_ge(hT_hi, 2 * c + i + 1)
                nc.vector.tensor_tensor(hT[1][:, i, :], h[:, i, :], hT[0][:, i, :], ALU.subtract).then_inc(hT_lo, 1)

            def low_then_mask(c):
                h_low(c, 0)
                mask(c, 1)

            def chunk(c, last):
                mask(c, 0)
                if last:
                    low_then_mask(c)
                    h_low(c, 1)
                else:
                    first_maxima(c + 1, 0, between=lambda: low_then_mask(c))
                    h_low(c, 1)
                    w1_low(c + 1, 0)
                    first_maxima(c + 1, 1, between=lambda: w1_low(c + 1, 1))

            c2_together(0)
            for kk in range(KD):
                x_low(0, kk)
            w1_low(0, 0)
            w1_low(0, 1)
            dve.wait_ge(t_hi, 1)
            nc.vector.scalar_tensor_tensor(t_stack[:, :], t_stack[:, :], neg_lo_t[:, 0:1], bank[4][:, :],
                                           ALU.mult, ALU.add).then_inc(t_lo, 1)
            first_maxima(0, 0)
            first_maxima(0, 1)
            for i in range(1, C2_PIECES):
                c2_together(i)
            with dve.Fori(0, NCHUNK - 1) as c:
                chunk(c, False)
            chunk(NCHUNK - 1, True)
            for t in range(TT):
                dve.wait_ge(y_made, 8 * (NCHUNK - 1) + last_down_count(t))
                nc.vector.tensor_tensor(x[:, t, :], bank[4 + t][:, :], x[:, t, :], ALU.add).then_inc(wo_added, 1)
                dve.wait_ge(wo_added, t + 1)
                tile_moments(t)
            layer_norm(2)

            def set_biases(s):
                nc.vector.tensor_copy(bias_q[:, :], bias_all[:, bass.ds(G * s, G)]).then_inc(bias_set, 1)
                nc.vector.tensor_copy(bias_k[:, :], bias_all[:, bass.ds(NHEAD + s, 1)]).then_inc(bias_set, 1)

            def k_low(s, b):
                if b == 0:
                    dve.wait_ge(bias_set, 2 * s + 2)
                dve.wait_ge(proj_hi, 8 * s + b + 1)
                nc.vector.scalar_tensor_tensor(k[1][:, b * CTX:(b + 1) * CTX], set_bank(b), bias_k[:, 0:1],
                                               k[0][:, b * CTX:(b + 1) * CTX], ALU.add, ALU.subtract)\
                    .then_inc(proj_read, 3 if isinstance(s, int) and s == 0 and b == 1 else 1)

            def vT_copy(s, b):
                dve.wait_ge(proj_made, 10 * s + 3 + b)
                nc.vector.tensor_copy(vT[:, b * CTX:(b + 1) * CTX], set_bank(2 + b)).then_inc(proj_read, 1)

            def v_low(s, b):
                dve.wait_ge(proj_hi, 8 * s + 3 + b)
                nc.vector.tensor_tensor(v[1][:, b * MT:(b + 1) * MT, :], set_bank(4 + b).rearrange("p (m d) -> p m d", m=MT),
                                        v[0][:, b * MT:(b + 1) * MT, :], ALU.subtract).then_inc(proj_read, 1)

            def q_low(s, head):
                dve.wait_ge(proj_hi, 8 * s + 5 + head)
                nc.vector.scalar_tensor_tensor(q[1][:, head, :], set_bank(6 + head), bias_q[:, head:head + 1],
                                               q[0][:, head, :], ALU.add, ALU.subtract).then_inc(proj_read, 1)

            def row_max(g, u):
                dve.wait_ge(s_made, UNITS * g + u + 1)
                nc.vector.tensor_reduce(neg_max[:, u:u + 1], s_bank(u), AX_X, ALU.max, negate=True).then_inc(nb_made, 1)
                dve.wait_ge(nb_made, UNITS * g + u + 1)
                nc.vector.tensor_scalar(neg_bias[:, u:u + 1], neg_max[:, u:u + 1], SCALE, None, ALU.mult).then_inc(max_made, 1)

            def inverse(g, u):
                dve.wait_ge(exp_made, UNITS * g + u + 1)
                nc.vector.reciprocal(exp_inv[:, u:u + 1], exp_sum[:, u:u + 1]).then_inc(inv_made, 1)

            def p_low(g, u):
                quad, j = u // 4, u % 4
                dve.wait_ge(pT_hi, UNITS * g + u + 1)
                nc.vector.tensor_tensor(probT[quad % 2][1][:, :, j * P:(j + 1) * P],
                                        bank[2 + u % 2][:, :].rearrange("p (m n) -> p m n", m=MT),
                                        probT[quad % 2][0][:, :, j * P:(j + 1) * P], ALU.subtract).then_inc(pT_lo, 1)

            def o_low(g, quad):
                b, hp = quad // 2, quad % 2
                if quad == 0:
                    dve.wait_ge(bv_set, g + 1)
                dve.wait_ge(o_hi, 4 * g + quad + 1)
                at = (slice(None), slice(2 * hp, 2 * hp + 2), slice(b * SEQ, (b + 1) * SEQ))
                nc.vector.scalar_tensor_tensor(o[1][at], o_bank(quad).rearrange("p (h n) -> p h n", h=2), bias_v[:, 0:1],
                                               o[0][at], ALU.add, ALU.subtract).then_inc(o_lo, 1)

            def add_output(g, t, last):
                dve.wait_ge(wo_added, 4 * g + t + 1)
                dve.wait_ge(wo_made, 4 * g + t + 1)
                nc.vector.tensor_tensor(x[:, t, :], out_bank(t, last), x[:, t, :], ALU.add).then_inc(wo_added, 1)

            def moments_after_output(t):
                dve.wait_ge(wo_added, 4 * NKV + t + 1)
                tile_moments(t)

            def group_head(g, first):
                nc.vector.tensor_copy(bias_v[:, :], bias_all[:, bass.ds(NHEAD + NKV + g, 1)]).then_inc(bv_set, 1)
                for u in range(2, 7):
                    row_max(g, u)
                    inverse(g, u - 1)
                    if u >= 3:
                        p_low(g, u - 3)
                if not first:
                    add_output(g - 1, 3, False)

            def group_rest(g, last):
                for u in range(7, UNITS):
                    row_max(g, u)
                    inverse(g, u - 1)
                    p_low(g, u - 3)
                    if u == 12:
                        o_low(g, 0)
                inverse(g, 15)
                o_low(g, 1)
                if not last:
                    set_biases(g + 1)
                    k_low(g + 1, 0)
                p_low(g, 13)
                if last:
                    add_output(g, 0, True)
                    moments_after_output(0)
                p_low(g, 14)
                o_low(g, 2)
                p_low(g, 15)
                if not last:
                    k_low(g + 1, 1)
                    vT_copy(g + 1, 0)
                    vT_copy(g + 1, 1)
                else:
                    add_output(g, 1, True)
                    moments_after_output(1)
                    layer_norm(3, range(2), between=lambda: o_low(g, 3))
                if not last:
                    o_low(g, 3)
                    v_low(g + 1, 0)
                    v_low(g + 1, 1)
                    for head in range(G):
                        q_low(g + 1, head)
                    add_output(g, 0, False)
                    row_max(g + 1, 0)
                    inverse(g + 1, 0)
                    add_output(g, 1, False)
                    row_max(g + 1, 1)
                    add_output(g, 2, False)
                else:
                    for t in (2, 3):
                        add_output(g, t, True)
                        moments_after_output(t)
                    layer_norm(4, range(2, TT))

            dve.wait_ge(setup_read, setup_count("bias"))
            set_biases(0)
            k_low(0, 0)
            k_low(0, 1)
            for kk in range(KD):
                x_low(1, kk)
            v_low(0, 0)
            v_low(0, 1)
            q_low(0, 0)
            q_low(0, 1)
            row_max(0, 0)
            row_max(0, 1)
            q_low(0, 2)
            inverse(0, 0)
            q_low(0, 3)
            group_head(0, True)
            dve.wait_ge(bo_added, TT)
            with dve.Fori(0, NKV - 1) as g:
                group_rest(g, False)
                group_head(g + 1, False)
            group_rest(NKV - 1, True)
            for b in range(BATCH):
                dve.wait_ge(routed, b + 1)
                at = slice(2 * b, 2 * b + 2)
                logits = hidden(b)[:, :, ER:ER + EXP]
                link(nc.vector.tensor_reduce(top[:, at], logits, AX_X, ALU.max))
                link(nc.vector.tensor_tensor(r_eq[:, at, :], logits, top[:, at].unsqueeze(2).to_broadcast([P, 2, EXP]),
                                             ALU.is_equal))
                link(nc.vector.tensor_tensor(r_key[:, at, :], r_eq[:, at, :], desc8[:, at, :], ALU.mult))
                link(nc.vector.tensor_reduce(r_first[:, at], r_key[:, at, :], AX_X, ALU.max))
                link(nc.vector.tensor_tensor(r_gate[:, at, :], r_key[:, at, :],
                                             r_first[:, at].unsqueeze(2).to_broadcast([P, 2, EXP]), ALU.is_equal))
                link(nc.vector.tensor_tensor(r_gate[:, at, :], r_gate[:, at, :],
                                             top[:, at].unsqueeze(2).to_broadcast([P, 2, EXP]), ALU.mult))
                for t in (2 * b, 2 * b + 1):
                    ins = nc.vector.tensor_tensor(wh[:, t, :].rearrange("p (e r) -> p e r", e=EXP),
                                                  hidden(b)[:, t % 2, 0:ER].rearrange("p (e r) -> p e r", e=EXP),
                                                  r_gate[:, t, :].unsqueeze(2).to_broadcast([P, EXP, ER // EXP]), ALU.mult)
                ins.then_inc(gated, 1)
            for t in range(TT):
                dve.wait_ge(out_made, t + 1)
                nc.vector.tensor_tensor(x[:, t, :], bank[t][:, :], x[:, t, :], ALU.add).then_inc(x_final, 1)


_INS = ["x", "ctx_4096", "L0_xattn_x1_scale", "L0_xattn_x1_zp", "L0_xattn_x2_scale", "L0_xattn_x2_zp", "L0_ffn_c1_w",
        "L0_ffn_c2_w", "L0_ffn_w1", "L0_ffn_w2t", "L1_xattn_Wq", "L1_xattn_bq", "L1_xattn_Wkv", "L1_xattn_bkv",
        "L1_xattn_Wo", "L1_xattn_bo", "L1_ffn_route_w", "L1_ffn_A", "L1_ffn_Bw"]
_OUTS = [((BATCH, SEQ, DIM), "float32")]


def kernel(**inputs):
    import numpy as _np
    import concourse.bacc as _bacc
    from concourse import mybir as _mybir
    from concourse.bass_utils import run_bass_kernel_spmd as _run

    nc = _bacc.Bacc("TRN2", target_bir_lowering=False, num_devices=1)
    arrays, args = {}, []
    for name in _INS:
        a = _np.ascontiguousarray(inputs[name])
        arrays[f"in_{name}_dram"] = a
        args.append(nc.dram_tensor(f"in_{name}_dram", a.shape, _mybir.dt.from_np(a.dtype), kind="ExternalInput").ap())
    for i, (shape, dtype) in enumerate(_OUTS):
        dt = _mybir.dt.from_np(_np.dtype(dtype))
        args.append(nc.dram_tensor(f"out_{i}_dram", shape, dt, kind="ExternalOutput").ap())
    xattn_ffn_kernel(nc, *args)
    r = _run(nc, [arrays], core_ids=[0])
    got = tuple(r.results[0][f"out_{i}_dram"] for i in range(len(_OUTS)))
    return got[0]
```
